# Optimizing a Trainium2 kernel written in Bass

```python
import numpy as np
import jax
import jax.numpy as jnp

def _softmax(x, axis=-1):
    return jax.nn.softmax(x, axis=axis)

def _gelu(x):
    return jax.nn.gelu(x, approximate=True)

def _silu(x):
    return jax.nn.silu(x)

def _sigmoid(x):
    return jax.nn.sigmoid(x)

def _layernorm(x, axis=-1, eps=1e-05):
    m = jnp.mean(x, axis=axis, keepdims=True)
    v = jnp.var(x, axis=axis, keepdims=True)
    return (x - m) / jnp.sqrt(v + eps)

def _scatter_add(tgt, idx, src, axis=0):
    return tgt.at[idx].add(src)

def _segment_sum(src, seg, n):
    return jax.ops.segment_sum(src, seg, n)
kernel_name = 'mk_adaln_d1_jaxref_r8_e88703'

def setup_inputs(seed: int=0):
    np.random.seed(seed)
    _w = jnp.asarray

    def _L0_attn_setup():
        import jax, jax.numpy as jnp
        import numpy as np
        H, DK, DV, GG = (16, 128, 128, 16)
        NG = DK // GG
        SCALE = DK ** (-0.5)
        EPS = 1e-05

        def _short_conv(x, w):
            K = w.shape[1]
            xp = jnp.pad(x, ((0, 0), (K - 1, 0), (0, 0)))
            y = jax.lax.conv_general_dilated(xp, jnp.transpose(w)[:, None, :], (1,), 'VALID', dimension_numbers=('NWC', 'WIO', 'NWC'), feature_group_count=w.shape[0])
            return jax.nn.silu(y)

        def _l2norm(x, eps=1e-06):
            return x * jax.lax.rsqrt(jnp.sum(x * x, -1, keepdims=True) + eps)

        def _forward(hidden_states, Wq, Wk, Wv, conv_q, conv_k, conv_v, Wf1, Wf2, Wb, A_log, dt_bias, Wg, bg, norm_w, Wo):
            B, T, D = hidden_states.shape
            q = _short_conv(hidden_states @ Wq, conv_q).reshape(B, T, H, DK)
            k = _short_conv(hidden_states @ Wk, conv_k).reshape(B, T, H, DK)
            v = _short_conv(hidden_states @ Wv, conv_v).reshape(B, T, H, DV)
            q = _l2norm(q) * SCALE
            k = _l2norm(k)
            g_grouped = (hidden_states @ Wf1 @ Wf2).reshape(B, T, H, NG)
            g_eff = -jnp.exp(A_log)[:, None] * jax.nn.softplus(g_grouped + dt_bias.reshape(H, NG))
            g_eff = jnp.repeat(g_eff, GG, axis=-1)
            beta = jax.nn.sigmoid(hidden_states @ Wb)

            def step(S, inp):
                qt, kt, vt, gt, bt = inp
                S = S * jnp.exp(gt)[..., None]
                err = jnp.einsum('bhk,bhkv->bhv', kt, S)
                delta = bt[..., None] * (vt - err)
                S = S + kt[..., None] * delta[:, :, None, :]
                ot = jnp.einsum('bhk,bhkv->bhv', qt, S)
                return (S, ot)
            tm = lambda x: jnp.moveaxis(x, 1, 0)
            S0 = jnp.zeros((B, H, DK, DV), hidden_states.dtype)
            _, o = jax.lax.scan(step, S0, (tm(q), tm(k), tm(v), tm(g_eff), tm(beta)))
            o = jnp.moveaxis(o, 0, 1)
            gate = (hidden_states @ Wg + bg).reshape(B, T, H, DV)
            y = o * jax.nn.silu(gate)
            y = y * jax.lax.rsqrt(jnp.mean(y * y, -1, keepdims=True) + EPS) * norm_w
            return y.reshape(B, T, H * DV) @ Wo
        key = jax.random.key(seed)
        ks = jax.random.split(key, 16)
        B, T, D = (2, 128, 256)
        KD, VD = (H * DK, H * DV)
        init = lambda k, sh: jax.random.normal(k, sh, jnp.float32) * 0.02
        return {'hidden_states': jax.random.normal(ks[0], (B, T, D), jnp.float32), 'Wq': init(ks[1], (D, KD)), 'Wk': init(ks[2], (D, KD)), 'Wv': init(ks[3], (D, VD)), 'conv_q': init(ks[4], (KD, 4)), 'conv_k': init(ks[5], (KD, 4)), 'conv_v': init(ks[6], (VD, 4)), 'Wf1': init(ks[7], (D, DV)), 'Wf2': init(ks[8], (DV, H * NG)), 'Wb': init(ks[9], (D, H)), 'A_log': jnp.log(jax.random.uniform(ks[10], (H,), jnp.float32, 1.0, 16.0)), 'dt_bias': jnp.zeros((H * NG,), jnp.float32), 'Wg': init(ks[11], (D, VD)), 'bg': jnp.zeros((VD,), jnp.float32), 'norm_w': jnp.ones((DV,), jnp.float32), 'Wo': init(ks[12], (VD, D))}
    _L0_attn_in = _L0_attn_setup()

    def _L0_ffn_setup():
        import jax, jax.numpy as jnp
        import numpy as np
        H, LAT, INTER, E, G, TOPK_G, TOP_K = (256, 128, 128, 32, 4, 2, 8)
        SHARED_INTER = 512
        ROUTED_SCALE = 2.5
        B, S = (2, 128)

        def relu2(x):
            return jnp.square(jax.nn.relu(x))
        key = jax.random.key(seed)
        ks = jax.random.split(key, 9)
        w = 0.02
        return {'hidden_states': jax.random.normal(ks[0], (B, S, H), jnp.float32), 'gate_w': jax.random.normal(ks[1], (E, H), jnp.float32) * w, 'gate_bias': jax.random.normal(ks[2], (E,), jnp.float32) * w, 'fc1_w': jax.random.normal(ks[3], (LAT, H), jnp.float32) * w, 'fc2_w': jax.random.normal(ks[4], (H, LAT), jnp.float32) * w, 'w1': jax.random.normal(ks[5], (E, INTER, LAT), jnp.float32) * w, 'w2': jax.random.normal(ks[6], (E, LAT, INTER), jnp.float32) * w, 'shared_up_w': jax.random.normal(ks[7], (SHARED_INTER, H), jnp.float32) * w, 'shared_down_w': jax.random.normal(ks[8], (H, SHARED_INTER), jnp.float32) * w}
    _L0_ffn_in = _L0_ffn_setup()
    _L0_c = _w((lambda *s: np.random.randn(*s).astype(np.float32) * 0.05)(4, 256))
    _L0_wmod = _w((lambda *s: np.random.randn(*s).astype(np.float32) * 0.05)(256, 6 * 256) * 256 ** (-0.5))
    _d = {'L0_attn_hidden_states': _L0_attn_in['hidden_states'], 'L0_attn_Wq': _L0_attn_in['Wq'], 'L0_attn_Wk': _L0_attn_in['Wk'], 'L0_attn_Wv': _L0_attn_in['Wv'], 'L0_attn_conv_q': _L0_attn_in['conv_q'], 'L0_attn_conv_k': _L0_attn_in['conv_k'], 'L0_attn_conv_v': _L0_attn_in['conv_v'], 'L0_attn_Wf1': _L0_attn_in['Wf1'], 'L0_attn_Wf2': _L0_attn_in['Wf2'], 'L0_attn_Wb': _L0_attn_in['Wb'], 'L0_attn_A_log': _L0_attn_in['A_log'], 'L0_attn_dt_bias': _L0_attn_in['dt_bias'], 'L0_attn_Wg': _L0_attn_in['Wg'], 'L0_attn_bg': _L0_attn_in['bg'], 'L0_attn_norm_w': _L0_attn_in['norm_w'], 'L0_attn_Wo': _L0_attn_in['Wo'], 'L0_ffn_gate_w': _L0_ffn_in['gate_w'], 'L0_ffn_gate_bias': _L0_ffn_in['gate_bias'], 'L0_ffn_fc1_w': _L0_ffn_in['fc1_w'], 'L0_ffn_fc2_w': _L0_ffn_in['fc2_w'], 'L0_ffn_w1': _L0_ffn_in['w1'], 'L0_ffn_w2': _L0_ffn_in['w2'], 'L0_ffn_shared_up_w': _L0_ffn_in['shared_up_w'], 'L0_ffn_shared_down_w': _L0_ffn_in['shared_down_w'], 'L0_c': _L0_c, 'L0_wmod': _L0_wmod}
    _x0 = _d['L0_attn_hidden_states']
    _d['L0_attn_hidden_states'] = jax.random.normal(jax.random.fold_in(jax.random.key(seed), 1), (4, 256, 256), dtype=_x0.dtype)
    del _x0
    return _d

def reference(L0_attn_hidden_states, L0_attn_Wq, L0_attn_Wk, L0_attn_Wv, L0_attn_conv_q, L0_attn_conv_k, L0_attn_conv_v, L0_attn_Wf1, L0_attn_Wf2, L0_attn_Wb, L0_attn_A_log, L0_attn_dt_bias, L0_attn_Wg, L0_attn_bg, L0_attn_norm_w, L0_attn_Wo, L0_ffn_gate_w, L0_ffn_gate_bias, L0_ffn_fc1_w, L0_ffn_fc2_w, L0_ffn_w1, L0_ffn_w2, L0_ffn_shared_up_w, L0_ffn_shared_down_w, L0_c, L0_wmod):

    def _L0_attn_ref(hidden_states, Wq, Wk, Wv, conv_q, conv_k, conv_v, Wf1, Wf2, Wb, A_log, dt_bias, Wg, bg, norm_w, Wo):
        import jax, jax.numpy as jnp
        import numpy as np
        H, DK, DV, GG = (16, 128, 128, 16)
        NG = DK // GG
        SCALE = DK ** (-0.5)
        EPS = 1e-05

        def _short_conv(x, w):
            K = w.shape[1]
            xp = jnp.pad(x, ((0, 0), (K - 1, 0), (0, 0)))
            y = jax.lax.conv_general_dilated(xp, jnp.transpose(w)[:, None, :], (1,), 'VALID', dimension_numbers=('NWC', 'WIO', 'NWC'), feature_group_count=w.shape[0])
            return jax.nn.silu(y)

        def _l2norm(x, eps=1e-06):
            return x * jax.lax.rsqrt(jnp.sum(x * x, -1, keepdims=True) + eps)

        def _forward(hidden_states, Wq, Wk, Wv, conv_q, conv_k, conv_v, Wf1, Wf2, Wb, A_log, dt_bias, Wg, bg, norm_w, Wo):
            B, T, D = hidden_states.shape
            q = _short_conv(hidden_states @ Wq, conv_q).reshape(B, T, H, DK)
            k = _short_conv(hidden_states @ Wk, conv_k).reshape(B, T, H, DK)
            v = _short_conv(hidden_states @ Wv, conv_v).reshape(B, T, H, DV)
            q = _l2norm(q) * SCALE
            k = _l2norm(k)
            g_grouped = (hidden_states @ Wf1 @ Wf2).reshape(B, T, H, NG)
            g_eff = -jnp.exp(A_log)[:, None] * jax.nn.softplus(g_grouped + dt_bias.reshape(H, NG))
            g_eff = jnp.repeat(g_eff, GG, axis=-1)
            beta = jax.nn.sigmoid(hidden_states @ Wb)

            def step(S, inp):
                qt, kt, vt, gt, bt = inp
                S = S * jnp.exp(gt)[..., None]
                err = jnp.einsum('bhk,bhkv->bhv', kt, S)
                delta = bt[..., None] * (vt - err)
                S = S + kt[..., None] * delta[:, :, None, :]
                ot = jnp.einsum('bhk,bhkv->bhv', qt, S)
                return (S, ot)
            tm = lambda x: jnp.moveaxis(x, 1, 0)
            S0 = jnp.zeros((B, H, DK, DV), hidden_states.dtype)
            _, o = jax.lax.scan(step, S0, (tm(q), tm(k), tm(v), tm(g_eff), tm(beta)))
            o = jnp.moveaxis(o, 0, 1)
            gate = (hidden_states @ Wg + bg).reshape(B, T, H, DV)
            y = o * jax.nn.silu(gate)
            y = y * jax.lax.rsqrt(jnp.mean(y * y, -1, keepdims=True) + EPS) * norm_w
            return y.reshape(B, T, H * DV) @ Wo
        return _forward(hidden_states, Wq, Wk, Wv, conv_q, conv_k, conv_v, Wf1, Wf2, Wb, A_log, dt_bias, Wg, bg, norm_w, Wo)

    def _L0_ffn_ref(hidden_states, gate_w, gate_bias, fc1_w, fc2_w, w1, w2, shared_up_w, shared_down_w):
        import jax, jax.numpy as jnp
        import numpy as np
        H, LAT, INTER, E, G, TOPK_G, TOP_K = (256, 128, 128, 32, 4, 2, 8)
        SHARED_INTER = 512
        ROUTED_SCALE = 2.5
        B, S = (2, 128)

        def relu2(x):
            return jnp.square(jax.nn.relu(x))
        orig_shape = hidden_states.shape
        x = hidden_states.reshape(-1, H)
        T = x.shape[0]
        logits = jnp.einsum('th,eh->te', x.astype(jnp.float32), gate_w)
        scores = jax.nn.sigmoid(logits)
        sb = scores + gate_bias
        grp = sb.reshape(T, G, E // G)
        group_scores = jax.lax.top_k(grp, 2)[0].sum(-1)
        _, gidx = jax.lax.top_k(group_scores, TOPK_G)
        gmask = jax.nn.one_hot(gidx, G, dtype=sb.dtype).sum(1)
        masked = jnp.where(gmask[:, :, None] > 0, grp, -jnp.inf).reshape(T, E)
        _, topi = jax.lax.top_k(masked, TOP_K)
        wsel = jnp.take_along_axis(scores, topi, axis=1)
        wsel = wsel / wsel.sum(-1, keepdims=True) * ROUTED_SCALE
        cw = jnp.zeros((T, E), jnp.float32).at[jnp.arange(T)[:, None], topi].add(wsel)
        x_lat = x @ fc1_w.T
        h = relu2(jnp.einsum('tl,eil->eti', x_lat, w1))
        h = h * cw.T[:, :, None]
        y_lat = jnp.einsum('eti,eli->tl', h, w2)
        routed = y_lat @ fc2_w.T
        shared = relu2(x @ shared_up_w.T) @ shared_down_w.T
        return (shared + routed).reshape(orig_shape)
    x = L0_attn_hidden_states
    mod = (_silu(L0_c) @ L0_wmod).reshape(L0_c.shape[0], 6, 1, -1)
    sa, ca, ga, sb, cb, gb = (mod[:, 0], mod[:, 1], mod[:, 2], mod[:, 3], mod[:, 4], mod[:, 5])
    ga = (2 * (ga >= 0) - 1) * jnp.maximum(jnp.abs(ga), 0.25)
    gb = (2 * (gb >= 0) - 1) * jnp.maximum(jnp.abs(gb), 0.25)
    h = _layernorm(x, axis=-1) * (1 + ca) + sa
    x = x + ga * _L0_attn_ref(h, L0_attn_Wq, L0_attn_Wk, L0_attn_Wv, L0_attn_conv_q, L0_attn_conv_k, L0_attn_conv_v, L0_attn_Wf1, L0_attn_Wf2, L0_attn_Wb, L0_attn_A_log, L0_attn_dt_bias, L0_attn_Wg, L0_attn_bg, L0_attn_norm_w, L0_attn_Wo)
    h = _layernorm(x, axis=-1) * (1 + cb) + sb
    x = x + gb * _L0_ffn_ref(h, L0_ffn_gate_w, L0_ffn_gate_bias, L0_ffn_fc1_w, L0_ffn_fc2_w, L0_ffn_w1, L0_ffn_w2, L0_ffn_shared_up_w, L0_ffn_shared_down_w)
    return x

_drawn_inputs = setup_inputs


def setup_inputs(seed=0):
    import zlib

    import numpy as np

    out = dict(_drawn_inputs(seed))
    spreads = {'L0_attn_dt_bias': (0.0, 0.8), 'L0_attn_bg': (0.0, 0.8), 'L0_attn_norm_w': (1.0, 0.6)}
    factors = {'L0_attn_Wq': 8.0,
     'L0_attn_Wk': 8.0,
     'L0_attn_Wv': 8.0,
     'L0_attn_conv_q': 8.0,
     'L0_attn_conv_k': 8.0,
     'L0_attn_conv_v': 8.0,
     'L0_attn_Wf1': 8.0,
     'L0_attn_Wf2': 8.0,
     'L0_attn_Wb': 8.0,
     'L0_attn_A_log': 8.0,
     'L0_attn_Wg': 8.0,
     'L0_attn_Wo': 8.0,
     'L0_ffn_gate_w': 8.0,
     'L0_ffn_gate_bias': 8.0,
     'L0_ffn_fc1_w': 8.0,
     'L0_ffn_fc2_w': 8.0,
     'L0_ffn_w1': 8.0,
     'L0_ffn_w2': 8.0,
     'L0_ffn_shared_up_w': 4.366,
     'L0_ffn_shared_down_w': 3.946,
     'L0_c': 4.0,
     'L0_wmod': 3.92}
    for name, (base, spread) in spreads.items():
        noise = np.random.default_rng([zlib.crc32(name.encode()), seed]).standard_normal(out[name].shape)
        drawn = base * np.exp(spread * noise) if base else spread * noise
        out[name] = jnp.asarray(drawn.astype(out[name].dtype))
    for name, factor in factors.items():
        out[name] = (out[name] * factor).astype(out[name].dtype)
    return out
```

```python
from contextlib import ExitStack

import numpy as np
import concourse.bass as bass
from concourse import mybir

ALU = mybir.AluOpType
ACT = mybir.ActivationFunctionType
F32 = mybir.dt.float32
BF16 = mybir.dt.bfloat16
I32 = mybir.dt.int32
AX = mybir.AxisListType

P = 128
B, T, D = 4, 256, 256
NT = B * T
NB = NT // P
DC = D // P
HALF = 512
H, DK = 16, 128
NG = 8
LEVELS = 8
SMALL = 5
KW = 4
E, G, EG, TOPG, TOPK = 32, 4, 8, 2, 8
SHC = 4
ROUTED_SCALE = 2.5
QSCALE = DK ** -0.5
LN_EPS, L2_EPS, RMS_EPS = 1e-5, 1e-6, 1e-5
FILL = -3.0e38
TAKEN = 3.0e38


def shape_constants():
    ident = np.eye(P, dtype=np.float32)
    ident32 = np.tile(np.eye(32, dtype=np.float32), (4, 1))
    spread = np.zeros((P, P), np.float32)
    for s in range(3):
        for g in range(NG):
            spread[s * NG + g, g * 16:(g + 1) * 16] = 1.0
    floats = np.concatenate([ident, ident32, spread], axis=1)
    masks = np.zeros((P, SMALL * 16 + 32), np.int32)
    for lv in range(SMALL):
        s = 1 << lv
        for c in range(16):
            i = (c // s) * 2 * s + s + c % s
            for p in range(P):
                j = p % 32
                masks[p, lv * 16 + c] = int(j // (2 * s) == i // (2 * s) and j % (2 * s) < s)
    masks[:, SMALL * 16:] = ident32.astype(np.int32)
    return floats, masks


def build(nc, d, out):
    ctx = ExitStack()
    with ctx:
        def sb(name, shape, dt=F32, where=ctx):
            return where.enter_context(nc.sbuf_tensor(name, shape, dt))[(slice(None),) * len(shape)]

        def pb(name, cols):
            return ctx.enter_context(nc.psum_tensor(name, [P, cols], F32))[:, :]

        def sem(name):
            return ctx.enter_context(nc.semaphore(name))

        pX, pW = pb("pX", 2 * HALF), pb("pW", 2 * HALF)
        pA, pM1, pM2, pM3 = pb("pA", HALF), pb("pM1", HALF), pb("pM2", HALF), pb("pM3", HALF)

        decay_dram = nc.dram_tensor("decay_dram", [3, P, LEVELS * NT], BF16, kind="Internal").ap()
        route_dram = nc.dram_tensor("route_dram", [E, NT], F32, kind="Internal").ap()

        x = sb("x", [P, NB, D])
        hT = sb("hT", [P, DC, NT])
        modT = sb("modT", [P, 12, B])
        consts = sb("consts", [P, P + 32 + P])
        masks = sb("masks", [P, SMALL * 16 + 32], I32)
        ident, ident32, spread_f = consts[:, 0:P], consts[:, P:P + 32], consts[:, P + 32:]
        spread = sb("spread", [3 * NG, P], BF16)
        ones = sb("ones", [P, P])
        beta = sb("beta", [P, NB, H])
        yT = sb("yT", [P, H, NT])
        nw = sb("nw", [P, 1])
        stats = sb("stats", [P, NB, 6])
        mv = sb("mv", [P, NB, 2])
        veps = sb("veps", [P, NB])
        rstd = sb("rstd", [P, NB])
        halfs = sb("halfs", [P, 2, NB])
        xn = sb("xn", [P, NB, D])

        s_x, s_mod_in, s_const, s_gw = (sem(n) for n in ("s_x", "s_mod_in", "s_const", "s_gw"))
        s_set, s_siluc, s_modps, s_mod = (sem(n) for n in ("s_set", "s_siluc", "s_modps", "s_mod"))
        s_ln, s_rstd, s_xn, s_xT, s_hT = (sem(n) for n in ("s_ln", "s_rstd", "s_xn", "s_xT", "s_hT"))
        s_gp, s_f1c, s_exp1, s_sp, s_a = (sem(n) for n in ("s_gp", "s_f1c", "s_exp1", "s_sp", "s_a"))
        s_lev, s_hi, s_sub1, s_mid, s_sub2, s_lo = (
            sem(n) for n in ("s_lev", "s_hi", "s_sub1", "s_mid", "s_sub2", "s_lo"))
        s_stored = [sem(f"s_stored{k}") for k in range(3)]

        def layer_norm(dve, done, base):
            for n in range(NB):
                last = dve.bn_stats(stats[:, n, :], x[:, n, :])
            last.then_inc(done, 1)
            dve.wait_ge(done, base + 1)
            for n in range(NB):
                last = dve.bn_aggr(mv[:, n, :], stats[:, n, :])
            last.then_inc(done, 1)
            dve.wait_ge(done, base + 2)
            dve.tensor_scalar(veps[:, :], mv[:, :, 1], LN_EPS, None, ALU.add).then_inc(done, 1)
            dve.wait_ge(s_rstd, (base // 3) + 1)
            for n in range(NB):
                dve.tensor_scalar(xn[:, n, :], x[:, n, :], mv[:, n, 0:1], rstd[:, n:n + 1],
                                  ALU.subtract, ALU.mult).then_inc(s_xn, 1)

        def turn_in(pe, base):
            for n in range(NB):
                pe.wait_ge(s_xn, base * NB + n + 1)
                for c, ps in enumerate((pX, pW)):
                    last = pe.transpose(ps[:, n * P:(n + 1) * P], xn[:, n, c * P:(c + 1) * P], ident)
                last.then_inc(s_xT, 1)

        def modulate(act, base, row):
            for b in range(B):
                act.wait_ge(s_xT, base * NB + 4 * (b // 2) + 4)
                for c, ps in enumerate((pX, pW)):
                    last = act.activation(hT[:, c, b * T:(b + 1) * T], ps[:, b * T:(b + 1) * T], ACT.Identity,
                                          bias=modT[:, row + c, b:b + 1], scale=modT[:, row + 2 + c, b:b + 1])
                last.then_inc(s_hT, 1)

        with ExitStack() as first:
            cT = sb("cT", [P, DC, B], where=first)
            siluc = sb("siluc", [P, DC, B], where=first)
            wmod = sb("wmod", [P, DC, 12 * P], where=first)
            gsign = sb("gsign", [P, 4, B], where=first)
            gmag = sb("gmag", [P, 4, B], where=first)
            wf1 = sb("wf1", [P, DC, P], where=first)
            wf2 = sb("wf2", [P, P], where=first)
            wb = sb("wb", [P, DC, H], where=first)
            dtb = sb("dtb", [P, 1], where=first)
            alog = sb("alog", [P, 1], where=first)
            nega = sb("nega", [P, 1], where=first)
            f1 = sb("f1", [P, NT], where=first)
            gx = sb("gx", [P, NT], where=first)
            u = sb("u", [P, NT], where=first)
            v1 = sb("v1", [P, NT], where=first)
            v2 = sb("v2", [P, NT], where=first)
            lev = yT[:, 0:LEVELS, :]
            pre = yT[:, LEVELS, :]
            suf = yT[:, LEVELS + 1, :]
            hi = sb("hi", [P, 2, NT], BF16, where=first)
            mid = sb("mid", [P, 2, NT], BF16, where=first)
            lo = sb("lo", [P, 2, NT], BF16, where=first)
            s_modc, s_gx, s_own = sem("s_modc"), sem("s_gx"), sem("s_own")

            with nc.Block() as block:
                @block.sync
                def _(sp):
                    sp.dma_start(cT[:, :, :], d["cT"].rearrange("(c p) b -> p c b", p=P)).then_inc(s_mod_in, 16)
                    sp.dma_start(wmod[:, :, :], d["wmod"].rearrange("(c p) n -> p c n", p=P)).then_inc(s_mod_in, 16)
                    sp.dma_start(x[:, :, :], d["x"].rearrange("(n p) f -> p n f", p=P)).then_inc(s_x, 16)
                    sp.dma_start(consts[:, :], d["floats"]).then_inc(s_const, 16)
                    sp.dma_start(masks[:, :], d["masks"]).then_inc(s_const, 16)
                    for t, n in ((wf1[:, :, :], "Wf1"), (wb[:, :, :], "Wb")):
                        sp.dma_start(t, d[n].rearrange("(c p) n -> p c n", p=P)).then_inc(s_gw, 16)
                    sp.dma_start(wf2[:, :], d["Wf2"]).then_inc(s_gw, 16)
                    sp.dma_start(dtb[:, :], d["dt"]).then_inc(s_gw, 16)
                    sp.dma_start(alog[:, :], d["A_log"]).then_inc(s_gw, 16)
                    sp.dma_start(nw[:, :], d["norm_w"]).then_inc(s_gw, 16)
                    for pair in range(LEVELS // 2):
                        cols = slice(2 * pair * NT, (2 * pair + 2) * NT)
                        for s, (t, ready) in enumerate(((hi, s_hi), (mid, s_mid), (lo, s_lo))):
                            sp.wait_ge(ready, 2 * pair + 2)
                            sp.dma_start(decay_dram[s, :, cols], t.rearrange("p a n -> p (a n)"))\
                              .then_inc(s_stored[s], 16)
                    for s in range(3):
                        sp.wait_ge(s_stored[s], 16 * (LEVELS // 2))

                @block.gpsimd
                def _(pool):
                    pool.memset(halfs[:, 0, :], -0.5)
                    pool.memset(halfs[:, 1, :], 0.5)
                    pool.memset(ones[:, :], 1.0).then_inc(s_set, 1)
                    pool.wait_ge(s_set, 1)
                    pool.wait_ge(s_ln, 3)
                    pool.tensor_tensor(rstd[:, :], veps[:, :], halfs[:, 0, :], ALU.pow).then_inc(s_rstd, 1)

                @block.scalar
                def _(act):
                    act.wait_ge(s_mod_in, 32)
                    act.activation(siluc[:, :, :], cT[:, :, :], ACT.Silu).then_inc(s_siluc, 1)
                    act.wait_ge(s_mod, 1)
                    modulate(act, 0, 0)
                    act.wait_ge(s_gw, 6 * 16)
                    act.activation(nega[:, :], alog[:, :], ACT.Exp).then_inc(s_exp1, 1)
                    act.wait_ge(s_gx, 1)
                    act.activation(u[:, :], gx[:, :], ACT.Abs).then_inc(s_exp1, 1)
                    act.wait_ge(s_exp1, 2)
                    act.activation(u[:, :], u[:, :], ACT.Exp, scale=-1.0).then_inc(s_exp1, 1)
                    act.wait_ge(s_gp, 3)
                    act.activation(beta[:, :, :], pA[:, 64:64 + NB * H].rearrange("p (n h) -> p n h", n=NB),
                                   ACT.Exp, scale=-1.0).then_inc(s_exp1, 1)
                    act.wait_ge(s_sp, 1)
                    act.activation(pre, v1[:, :], ACT.Exp, scale=nega[:, 0:1]).then_inc(s_a, 1)
                    for lv in range(LEVELS):
                        act.wait_ge(s_lev, lv + 1)
                        if lv >= 2 and lv % 2 == 0:
                            act.wait_ge(s_stored[0], 16 * (lv // 2))
                        act.copy(hi[:, lv % 2, :], lev[:, lv, :]).then_inc(s_hi, 1)
                        if lv >= 2 and lv % 2 == 0:
                            act.wait_ge(s_stored[1], 16 * (lv // 2))
                        act.wait_ge(s_sub1, lv + 1)
                        act.copy(mid[:, lv % 2, :], lev[:, lv, :]).then_inc(s_mid, 1)
                        if lv >= 2 and lv % 2 == 0:
                            act.wait_ge(s_stored[2], 16 * (lv // 2))
                        act.wait_ge(s_sub2, lv + 1)
                        act.copy(lo[:, lv % 2, :], lev[:, lv, :]).then_inc(s_lo, 1)

                @block.vector
                def _(dve):
                    dve.wait_ge(s_x, 16)
                    layer_norm(dve, s_ln, 0)
                    dve.wait_ge(s_modps, 1)
                    dve.tensor_copy(modT[:, :, :], pA[:, 0:48].rearrange("p (j b) -> p j b", b=B)).then_inc(s_modc, 1)
                    dve.wait_ge(s_modc, 1)
                    for r in (2, 8):
                        dve.tensor_scalar(modT[:, r:r + 2, :], modT[:, r:r + 2, :], 1.0, None, ALU.add)
                    for k, r in enumerate((4, 10)):
                        gate = modT[:, r:r + 2, :]
                        dve.tensor_scalar(gsign[:, 2 * k:2 * k + 2, :], gate, 0.0, 2.0, ALU.is_ge, ALU.mult)
                        last = dve.scalar_tensor_tensor(gmag[:, 2 * k:2 * k + 2, :], gate, -1.0, gate, ALU.mult, ALU.max)
                    last.then_inc(s_own, 1)
                    dve.wait_ge(s_own, 1)
                    dve.tensor_scalar(gsign[:, :, :], gsign[:, :, :], -1.0, None, ALU.add).then_inc(s_own, 1)
                    dve.wait_ge(s_own, 2)
                    for k, r in enumerate((4, 10)):
                        last = dve.scalar_tensor_tensor(modT[:, r:r + 2, :], gmag[:, 2 * k:2 * k + 2, :], 0.25,
                                                        gsign[:, 2 * k:2 * k + 2, :], ALU.max, ALU.mult)
                    last.then_inc(s_mod, 1)
                    dve.wait_ge(s_const, 32)
                    dve.tensor_copy(spread[:, :], spread_f[0:3 * NG, :])
                    dve.wait_ge(s_gp, 1)
                    dve.tensor_copy(f1[:, :], pX[:, :]).then_inc(s_f1c, 1)
                    dve.wait_ge(s_gp, 2)
                    dve.tensor_scalar(gx[:, :], pW[:, :], dtb[:, 0:1], None, ALU.add).then_inc(s_gx, 1)
                    own = 2

                    def step(ins):
                        nonlocal own
                        own += 1
                        ins.then_inc(s_own, 1)
                        dve.wait_ge(s_own, own)

                    dve.wait_ge(s_exp1, 3)
                    dve.tensor_scalar(nega[:, :], nega[:, :], -1.0, None, ALU.mult)
                    step(dve.tensor_scalar(v1[:, :], u[:, :], 2.0, None, ALU.add))
                    step(dve.reciprocal(v1[:, :], v1[:, :]))
                    step(dve.tensor_tensor(u[:, :], u[:, :], v1[:, :], ALU.mult))
                    step(dve.tensor_tensor(v2[:, :], u[:, :], u[:, :], ALU.mult))
                    step(dve.tensor_scalar(v1[:, :], v2[:, :], 1.0 / 15, None, ALU.mult))
                    for k in (13, 11, 9, 7, 5, 3):
                        step(dve.scalar_tensor_tensor(v1[:, :], v1[:, :], 1.0 / k, v2[:, :], ALU.add, ALU.mult))
                    step(dve.scalar_tensor_tensor(v1[:, :], v1[:, :], 1.0, u[:, :], ALU.add, ALU.mult))
                    step(dve.tensor_scalar(v2[:, :], gx[:, :], 0.0, None, ALU.max))
                    dve.scalar_tensor_tensor(v1[:, :], v1[:, :], 2.0, v2[:, :], ALU.mult, ALU.add).then_inc(s_sp, 1)
                    dve.wait_ge(s_exp1, 4)
                    step(dve.tensor_scalar(beta[:, :, :], beta[:, :, :], 1.0, None, ALU.add))
                    dve.reciprocal(beta[:, :, :], beta[:, :, :])
                    step(dve.memset(suf, 1.0))
                    dve.wait_ge(s_a, 1)
                    for lv in range(LEVELS):
                        s = 1 << lv
                        w, p_, f_ = (t.rearrange("p (m u s) -> p m u s", u=2, s=s) for t in (lev[:, lv, :], pre, suf))
                        dve.tensor_copy(w[:, :, 0, :], f_[:, :, 0, :])
                        dve.tensor_copy(w[:, :, 1, :], p_[:, :, 1, :]).then_inc(s_lev, 1)
                        if lv < LEVELS - 1:
                            m = NT // (2 * s)
                            step(dve.tensor_tensor(f_[:, :, 0, :], f_[:, :, 0, :],
                                                   p_[:, :, 1, s - 1:s].to_broadcast([P, m, s]), ALU.mult))
                            step(dve.tensor_tensor(p_[:, :, 1, :], p_[:, :, 1, :],
                                                   p_[:, :, 0, s - 1:s].to_broadcast([P, m, s]), ALU.mult))
                    for lv in range(LEVELS):
                        dve.wait_ge(s_hi, lv + 1)
                        dve.tensor_tensor(lev[:, lv, :], lev[:, lv, :], hi[:, lv % 2, :], ALU.subtract)\
                           .then_inc(s_sub1, 1)
                        dve.wait_ge(s_mid, lv + 1)
                        dve.tensor_tensor(lev[:, lv, :], lev[:, lv, :], mid[:, lv % 2, :], ALU.subtract)\
                           .then_inc(s_sub2, 1)

                @block.tensor
                def _(pe):
                    pe.wait_ge(s_siluc, 1)
                    for j in range(12):
                        for c in range(DC):
                            last = pe.matmul(pA[:, j * B:(j + 1) * B], wmod[:, c, j * P:(j + 1) * P], siluc[:, c, :],
                                             start=c == 0, stop=c == DC - 1)
                    last.then_inc(s_modps, 1)
                    pe.wait_ge(s_const, 32)
                    turn_in(pe, 0)
                    pe.wait_ge(s_gw, 6 * 16)
                    pe.wait_ge(s_hT, B)
                    for hf in range(2):
                        for c in range(DC):
                            last = pe.matmul(pX[:, hf * HALF:(hf + 1) * HALF], wf1[:, c, :],
                                             hT[:, c, hf * HALF:(hf + 1) * HALF], start=c == 0, stop=c == DC - 1)
                    last.then_inc(s_gp, 1)
                    pe.wait_ge(s_f1c, 1)
                    for hf in range(2):
                        last = pe.matmul(pW[:, hf * HALF:(hf + 1) * HALF], wf2[:, :],
                                         f1[:, hf * HALF:(hf + 1) * HALF], start=True, stop=True)
                    last.then_inc(s_gp, 1)
                    for n in range(NB):
                        for c in range(DC):
                            last = pe.matmul(pA[:, 64 + n * H:64 + (n + 1) * H], hT[:, c, n * P:(n + 1) * P],
                                             wb[:, c, :], start=c == 0, stop=c == DC - 1)
                    last.then_inc(s_gp, 1)

        PER, START = {}, {}

        def hsem(name, per, start=0):
            s = sem(name)
            PER[id(s)], START[id(s)] = per, start
            return s

        def nth(s, h, k):
            return h * PER[id(s)] + k + START[id(s)]

        with ExitStack() as heads:
            def hb(name, shape, dt=F32):
                return sb(name, shape, dt, where=heads)

            wh = hb("wh", [P, 4, DC, P])
            cw = hb("cw", [P, 16])
            dec = hb("dec", [3 * NG, LEVELS * NT], BF16)
            K, Q, V = hb("K", [P, NT]), hb("Q", [P, NT]), hb("V", [P, NT])
            SG = hb("SG", [P, NT])
            sqk, sqq = hb("sqk", [P, NT]), hb("sqq", [P, NT])
            KQ = hb("KQ", [P, 2, 2, NT])
            A = hb("A", [P, SMALL, NB, 32])
            AqP = hb("AqP", [P, NB, 32])
            AqT = hb("AqT", [P, NB, P])
            A5 = hb("A5", [P, NB, 32])
            A6 = hb("A6", [64, NB, 64])
            A7, Aq7 = hb("A7", [P, B, P]), hb("Aq7", [P, B, P])
            Tm, TT = hb("Tm", [P, NB, 32]), hb("TT", [P, NB, 32])
            TC = hb("TC", [P, NB, 64])
            M1 = hb("M1", [P, NB, 32])
            R = hb("R", [P, NB, P])
            dl = hb("dl", [P, NB, P])
            sse = hb("sse", [P, 2 * NB])
            kn, rqs = hb("kn", [P, NB]), hb("rqs", [P, NB])
            bh, cc, nc_ = hb("bh", [P, NB]), hb("cc", [P, NB]), hb("nc_", [P, NB])
            t2, ms, rms, fr = hb("t2", [P, NB]), hb("ms", [P, NB]), hb("rms", [P, NB]), hb("fr", [P, NB])
            diag = KQ[:, 0, 0, :].rearrange("p (n t) -> p n t", n=NB)

            s_w, s_dec = hsem("s_w", 32), hsem("s_dec", 48)
            s_proj = hsem("s_proj", 4, 1)
            s_ss, s_vt = hsem("s_ss", 2), hsem("s_vt", 1)
            s_e, s_A = hsem("s_e", 8, 1), hsem("s_A", 9)
            s_m1, s_m2 = hsem("s_m1", 6), hsem("s_m2", 6)
            s_app = hsem("s_app", 7)
            s_o, s_ssz, s_f = hsem("s_o", 1), hsem("s_ssz", 1), hsem("s_f", 1)
            s_tap, s_silu, s_sq = hsem("s_tap", 3), hsem("s_silu", 4, 1), hsem("s_sq", 2)
            s_big, s_dl, s_sqz = hsem("s_big", 2), hsem("s_dl", 4), hsem("s_sqz", 1)
            s_fir, s_scaled, s_ev = hsem("s_fir", 9, 1), hsem("s_scaled", 8), hsem("s_ev", 7)
            s_M, s_T, s_sse, s_c, s_R = hsem("s_M", 6), hsem("s_T", 6), hsem("s_sse", 1), hsem("s_c", 3), hsem("s_R", 4)
            s_z, s_ms, s_diag, s_y = hsem("s_z", 1), hsem("s_ms", 5), hsem("s_diag", 1), hsem("s_y", 1, 1)
            s_root, s_rms, s_aq = hsem("s_root", 2), hsem("s_rms", 1), hsem("s_aq", 1)
            s_zero = sem("s_zero")
            s_passed_sp = sem("s_passed_sp")
            s_passed, s_passed_dve, s_passed_pool = sem("s_passed"), sem("s_passed_dve"), sem("s_passed_pool")

            def bc(t, rows, n):
                return t.unsqueeze(2).to_broadcast([rows, t.shape[1], n])

            def later(t, s):
                return t.rearrange("p (m u s) -> p m u s", u=2, s=s)[:, :, 1, :]

            def seqs(t, blk, rows=slice(0, P)):
                return t.rearrange("p (b u) n -> p b u n", u=2)[rows, :, blk, :]

            with nc.Block() as block:
                @block.sync
                def _(sp):
                    for s in (s_proj, s_e, s_silu, s_fir, s_y):
                        sp.sem_inc(s, 1)
                    with sp.Fori(0, H) as h:
                        sp.wait_ge(s_proj, nth(s_proj, h, 0))
                        sp.dma_start(wh[:, :, :, :], d["Wh"][bass.ds(h, 1)].rearrange("a p w c n -> (a p) w c n"))\
                          .then_inc(s_w, 16)
                        sp.wait_ge(s_silu, nth(s_silu, h, 0))
                        sp.sem_inc(s_passed_sp, 1)
                        sp.wait_ge(s_fir, nth(s_fir, h, 0))
                        sp.dma_start(cw[:, :], d["cw"][bass.ds(h, 1)].rearrange("a p n -> (a p) n")).then_inc(s_w, 16)
                        sp.wait_ge(s_e, nth(s_e, h, 0))
                        for s in range(3):
                            sp.dma_start(dec[s * NG:(s + 1) * NG, :], decay_dram[s, bass.ds(h * NG, NG), :])\
                              .then_inc(s_dec, 16)

                @block.gpsimd
                def _(pool):
                    for t in (A, AqP, AqT, TC):
                        last = pool.memset(t, 0.0)
                    last.then_inc(s_zero, 1)
                    pool.wait_ge(s_zero, 1)
                    with pool.Fori(0, H) as h:
                        pool.wait_ge(s_sse, nth(s_sse, h, 1))
                        pool.tensor_tensor(kn[:, :], sse[:, 0:NB], halfs[:, 1, :], ALU.pow).then_inc(s_root, 1)
                        pool.tensor_tensor(rqs[:, :], sse[:, NB:2 * NB], halfs[:, 0, :], ALU.pow).then_inc(s_root, 1)
                        pool.wait_ge(s_ev, nth(s_ev, h, 6))
                        pool.sem_inc(s_passed_pool, 1)
                        for q in range(4):
                            r = slice(32 * q, 32 * q + 32)
                            last = pool.tensor_copy(AqT[r, :, r], AqP[r, :, :])
                        last.then_inc(s_aq, 1)
                        pool.wait_ge(s_ms, nth(s_ms, h, 4))
                        pool.tensor_tensor(rms[:, :], ms[:, :], halfs[:, 0, :], ALU.pow).then_inc(s_rms, 1)

                @block.scalar
                def _(act):
                    with act.Fori(0, H) as h:
                        act.wait_ge(s_w, nth(s_w, h, 32))
                        act.wait_ge(s_proj, nth(s_proj, h, 1))
                        act.mul(K[:, :], pX[:, :], cw[:, 3:4]).then_inc(s_tap, 1)
                        act.wait_ge(s_proj, nth(s_proj, h, 2))
                        act.mul(Q[:, :], pW[:, :], cw[:, 7:8]).then_inc(s_tap, 1)
                        act.wait_ge(s_fir, nth(s_fir, h, 3))
                        act.activation(K[:, :], K[:, :], ACT.Silu).then_inc(s_silu, 1)
                        act.wait_ge(s_proj, nth(s_proj, h, 3))
                        act.mul(V[:, :], pX[:, :], cw[:, 11:12]).then_inc(s_tap, 1)
                        act.wait_ge(s_fir, nth(s_fir, h, 6))
                        act.activation(Q[:, :], Q[:, :], ACT.Silu).then_inc(s_silu, 1)
                        act.wait_ge(s_silu, nth(s_silu, h, 2))
                        act.activation(sqk[:, :], K[:, :], ACT.Square).then_inc(s_sq, 1)
                        act.activation(sqq[:, :], Q[:, :], ACT.Square).then_inc(s_sq, 1)
                        act.wait_ge(s_proj, nth(s_proj, h, 4))
                        act.activation(SG[:, :], pW[:, :], ACT.Silu, bias=cw[:, 12:13]).then_inc(s_silu, 1)
                        act.wait_ge(s_fir, nth(s_fir, h, 9))
                        act.activation(V[:, :], V[:, :], ACT.Silu).then_inc(s_silu, 1)
                        act.wait_ge(s_zero, 1)
                        act.wait_ge(s_A, nth(s_A, h, 8))
                        px64 = pX[0:64, :].rearrange("p (k n i) -> p k n i", k=2, n=NB)
                        act.copy(A6[:, :, :], px64[:, 0, :, :])
                        act.copy(AqT[0:64, :, 64:128], px64[:, 1, :, :]).then_inc(s_big, 1)
                        act.wait_ge(s_A, nth(s_A, h, 9))
                        px = pX.rearrange("p (k b i) -> p k b i", k=2, b=B)
                        act.copy(A7[:, :, :], px[:, 0, :, :])
                        act.copy(Aq7[:, :, :], px[:, 1, :, :]).then_inc(s_big, 1)
                        for k, (app, blk, r, ps) in enumerate(((1, 0, slice(0, 64), pM1), (3, 0, slice(64, P), pM3),
                                                               (5, 1, slice(0, 64), pM1), (7, 1, slice(64, P), pM3))):
                            act.wait_ge(s_app, nth(s_app, h, app))
                            act.copy(seqs(dl, blk, r), ps[r, :].rearrange("p (b n) -> p b n", b=B)).then_inc(s_dl, 1)
                        act.wait_ge(s_z, nth(s_z, h, 1))
                        act.activation(sqk[:, :], Q[:, :], ACT.Square).then_inc(s_sqz, 1)

                @block.vector
                def _(dve):
                    dve.wait_ge(s_zero, 1)
                    mk = [masks[:, lv * 16:(lv + 1) * 16] for lv in range(SMALL)]

                    def fir(h, k, acc, ps, c0):
                        a, p_ = (t.rearrange("p (b t) -> p b t", b=B) for t in (acc, ps))
                        for sh in (1, 2, 3):
                            if sh > 1:
                                dve.wait_ge(s_fir, nth(s_fir, h, 3 * k + sh - 1))
                            dve.scalar_tensor_tensor(a[:, :, sh:], p_[:, :, 0:T - sh], cw[:, c0 + 3 - sh:c0 + 4 - sh],
                                                     a[:, :, sh:], ALU.mult, ALU.add).then_inc(s_fir, 1)

                    def scale(h, lv):
                        dve.wait_ge(s_e, nth(s_e, h, lv + 1))
                        if lv >= 2:
                            dve.wait_ge(s_A, nth(s_A, h, lv))
                        s = 1 << lv
                        dve.tensor_tensor(KQ[:, lv % 2, 0, :], pW[:, :], K[:, :], ALU.mult)
                        dve.tensor_tensor(later(KQ[:, lv % 2, 1, :], s), later(pW[:, :], s), later(Q[:, :], s),
                                          ALU.mult).then_inc(s_scaled, 1)

                    def pick(h, lv):
                        s = 1 << lv
                        dve.wait_ge(s_A, nth(s_A, h, lv + 2))
                        dve.sem_inc(s_passed_dve, 1)
                        ps = pA[:, 0:NB * 32].rearrange("p (n k m s) -> p n k m s", k=2, m=16 // s, s=s)
                        m = mk[lv].rearrange("p (m s) -> p m s", s=s).unsqueeze(1).to_broadcast([P, NB, 16 // s, s])
                        to = [t.rearrange("p n (m u s) -> p n m u s", u=2, s=s)[:, :, :, 1, :]
                              for t in (A[:, lv, :, :], AqP)]
                        for k in range(2):
                            last = dve.copy_predicated(to[k], m, ps[:, :, k, :, :])
                        last.then_inc(s_ev, 1)

                    def m_rows(h, lv):
                        dve.wait_ge(s_m1, nth(s_m1, h, lv + 1))
                        dve.tensor_tensor(M1[:, :, :], pM1[:, 0:NB * 32].rearrange("p (n j) -> p n j", n=NB),
                                          bc(nc_, P, 32), ALU.mult).then_inc(s_M, 1)

                    def t_add(h, lv):
                        dve.wait_ge(s_m2, nth(s_m2, h, lv + 1))
                        dve.tensor_tensor(Tm[:, :, :], pM2[:, 0:NB * 32].rearrange("p (n j) -> p n j", n=NB),
                                          Tm[:, :, :], ALU.add)
                        dve.tensor_tensor(TT[:, :, :], pM3[:, 0:NB * 32].rearrange("p (n j) -> p n j", n=NB),
                                          TT[:, :, :], ALU.add).then_inc(s_T, 1)

                    with dve.Fori(0, H) as h:
                        dve.tensor_copy(bh[:, :], beta[:, :, bass.ds(h, 1)].rearrange("p n a -> p (n a)"))\
                           .then_inc(s_c, 1)
                        id_b = ident32.unsqueeze(1).to_broadcast([P, NB, 32])
                        for k, (acc, ps) in enumerate(((K, pX), (Q, pW), (V, pX))):
                            dve.wait_ge(s_tap, nth(s_tap, h, k + 1))
                            fir(h, k, acc, ps, 4 * k)
                            if k == 1:
                                dve.tensor_copy(Tm[:, :, :], id_b)
                                dve.tensor_copy(TT[:, :, :], id_b)
                        dve.wait_ge(s_ss, nth(s_ss, h, 2))
                        dve.tensor_scalar(sse[:, :], pM1[:, 0:2 * NB], L2_EPS, None, ALU.add).then_inc(s_sse, 1)
                        dve.wait_ge(s_sse, nth(s_sse, h, 1))
                        dve.reciprocal(cc[:, :], sse[:, 0:NB]).then_inc(s_c, 1)
                        dve.wait_ge(s_c, nth(s_c, h, 2))
                        dve.tensor_tensor(cc[:, :], cc[:, :], bh[:, :], ALU.mult).then_inc(s_c, 1)
                        dve.wait_ge(s_c, nth(s_c, h, 3))
                        dve.tensor_scalar(nc_[:, :], cc[:, :], -1.0, None, ALU.mult)
                        scale(h, 0)
                        dve.wait_ge(s_A, nth(s_A, h, 1))
                        dve.sem_inc(s_passed_dve, 1)
                        dve.copy_predicated(AqP[:, :, :],
                                            masks[:, SMALL * 16:].unsqueeze(1).to_broadcast([P, NB, 32]),
                                            pA[:, 0:NB * 32].rearrange("p (n i) -> p n i", n=NB)).then_inc(s_ev, 1)
                        pick(h, 0)
                        dve.wait_ge(s_vt, nth(s_vt, h, 1))
                        dve.wait_ge(s_root, nth(s_root, h, 2))
                        dve.tensor_tensor(R[:, :, :], pX.rearrange("p (n j) -> p n j", n=NB), bc(kn, P, P),
                                          ALU.mult).then_inc(s_R, 1)
                        for lv in range(1, SMALL):
                            scale(h, lv)
                            m_rows(h, lv - 1)
                            pick(h, lv)
                            t_add(h, lv - 1)
                        scale(h, 5)
                        m_rows(h, 4)
                        dve.wait_ge(s_A, nth(s_A, h, 7))
                        pa = pA.rearrange("p (n k i) -> p n k i", n=NB, k=2)
                        for p0 in (0, 64):
                            r = slice(p0, p0 + 32)
                            dve.tensor_copy(A5[r, :, :], pa[r, :, 0, :])
                            last = dve.tensor_copy(AqT[r, :, p0 + 32:p0 + 64], pa[r, :, 1, :])
                        last.then_inc(s_ev, 1)
                        t_add(h, 4)
                        scale(h, 6)
                        dve.wait_ge(s_T, nth(s_T, h, 5))
                        for q in range(4):
                            r = slice(32 * q, 32 * q + 32)
                            c0 = 32 * (q % 2)
                            dve.tensor_tensor(TC[r, :, c0:c0 + 32], TT[r, :, :], bc(cc[r, :], 32, 32), ALU.mult)
                        dve.wait_ge(s_m1, nth(s_m1, h, 6))
                        for p0 in (32, 96):
                            r = slice(p0, p0 + 32)
                            last = dve.tensor_tensor(M1[r, :, :],
                                                     pM1[r, 0:NB * 32].rearrange("p (n j) -> p n j", n=NB),
                                                     bc(nc_[r, :], 32, 32), ALU.mult)
                        last.then_inc(s_M, 1)
                        scale(h, 7)
                        dve.wait_ge(s_m2, nth(s_m2, h, 6))
                        for p0 in (0, 64):
                            r = slice(p0, p0 + 32)
                            last = dve.tensor_tensor(TC[r, :, 32:64],
                                                     pM3[r, 0:NB * 32].rearrange("p (n j) -> p n j", n=NB),
                                                     bc(cc[r, :], 32, 32), ALU.mult)
                        last.then_inc(s_T, 1)
                        for k, (app, blk, r, ps) in enumerate(((2, 0, slice(64, P), pM2), (4, 1, slice(0, P), pA),
                                                               (6, 1, slice(64, P), pM2))):
                            dve.wait_ge(s_app, nth(s_app, h, app))
                            if k == 2:
                                dve.wait_ge(s_R, nth(s_R, h, 3))
                            dve.tensor_tensor(seqs(R, blk, r), seqs(R, blk, r),
                                              ps[r, :].rearrange("p (b n) -> p b n", b=B), ALU.subtract)\
                               .then_inc(s_R, 1)
                        dve.tensor_scalar(t2[:, :], rqs[:, :], QSCALE, None, ALU.mult).then_inc(s_ms, 1)
                        dve.wait_ge(s_o, nth(s_o, h, 1))
                        dve.tensor_tensor(Q[:, :], pW[:, :], SG[:, :], ALU.mult).then_inc(s_z, 1)
                        dve.wait_ge(s_ms, nth(s_ms, h, 1))
                        dve.tensor_tensor(ms[:, :], t2[:, :], t2[:, :], ALU.mult).then_inc(s_ms, 1)
                        dve.wait_ge(s_ssz, nth(s_ssz, h, 1))
                        dve.wait_ge(s_ms, nth(s_ms, h, 2))
                        dve.tensor_tensor(ms[:, :], pM1[:, 0:NB], ms[:, :], ALU.mult).then_inc(s_ms, 1)
                        dve.wait_ge(s_ms, nth(s_ms, h, 3))
                        dve.tensor_scalar(ms[:, :], ms[:, :], 1.0 / DK, RMS_EPS, ALU.mult, ALU.add).then_inc(s_ms, 1)
                        dve.wait_ge(s_rms, nth(s_rms, h, 1))
                        dve.tensor_tensor(fr[:, :], t2[:, :], rms[:, :], ALU.mult).then_inc(s_ms, 1)
                        dve.wait_ge(s_ms, nth(s_ms, h, 5))
                        dve.tensor_tensor(diag, bc(fr, P, P), ident.unsqueeze(1).to_broadcast([P, NB, P]), ALU.mult)\
                           .then_inc(s_diag, 1)
                        dve.wait_ge(s_f, nth(s_f, h, 1))
                        dve.scalar_tensor_tensor(yT[:, bass.ds(h, 1), :].rearrange("p a t -> p (a t)"), Q[:, :],
                                                 nw[:, 0:1], pX[:, :], ALU.mult, ALU.mult).then_inc(s_y, 1)

                @block.tensor
                def _(pe):
                    def passed():
                        pe.sem_inc(s_passed, 1)

                    def project(h, k, ps):
                        for hf in range(2):
                            for c in range(DC):
                                last = pe.matmul(ps[:, hf * HALF:(hf + 1) * HALF], wh[:, k, c, :],
                                                 hT[:, c, hf * HALF:(hf + 1) * HALF], start=c == 0, stop=c == DC - 1)
                        last.then_inc(s_proj, 1)

                    def spread_decay(h, lv):
                        if lv:
                            pe.wait_ge(s_scaled, nth(s_scaled, h, lv))
                        for hf in range(2):
                            c0 = lv * NT + hf * HALF
                            last = pe.matmul(pW[:, hf * HALF:(hf + 1) * HALF], spread[:, :], dec[:, c0:c0 + HALF],
                                             start=True, stop=True)
                        last.then_inc(s_e, 1)

                    def products(h, lv):
                        s = 1 << lv
                        if lv < 6:
                            pe.wait_ge(s_ev, nth(s_ev, h, lv + 1))
                        pe.wait_ge(s_scaled, nth(s_scaled, h, lv + 1))
                        passed()
                        kq = KQ[:, lv % 2, :, :]
                        if lv < SMALL:
                            mv_ = kq.rearrange("p k (m u s) -> p k m u s", u=2, s=s)
                            for n in range(NB):
                                for q in range(4):
                                    t0 = n * P + 32 * q
                                    m0 = t0 // (2 * s)
                                    last = pe.matmul(pA[32 * q:32 * q + 32, n * 32:(n + 1) * 32], kq[:, 0, t0:t0 + 32],
                                                     mv_[:, :, m0:m0 + 16 // s, 1, :], start=True, stop=True)
                        elif lv == 5:
                            for n in range(NB):
                                for p0 in (0, 64):
                                    t0 = n * P + p0
                                    last = pe.matmul(pA[p0:p0 + 32, n * 64:(n + 1) * 64], kq[:, 0, t0:t0 + 32],
                                                     kq[:, :, t0 + 32:t0 + 64], start=True, stop=True)
                        elif lv == 6:
                            px = pX[0:64, :].rearrange("p (k n i) -> p k n i", k=2, n=NB)
                            for n in range(NB):
                                for k in range(2):
                                    last = pe.matmul(px[:, k, n, :], kq[:, 0, n * P:n * P + 64],
                                                     kq[:, k, n * P + 64:(n + 1) * P], start=True, stop=True)
                        else:
                            pe.wait_ge(s_big, nth(s_big, h, 1))
                            for b in range(B):
                                for k in range(2):
                                    last = pe.matmul(pX[:, k * HALF + b * P:k * HALF + (b + 1) * P],
                                                     kq[:, 0, b * T:b * T + P], kq[:, k, b * T + P:(b + 1) * T],
                                                     start=True, stop=True)
                        last.then_inc(s_A, 1)

                    def mult_1(h, lv):
                        if lv:
                            pe.wait_ge(s_T, nth(s_T, h, lv))
                        pe.wait_ge(s_ev, nth(s_ev, h, lv + 2))
                        passed()
                        for n in range(NB):
                            if lv < SMALL:
                                for q in range(4):
                                    r = slice(32 * q, 32 * q + 32)
                                    last = pe.matmul(pM1[r, n * 32:(n + 1) * 32], A[r, lv, n, :], Tm[r, n, :],
                                                     start=True, stop=True)
                            else:
                                for p0 in (0, 64):
                                    last = pe.matmul(pM1[p0 + 32:p0 + 64, n * 32:(n + 1) * 32], A5[p0:p0 + 32, n, :],
                                                     Tm[p0:p0 + 32, n, :], start=True, stop=True)
                        last.then_inc(s_m1, 1)

                    def mult_2(h, lv):
                        pe.wait_ge(s_M, nth(s_M, h, lv + 1))
                        passed()
                        for n in range(NB):
                            c = slice(n * 32, (n + 1) * 32)
                            if lv < SMALL:
                                for q in range(4):
                                    r = slice(32 * q, 32 * q + 32)
                                    pe.matmul(pM2[r, c], TT[r, n, :], M1[r, n, :], start=True, stop=True)
                                    last = pe.matmul(pM3[r, c], M1[r, n, :], TT[r, n, :], start=True, stop=True)
                            else:
                                for p0 in (0, 64):
                                    r = slice(p0 + 32, p0 + 64)
                                    last = pe.matmul(pM3[p0:p0 + 32, c], M1[r, n, :], TT[r, n, :],
                                                     start=True, stop=True)
                        last.then_inc(s_m2, 1)

                    with pe.Fori(0, H) as h:
                        pe.wait_ge(s_w, nth(s_w, h, 32))
                        pe.wait_ge(s_y, nth(s_y, h, 0))
                        project(h, 0, pX)
                        project(h, 1, pW)
                        pe.wait_ge(s_fir, nth(s_fir, h, 3))
                        project(h, 2, pX)
                        pe.wait_ge(s_fir, nth(s_fir, h, 6))
                        project(h, 3, pW)
                        for k, t in enumerate((sqk, sqq)):
                            pe.wait_ge(s_sq, nth(s_sq, h, k + 1))
                            for n in range(NB):
                                last = pe.matmul(pM1[:, k * NB + n:k * NB + n + 1], t[:, n * P:(n + 1) * P],
                                                 ones[:, 0:1], start=True, stop=True)
                            last.then_inc(s_ss, 1)
                        passed()
                        for n in range(NB):
                            for q in range(4):
                                t0 = n * P + 32 * q
                                last = pe.matmul(pA[32 * q:32 * q + 32, n * 32:(n + 1) * 32], K[:, t0:t0 + 32],
                                                 Q[:, t0:t0 + 32], start=True, stop=True)
                        last.then_inc(s_A, 1)
                        pe.wait_ge(s_dec, nth(s_dec, h, 48))
                        pe.wait_ge(s_silu, nth(s_silu, h, 3))
                        spread_decay(h, 0)
                        products(h, 0)
                        pe.wait_ge(s_silu, nth(s_silu, h, 4))
                        for n in range(NB):
                            last = pe.transpose(pX[:, n * P:(n + 1) * P], V[:, n * P:(n + 1) * P], ident)
                        last.then_inc(s_vt, 1)
                        for lv in range(1, SMALL):
                            spread_decay(h, lv)
                            mult_1(h, lv - 1)
                            products(h, lv)
                            mult_2(h, lv - 1)
                        spread_decay(h, 5)
                        mult_1(h, 4)
                        products(h, 5)
                        mult_2(h, 4)
                        spread_decay(h, 6)
                        mult_1(h, 5)
                        pe.wait_ge(s_R, nth(s_R, h, 1))
                        products(h, 6)
                        mult_2(h, 5)
                        spread_decay(h, 7)
                        products(h, 7)
                        pe.wait_ge(s_T, nth(s_T, h, 6))
                        pe.wait_ge(s_big, nth(s_big, h, 2))
                        passed()
                        lo_, up = slice(0, 64), slice(64, P)
                        k = 0
                        for blk in range(2):
                            if blk:
                                pe.wait_ge(s_dl, nth(s_dl, h, 2))
                                for b in range(B):
                                    last = pe.matmul(pA[:, b * P:(b + 1) * P], A7[:, b, :], dl[:, 2 * b, :],
                                                     start=True, stop=True)
                                last.then_inc(s_app, 1)
                                pe.wait_ge(s_R, nth(s_R, h, 3))
                                passed()
                            for b in range(B):
                                n = 2 * b + blk
                                last = pe.matmul(pM1[lo_, b * P:(b + 1) * P], TC[lo_, n, :], R[lo_, n, :],
                                                 start=True, stop=True)
                            last.then_inc(s_app, 1)
                            pe.wait_ge(s_dl, nth(s_dl, h, 1 + 2 * blk))
                            passed()
                            for b in range(B):
                                n = 2 * b + blk
                                last = pe.matmul(pM2[up, b * P:(b + 1) * P], A6[:, n, :], dl[lo_, n, :],
                                                 start=True, stop=True)
                            last.then_inc(s_app, 1)
                            pe.wait_ge(s_R, nth(s_R, h, 2 + 2 * blk))
                            passed()
                            for b in range(B):
                                n = 2 * b + blk
                                last = pe.matmul(pM3[up, b * P:(b + 1) * P], TC[up, n, :], R[up, n, :],
                                                 start=True, stop=True)
                            last.then_inc(s_app, 1)
                        pe.wait_ge(s_aq, nth(s_aq, h, 1))
                        pe.wait_ge(s_scaled, nth(s_scaled, h, 8))
                        for blk in range(2):
                            if blk:
                                pe.wait_ge(s_dl, nth(s_dl, h, 4))
                            for b in range(B):
                                n = 2 * b + blk
                                o = pW[:, n * P:(n + 1) * P]
                                last = pe.matmul(o, dl[:, n, :], AqT[:, n, :], start=True, stop=blk == 0)
                                if blk:
                                    last = pe.matmul(o, dl[:, n - 1, :], Aq7[:, b, :], start=False, stop=True)
                        last.then_inc(s_o, 1)
                        pe.wait_ge(s_sqz, nth(s_sqz, h, 1))
                        for n in range(NB):
                            last = pe.matmul(pM1[:, n:n + 1], sqk[:, n * P:(n + 1) * P], ones[:, 0:1],
                                             start=True, stop=True)
                        last.then_inc(s_ssz, 1)
                        pe.wait_ge(s_diag, nth(s_diag, h, 1))
                        for hf in range(2):
                            last = pe.matmul(pX[:, hf * HALF:(hf + 1) * HALF], ones[:, :],
                                             KQ[:, 0, 0, hf * HALF:(hf + 1) * HALF], start=True, stop=True)
                        last.then_inc(s_f, 1)

        rt_steps = []

        with ExitStack() as ffn:
            def fb(name, shape, dt=F32):
                return sb(name, shape, dt, where=ffn)

            wo = fb("wo", [P, H, D])
            oT = fb("oT", [P, DC, NT])
            gw = fb("gw", [P, DC, E])
            gbias = fb("gbias", [P, E])
            fc1 = fb("fc1", [P, DC, P])
            fc2 = fb("fc2", [P, D])
            up = fb("up", [P, DC, SHC * P])
            down = fb("down", [P, SHC, D])
            sc_, sbs = fb("sc_", [P, NB, E]), fb("sbs", [P, NB, E])
            top2 = fb("top2", [P, NB, G, 8])
            gs = fb("gs", [P, NB, G])
            cmp_, cnt = fb("cmp_", [P, NB, G]), fb("cnt", [P, NB, G])
            keep = fb("keep", [P, NB, G], I32)
            cand = fb("cand", [P, NB, E])
            top8 = fb("top8", [P, NB, 8])
            taken = fb("taken", [P, NB, E])
            wsum, winv = fb("wsum", [P, NB]), fb("winv", [P, NB])
            cwT = fb("cwT", [E, NT])
            xl = fb("xl", [P, NT])
            s_wo, s_fw, s_or, s_oT, s_ot, s_x1 = (sem(n) for n in ("s_wo", "s_fw", "s_or", "s_oT", "s_ot", "s_x1"))
            s_ln2, s_lg, s_sig, s_rt, s_cwt, s_cwc, s_cwd = (
                sem(n) for n in ("s_ln2", "s_lg", "s_sig", "s_rt", "s_cwt", "s_cwc", "s_cwd"))
            s_xl, s_xlc = sem("s_xl"), sem("s_xlc")

            def gate_out(act, row, ready, base, done):
                act.wait_ge(ready, base)
                for c, ps in enumerate((pX, pW)):
                    for b in range(B):
                        last = act.mul(oT[:, c, b * T:(b + 1) * T], ps[:, b * T:(b + 1) * T],
                                       modT[:, row + c, b:b + 1])
                last.then_inc(done, 1)

            def turn_out(pe, ready, done):
                pe.wait_ge(ready, 1)
                for n in range(NB):
                    ps = (pX, pW)[n // 4]
                    for c in range(DC):
                        c0 = (n % 4) * D + c * P
                        last = pe.transpose(ps[:, c0:c0 + P], oT[:, c, n * P:(n + 1) * P], ident)
                last.then_inc(done, 1)

            def add_in(dve, ready, done):
                dve.wait_ge(ready, 1)
                for k, ps in enumerate((pX, pW)):
                    last = dve.tensor_tensor(x[:, 4 * k:4 * k + 4, :], x[:, 4 * k:4 * k + 4, :],
                                             ps.rearrange("p (n f) -> p n f", n=4), ALU.add)
                last.then_inc(done, 1)

            with nc.Block() as block:
                @block.sync
                def _(sp):
                    sp.dma_start(wo[:, :, :], d["Wo"].rearrange("h p n -> p h n")).then_inc(s_wo, 16)
                    sp.dma_start(gw[:, :, :], d["gate_w"].rearrange("(c p) n -> p c n", p=P)).then_inc(s_fw, 16)
                    sp.dma_start(gbias[:, :], d["gate_bias"].to_broadcast([P, E])).then_inc(s_fw, 16)
                    sp.dma_start(fc1[:, :, :], d["fc1"].rearrange("(c p) n -> p c n", p=P)).then_inc(s_fw, 16)
                    sp.dma_start(fc2[:, :], d["fc2"]).then_inc(s_fw, 16)
                    sp.dma_start(up[:, :, :], d["up"].rearrange("(c p) n -> p c n", p=P)).then_inc(s_fw, 16)
                    sp.dma_start(down[:, :, :], d["down"].rearrange("(c p) n -> p c n", p=P)).then_inc(s_fw, 16)
                    sp.wait_ge(s_cwc, 1)
                    sp.dma_start(route_dram, cwT[:, :]).then_inc(s_cwd, 16)
                    sp.wait_ge(s_cwd, 16)
                    sp.wait_ge(s_fw, 6 * 16)

                @block.gpsimd
                def _(pool):
                    pool.wait_ge(s_ln2, 3)
                    pool.tensor_tensor(rstd[:, :], veps[:, :], halfs[:, 0, :], ALU.pow).then_inc(s_rstd, 1)

                @block.scalar
                def _(act):
                    gate_out(act, 4, s_or, 1, s_oT)
                    modulate(act, 1, 6)
                    act.wait_ge(s_lg, 1)
                    act.activation(sc_[:, :, :], pA[:, 0:NB * E].rearrange("p (n e) -> p n e", n=NB), ACT.Exp,
                                   scale=-1.0).then_inc(s_sig, 1)
                    act.wait_ge(s_xl, 1)
                    act.copy(xl[:, :], pX[:, :]).then_inc(s_xlc, 1)

                @block.vector
                def _(dve):
                    add_in(dve, s_ot, s_x1)
                    dve.wait_ge(s_x1, 1)
                    for n in range(NB):
                        last = dve.bn_stats(stats[:, n, :], x[:, n, :])
                    last.then_inc(s_ln2, 1)
                    dve.wait_ge(s_ln2, 1)
                    for n in range(NB):
                        last = dve.bn_aggr(mv[:, n, :], stats[:, n, :])
                    last.then_inc(s_ln2, 1)
                    dve.wait_ge(s_ln2, 2)
                    dve.tensor_scalar(veps[:, :], mv[:, :, 1], LN_EPS, None, ALU.add).then_inc(s_ln2, 1)
                    dve.wait_ge(s_rstd, 2)
                    for n in range(NB):
                        dve.tensor_scalar(xn[:, n, :], x[:, n, :], mv[:, n, 0:1], rstd[:, n:n + 1],
                                          ALU.subtract, ALU.mult).then_inc(s_xn, 1)
                    steps = 0

                    def step(ins):
                        nonlocal steps
                        steps += 1
                        ins.then_inc(s_rt, 1)
                        dve.wait_ge(s_rt, steps)

                    dve.wait_ge(s_fw, 6 * 16)
                    dve.wait_ge(s_sig, 1)
                    step(dve.tensor_scalar(sc_[:, :, :], sc_[:, :, :], 1.0, None, ALU.add))
                    step(dve.reciprocal(sc_[:, :, :], sc_[:, :, :]))
                    step(dve.tensor_tensor(sbs[:, :, :], sc_[:, :, :],
                                           gbias.unsqueeze(1).to_broadcast([P, NB, E]), ALU.add))
                    for n in range(NB):
                        for g in range(G):
                            last = dve.max(top2[:, n, g, :], sbs[:, n, g * EG:(g + 1) * EG])
                    step(last)
                    step(dve.tensor_tensor(gs[:, :, :], top2[:, :, :, 0], top2[:, :, :, 1], ALU.add))
                    step(dve.memset(cnt[:, :, :], 0.0))
                    for g in range(G):
                        one = gs[:, :, g:g + 1]
                        if g > 0:
                            dve.tensor_tensor(cmp_[:, :, 0:g], one.to_broadcast([P, NB, g]), gs[:, :, 0:g], ALU.is_gt)
                        if g < G - 1:
                            dve.tensor_tensor(cmp_[:, :, g + 1:], one.to_broadcast([P, NB, G - 1 - g]),
                                              gs[:, :, g + 1:], ALU.is_ge)
                        step(dve.memset(cmp_[:, :, g:g + 1], 0.0))
                        step(dve.tensor_tensor(cnt[:, :, :], cnt[:, :, :], cmp_[:, :, :], ALU.add))
                    dve.memset(cand[:, :, :], FILL)
                    step(dve.tensor_scalar(keep[:, :, :], cnt[:, :, :], float(TOPG), None, ALU.is_lt))
                    step(dve.copy_predicated(cand.rearrange("p n (g e) -> p n g e", g=G),
                                             keep.unsqueeze(3).to_broadcast([P, NB, G, EG]),
                                             sbs.rearrange("p n (g e) -> p n g e", g=G)))
                    for n in range(NB):
                        last = dve.max(top8[:, n, :], cand[:, n, :])
                    step(last)
                    for n in range(NB):
                        last = dve.match_replace(taken[:, n, :], top8[:, n, :], cand[:, n, :], TAKEN)
                    step(last)
                    step(dve.scalar_tensor_tensor(cand[:, :, :], taken[:, :, :], TAKEN, sc_[:, :, :],
                                                  ALU.is_ge, ALU.mult))
                    step(dve.tensor_reduce(wsum[:, :], cand[:, :, :], AX.X, ALU.add))
                    step(dve.reciprocal(winv[:, :], wsum[:, :]))
                    step(dve.tensor_scalar(winv[:, :], winv[:, :], ROUTED_SCALE, None, ALU.mult))
                    dve.tensor_tensor(cand[:, :, :], cand[:, :, :], winv.unsqueeze(2).to_broadcast([P, NB, E]),
                                      ALU.mult).then_inc(s_rt, 1)
                    dve.wait_ge(s_cwt, 1)
                    dve.tensor_copy(cwT[:, :], pW[0:E, :]).then_inc(s_cwc, 1)
                    rt_steps.append(steps + 1)

                @block.tensor
                def _(pe):
                    pe.wait_ge(s_wo, 16)
                    for c, ps in enumerate((pX, pW)):
                        for hf in range(2):
                            for hd in range(H):
                                last = pe.matmul(ps[:, hf * HALF:(hf + 1) * HALF], wo[:, hd, c * P:(c + 1) * P],
                                                 yT[:, hd, hf * HALF:(hf + 1) * HALF], start=hd == 0, stop=hd == H - 1)
                    last.then_inc(s_or, 1)
                    turn_out(pe, s_oT, s_ot)
                    pe.wait_ge(s_x1, 1)
                    turn_in(pe, 1)
                    pe.wait_ge(s_fw, 6 * 16)
                    pe.wait_ge(s_hT, 2 * B)
                    for n in range(NB):
                        for c in range(DC):
                            last = pe.matmul(pA[:, n * E:(n + 1) * E], hT[:, c, n * P:(n + 1) * P], gw[:, c, :],
                                             start=c == 0, stop=c == DC - 1)
                    last.then_inc(s_lg, 1)
                    for hf in range(2):
                        for c in range(DC):
                            last = pe.matmul(pX[:, hf * HALF:(hf + 1) * HALF], fc1[:, c, :],
                                             hT[:, c, hf * HALF:(hf + 1) * HALF], start=c == 0, stop=c == DC - 1)
                    last.then_inc(s_xl, 1)
                    pe.wait_ge(s_rt, rt_steps[0])
                    for n in range(NB):
                        last = pe.transpose(pW[0:E, n * P:(n + 1) * P], cand[:, n, :], ident)
                    last.then_inc(s_cwt, 1)

            w1 = [fb(f"w1_{k}", [P, P]) for k in range(2)]
            w2 = [fb(f"w2_{k}", [P, P]) for k in range(2)]
            cwb = [fb(f"cwb{k}", [P, NT]) for k in range(2)]
            rl = [fb(f"rl{k}", [P, NT]) for k in range(2)]
            hw = [fb(f"hw{k}", [P, NT]) for k in range(2)]
            zero = fb("zero", [P, P])
            PH = (pX, pW)
            pY = (pM1, pM2)
            rlu = fb("rlu", [P, SHC, NT])
            s_in = [sem(f"s_in{k}") for k in range(2)]
            s_up = [sem(f"s_up{k}") for k in range(2)]
            s_rl = [sem(f"s_rl{k}") for k in range(2)]
            s_cm = [sem(f"s_cm{k}") for k in range(2)]
            s_hw = [sem(f"s_hw{k}") for k in range(2)]
            s_dn = [sem(f"s_dn{k}") for k in range(2)]
            s_z0, s_yl, s_ylc, s_sh, s_shr, s_shs, s_fo, s_fT, s_ft, s_fin, s_out = (
                sem(n) for n in ("s_z0", "s_yl", "s_ylc", "s_sh", "s_shr", "s_shs", "s_fo", "s_fT", "s_ft", "s_fin",
                                 "s_out"))

            with nc.Block() as block:
                @block.sync
                def _(sp):
                    for k in range(2):
                        for s in (s_dn[k], s_hw[k], s_rl[k]):
                            sp.sem_inc(s, 1)
                    with sp.Fori(0, E // 2) as i:
                        for k in range(2):
                            e = 2 * i + k
                            sp.wait_ge(s_dn[k], i + 1)
                            sp.dma_start(w1[k][:, :], d["w1"][bass.ds(e, 1)].rearrange("a p n -> (a p) n"))\
                              .then_inc(s_in[k], 16)
                            sp.dma_start(w2[k][:, :], d["w2"][bass.ds(e, 1)].rearrange("a p n -> (a p) n"))\
                              .then_inc(s_in[k], 16)
                            sp.dma_start(cwb[k][:, :], route_dram[bass.ds(e, 1), :].to_broadcast([P, NT]))\
                              .then_inc(s_in[k], 16)
                    sp.wait_ge(s_fin, 1)
                    sp.dma_start(out.rearrange("(n p) f -> p n f", p=P), x[:, :, :]).then_inc(s_out, 16)
                    sp.wait_ge(s_out, 16)

                @block.gpsimd
                def _(pool):
                    pool.memset(zero[:, :], 0.0).then_inc(s_z0, 1)

                @block.scalar
                def _(act):
                    with act.Fori(0, E // 2) as i:
                        for k in range(2):
                            act.wait_ge(s_up[k], i + 1)
                            act.wait_ge(s_hw[k], i + 1)
                            act.activation(rl[k][:, :], PH[k][:, :], ACT.Relu).then_inc(s_rl[k], 1)
                    act.wait_ge(s_yl, 1)
                    act.copy(xl[:, 0:HALF], pM1[:, :])
                    act.copy(xl[:, HALF:], pM2[:, :]).then_inc(s_ylc, 1)
                    for j in range(SHC):
                        act.wait_ge(s_sh, j + 1)
                        act.activation(rlu[:, j, :], PH[j % 2][:, :], ACT.Relu).then_inc(s_shr, 1)
                        act.wait_ge(s_shr, j + 1)
                        act.activation(rlu[:, j, :], rlu[:, j, :], ACT.Square).then_inc(s_shs, 1)
                    gate_out(act, 10, s_fo, 1, s_fT)

                @block.vector
                def _(dve):
                    with dve.Fori(0, E // 2) as i:
                        for k in range(2):
                            dve.wait_ge(s_in[k], 48 * i + 48)
                            dve.wait_ge(s_rl[k], i + 2)
                            dve.wait_ge(s_dn[k], i + 1)
                            dve.tensor_tensor(hw[k][:, :], rl[k][:, :], cwb[k][:, :], ALU.mult).then_inc(s_cm[k], 1)
                            dve.wait_ge(s_cm[k], i + 1)
                            dve.tensor_tensor(hw[k][:, :], hw[k][:, :], rl[k][:, :], ALU.mult).then_inc(s_hw[k], 1)
                    add_in(dve, s_ft, s_fin)

                @block.tensor
                def _(pe):
                    pe.wait_ge(s_z0, 1)
                    for hf in range(2):
                        pe.matmul(pY[hf][:, :], zero[:, :], xl[:, hf * HALF:(hf + 1) * HALF], start=True, stop=False,
                                  skip_group_check=True)
                    with pe.Fori(0, E // 2) as i:
                        for k in range(2):
                            pe.wait_ge(s_in[k], 48 * i + 48)
                            pe.wait_ge(s_rl[k], i + 1)
                            for hf in range(2):
                                last = pe.matmul(PH[k][:, hf * HALF:(hf + 1) * HALF], w1[k][:, :],
                                                 xl[:, hf * HALF:(hf + 1) * HALF], start=True, stop=True)
                            last.then_inc(s_up[k], 1)
                        for k in range(2):
                            pe.wait_ge(s_hw[k], i + 2)
                            for hf in range(2):
                                last = pe.matmul(pY[hf][:, :], w2[k][:, :], hw[k][:, hf * HALF:(hf + 1) * HALF],
                                                 start=False, stop=False, skip_group_check=True)
                            last.then_inc(s_dn[k], 1)
                    for hf in range(2):
                        last = pe.matmul(pY[hf][:, :], zero[:, :], xl[:, hf * HALF:(hf + 1) * HALF],
                                         start=False, stop=True, skip_group_check=True)
                    last.then_inc(s_yl, 1)
                    for j in range(SHC):
                        if j < 2:
                            pe.wait_ge(s_rl[j], E // 2 + 1)
                        else:
                            pe.wait_ge(s_shr, j - 1)
                        for hf in range(2):
                            for c in range(DC):
                                last = pe.matmul(PH[j % 2][:, hf * HALF:(hf + 1) * HALF], up[:, c, j * P:(j + 1) * P],
                                                 hT[:, c, hf * HALF:(hf + 1) * HALF], start=c == 0, stop=c == DC - 1)
                        last.then_inc(s_sh, 1)
                    pe.wait_ge(s_shs, SHC)
                    pe.wait_ge(s_ylc, 1)
                    for c in range(DC):
                        for hf in range(2):
                            r = slice(hf * HALF, (hf + 1) * HALF)
                            for j in range(SHC):
                                pe.matmul(PH[c][:, r], down[:, j, c * P:(c + 1) * P], rlu[:, j, r],
                                          start=j == 0, stop=False)
                            last = pe.matmul(PH[c][:, r], fc2[:, c * P:(c + 1) * P], xl[:, r], start=False, stop=True)
                    last.then_inc(s_fo, 1)
                    turn_out(pe, s_fT, s_ft)


def kernel(**inputs):
    import numpy as _np
    import concourse.bacc as _bacc
    from concourse import mybir as _mybir
    from concourse.bass_utils import run_bass_kernel_spmd as _run

    a = {k: _np.asarray(v) for k, v in inputs.items()}
    at, ff = "L0_attn_", "L0_ffn_"

    def by_head(w):
        return w.reshape(DC, P, H, DK).transpose(2, 1, 0, 3)

    cw = _np.zeros((H, P, 16), _np.float32)
    for k, n in enumerate(("conv_k", "conv_q", "conv_v")):
        cw[:, :, 4 * k:4 * k + 4] = a[at + n].reshape(H, P, KW)
    cw[:, :, 12] = a[at + "bg"].reshape(H, P)
    floats, masks = shape_constants()
    arrays = {
        "x": a[at + "hidden_states"].reshape(NT, D),
        "cT": a["L0_c"].T,
        "wmod": a["L0_wmod"],
        "Wh": _np.stack([by_head(a[at + n]) for n in ("Wk", "Wq", "Wv", "Wg")], axis=2),
        "cw": cw,
        "Wf1": a[at + "Wf1"], "Wf2": a[at + "Wf2"], "Wb": a[at + "Wb"],
        "dt": a[at + "dt_bias"].reshape(P, 1),
        "A_log": _np.repeat(a[at + "A_log"], NG).reshape(P, 1),
        "norm_w": a[at + "norm_w"].reshape(P, 1),
        "Wo": a[at + "Wo"].reshape(H, DK, D),
        "gate_w": a[ff + "gate_w"].T, "gate_bias": a[ff + "gate_bias"].reshape(1, E),
        "fc1": a[ff + "fc1_w"].T, "fc2": a[ff + "fc2_w"].T,
        "w1": a[ff + "w1"].transpose(0, 2, 1), "w2": a[ff + "w2"].transpose(0, 2, 1),
        "up": a[ff + "shared_up_w"].T, "down": a[ff + "shared_down_w"].T,
        "floats": floats, "masks": masks,
    }
    arrays = {k: _np.ascontiguousarray(v) for k, v in arrays.items()}
    nc = _bacc.Bacc("TRN2", target_bir_lowering=False, num_devices=1)
    args = {k: nc.dram_tensor(k + "_dram", v.shape, _mybir.dt.from_np(v.dtype), kind="ExternalInput").ap()
            for k, v in arrays.items()}
    out = nc.dram_tensor("out_dram", (NT, D), F32, kind="ExternalOutput").ap()
    build(nc, args, out)
    r = _run(nc, [{k + "_dram": v for k, v in arrays.items()}], core_ids=[0])
    return r.results[0]["out_dram"].reshape(B, T, D)
```

```python
from contextlib import ExitStack

import numpy as np
import concourse.bass as bass
from concourse import mybir

ALU = mybir.AluOpType
ACT = mybir.ActivationFunctionType
F32 = mybir.dt.float32
I32 = mybir.dt.int32
AX = mybir.AxisListType

P = 128
B, T, D = 4, 256, 256
NT = B * T
NB = NT // P
DC = D // P
HALF = 512
H, DK = 16, 128
NG = 8
GC = DK // NG
LEVELS = 8
SMALL = 5
KW = 4
E, G, EG, TOPG, TOPK = 32, 4, 8, 2, 8
SHC = 4
ROUTED_SCALE = 2.5
QSCALE = DK ** -0.5
LN_EPS, L2_EPS, RMS_EPS = 1e-5, 1e-6, 1e-5
FILL = -3.0e38
TAKEN = 3.0e38


def shape_constants():
    ident = np.eye(P, dtype=np.float32)
    ident32 = np.tile(np.eye(32, dtype=np.float32), (4, 1))
    floats = np.concatenate([ident, ident32], axis=1)
    masks = np.zeros((P, SMALL * 16 + 32), np.int32)
    for lv in range(SMALL):
        s = 1 << lv
        for c in range(16):
            i = (c // s) * 2 * s + s + c % s
            for p in range(P):
                j = p % 32
                masks[p, lv * 16 + c] = int(j // (2 * s) == i // (2 * s) and j % (2 * s) < s)
    masks[:, SMALL * 16:] = ident32.astype(np.int32)
    return floats, masks


def build(nc, d, out):
    ctx = ExitStack()
    with ctx:
        def sb(name, shape, dt=F32, where=ctx):
            return where.enter_context(nc.sbuf_tensor(name, shape, dt))[(slice(None),) * len(shape)]

        def pb(name, cols):
            return ctx.enter_context(nc.psum_tensor(name, [P, cols], F32))[:, :]

        def sem(name):
            return ctx.enter_context(nc.semaphore(name))

        pX, pW = pb("pX", 2 * HALF), pb("pW", 2 * HALF)
        pM = pb("pM", 4 * HALF)
        pM1, pM2, pM3, pA = (pM[:, k * HALF:(k + 1) * HALF] for k in range(4))

        decay_dram = nc.dram_tensor("decay_dram", [P, LEVELS, NT], F32, kind="Internal").ap()
        route_dram = nc.dram_tensor("route_dram", [E, NT], F32, kind="Internal").ap()

        x = sb("x", [P, NB, D])
        hT = sb("hT", [P, DC, NT])
        modT = sb("modT", [P, 12, B])
        consts = sb("consts", [P, P + 32])
        masks = sb("masks", [P, SMALL * 16 + 32], I32)
        ident, ident32 = consts[:, 0:P], consts[:, P:P + 32]
        ones = sb("ones", [P, P])
        beta = sb("beta", [P, NB, H])
        attn = sb("attn", [P, NB, D])
        gates = sb("gates", [P, 2, B, D])
        nw = sb("nw", [P, 1])
        stats = sb("stats", [P, NB, 6])
        mv = sb("mv", [P, NB, 2])
        veps = sb("veps", [P, NB])
        rstd = sb("rstd", [P, NB])
        halfs = sb("halfs", [P, 2, NB])
        xn = sb("xn", [P, NB, D])
        gw = sb("gw", [P, DC, E])
        gbias = sb("gbias", [P, E])
        fc1 = sb("fc1", [P, DC, P])
        fc2 = sb("fc2", [P, D])
        up = sb("up", [P, DC, SHC * P])
        down = sb("down", [P, SHC, D])
        s_fw = sem("s_fw")

        s_x, s_mod_in, s_const, s_gw = (sem(n) for n in ("s_x", "s_mod_in", "s_const", "s_gw"))
        s_set, s_siluc, s_modps, s_mod = (sem(n) for n in ("s_set", "s_siluc", "s_modps", "s_mod"))
        s_ln, s_rstd, s_xn, s_xT, s_hT = (sem(n) for n in ("s_ln", "s_rstd", "s_xn", "s_xT", "s_hT"))
        s_gp, s_f1c, s_exp1, s_sp, s_a = (sem(n) for n in ("s_gp", "s_f1c", "s_exp1", "s_sp", "s_a"))
        s_lev, s_stored, s_gd, s_gps, s_gates = (sem(n) for n in ("s_lev", "s_stored", "s_gd", "s_gps", "s_gates"))

        def layer_norm(dve, done, base):
            for n in range(NB):
                last = dve.bn_stats(stats[:, n, :], x[:, n, :])
            last.then_inc(done, 1)
            dve.wait_ge(done, base + 1)
            for n in range(NB):
                last = dve.bn_aggr(mv[:, n, :], stats[:, n, :])
            last.then_inc(done, 1)
            dve.wait_ge(done, base + 2)
            dve.tensor_scalar(veps[:, :], mv[:, :, 1], LN_EPS, None, ALU.add).then_inc(done, 1)
            dve.wait_ge(s_rstd, (base // 3) + 1)
            for n in range(NB):
                dve.tensor_scalar(xn[:, n, :], x[:, n, :], mv[:, n, 0:1], rstd[:, n:n + 1],
                                  ALU.subtract, ALU.mult).then_inc(s_xn, 1)

        def turn_in(pe, base):
            for n in range(NB):
                pe.wait_ge(s_xn, base * NB + n + 1)
                for c, ps in enumerate((pX, pW)):
                    last = pe.transpose(ps[:, n * P:(n + 1) * P], xn[:, n, c * P:(c + 1) * P], ident)
                last.then_inc(s_xT, 1)

        def modulate(act, base, row):
            for b in range(B):
                act.wait_ge(s_xT, base * NB + 4 * (b // 2) + 4)
                for c, ps in enumerate((pX, pW)):
                    last = act.activation(hT[:, c, b * T:(b + 1) * T], ps[:, b * T:(b + 1) * T], ACT.Identity,
                                          bias=modT[:, row + c, b:b + 1], scale=modT[:, row + 2 + c, b:b + 1])
                last.then_inc(s_hT, 1)

        with ExitStack() as first:
            cT = sb("cT", [P, DC, B], where=first)
            siluc = sb("siluc", [P, DC, B], where=first)
            wmod = sb("wmod", [P, DC, 12 * P], where=first)
            gsign = sb("gsign", [P, 4, B], where=first)
            gmag = sb("gmag", [P, 4, B], where=first)
            wf1 = sb("wf1", [P, DC, P], where=first)
            wf2 = sb("wf2", [P, P], where=first)
            wb = sb("wb", [P, DC, H], where=first)
            dtb = sb("dtb", [P, 1], where=first)
            alog = sb("alog", [P, 1], where=first)
            nega = sb("nega", [P, 1], where=first)
            f1 = sb("f1", [P, NT], where=first)
            gx = sb("gx", [P, NT], where=first)
            u = sb("u", [P, NT], where=first)
            v1 = sb("v1", [P, NT], where=first)
            v2 = sb("v2", [P, NT], where=first)
            lev = sb("lev", [P, LEVELS, NT], where=first)
            pre = sb("pre", [P, NT], where=first)
            suf = sb("suf", [P, NT], where=first)
            gdiag = sb("gdiag", [P, 4, B, P], where=first)
            s_modc, s_gx, s_own = sem("s_modc"), sem("s_gx"), sem("s_own")

            with nc.Block() as block:
                @block.sync
                def _(sp):
                    sp.dma_start(cT[:, :, :], d["cT"].rearrange("(c p) b -> p c b", p=P)).then_inc(s_mod_in, 16)
                    sp.dma_start(wmod[:, :, :], d["wmod"].rearrange("(c p) n -> p c n", p=P)).then_inc(s_mod_in, 16)
                    sp.dma_start(x[:, :, :], d["x"].rearrange("(n p) f -> p n f", p=P)).then_inc(s_x, 16)
                    sp.dma_start(consts[:, :], d["floats"]).then_inc(s_const, 16)
                    sp.dma_start(masks[:, :], d["masks"]).then_inc(s_const, 16)
                    for t, n in ((wf1[:, :, :], "Wf1"), (wb[:, :, :], "Wb")):
                        sp.dma_start(t, d[n].rearrange("(c p) n -> p c n", p=P)).then_inc(s_gw, 16)
                    sp.dma_start(wf2[:, :], d["Wf2"]).then_inc(s_gw, 16)
                    sp.dma_start(dtb[:, :], d["dt"]).then_inc(s_gw, 16)
                    sp.dma_start(alog[:, :], d["A_log"]).then_inc(s_gw, 16)
                    sp.dma_start(nw[:, :], d["norm_w"]).then_inc(s_gw, 16)
                    for lv in range(LEVELS):
                        sp.wait_ge(s_lev, lv + 1)
                        sp.dma_start(decay_dram[:, lv, :], lev[:, lv, :]).then_inc(s_stored, 16)
                    sp.wait_ge(s_stored, 16 * LEVELS)

                @block.gpsimd
                def _(pool):
                    pool.memset(halfs[:, 0, :], -0.5)
                    pool.memset(halfs[:, 1, :], 0.5)
                    pool.memset(attn[:, :, :], 0.0)
                    pool.memset(ones[:, :], 1.0).then_inc(s_set, 1)
                    pool.wait_ge(s_set, 1)
                    pool.wait_ge(s_ln, 3)
                    pool.tensor_tensor(rstd[:, :], veps[:, :], halfs[:, 0, :], ALU.pow).then_inc(s_rstd, 1)

                @block.scalar
                def _(act):
                    act.wait_ge(s_mod_in, 32)
                    act.activation(siluc[:, :, :], cT[:, :, :], ACT.Silu).then_inc(s_siluc, 1)
                    act.wait_ge(s_mod, 1)
                    modulate(act, 0, 0)
                    act.wait_ge(s_gw, 6 * 16)
                    act.activation(nega[:, :], alog[:, :], ACT.Exp).then_inc(s_exp1, 1)
                    act.wait_ge(s_gx, 1)
                    act.activation(u[:, :], gx[:, :], ACT.Abs).then_inc(s_exp1, 1)
                    act.wait_ge(s_exp1, 2)
                    act.activation(u[:, :], u[:, :], ACT.Exp, scale=-1.0).then_inc(s_exp1, 1)
                    act.wait_ge(s_gp, 3)
                    act.activation(beta[:, :, :], pA[:, 64:64 + NB * H].rearrange("p (n h) -> p n h", n=NB),
                                   ACT.Exp, scale=-1.0).then_inc(s_exp1, 1)
                    act.wait_ge(s_sp, 1)
                    act.activation(pre, v1[:, :], ACT.Exp, scale=nega[:, 0:1]).then_inc(s_a, 1)
                    act.wait_ge(s_gps, 1)
                    for k in range(2):
                        for c in range(DC):
                            r = 2 * k + c
                            last = act.copy(gates[:, k, :, c * P:(c + 1) * P],
                                            pM[:, r * HALF:(r + 1) * HALF].rearrange("p (b n) -> p b n", b=B))
                    last.then_inc(s_gates, 1)

                @block.vector
                def _(dve):
                    dve.wait_ge(s_x, 16)
                    layer_norm(dve, s_ln, 0)
                    dve.wait_ge(s_modps, 1)
                    dve.tensor_copy(modT[:, :, :], pA[:, 0:48].rearrange("p (j b) -> p j b", b=B)).then_inc(s_modc, 1)
                    dve.wait_ge(s_modc, 1)
                    for r in (2, 8):
                        dve.tensor_scalar(modT[:, r:r + 2, :], modT[:, r:r + 2, :], 1.0, None, ALU.add)
                    for k, r in enumerate((4, 10)):
                        gate = modT[:, r:r + 2, :]
                        dve.tensor_scalar(gsign[:, 2 * k:2 * k + 2, :], gate, 0.0, 2.0, ALU.is_ge, ALU.mult)
                        last = dve.scalar_tensor_tensor(gmag[:, 2 * k:2 * k + 2, :], gate, -1.0, gate, ALU.mult, ALU.max)
                    last.then_inc(s_own, 1)
                    dve.wait_ge(s_own, 1)
                    dve.tensor_scalar(gsign[:, :, :], gsign[:, :, :], -1.0, None, ALU.add).then_inc(s_own, 1)
                    dve.wait_ge(s_own, 2)
                    for k, r in enumerate((4, 10)):
                        last = dve.scalar_tensor_tensor(modT[:, r:r + 2, :], gmag[:, 2 * k:2 * k + 2, :], 0.25,
                                                        gsign[:, 2 * k:2 * k + 2, :], ALU.max, ALU.mult)
                    last.then_inc(s_mod, 1)
                    dve.wait_ge(s_const, 32)
                    dve.wait_ge(s_mod, 1)
                    for k, r in enumerate((4, 10)):
                        last = dve.tensor_tensor(gdiag[:, 2 * k:2 * k + 2, :, :],
                                                 modT[:, r:r + 2, :].unsqueeze(3).to_broadcast([P, 2, B, P]),
                                                 ident.unsqueeze(1).unsqueeze(1).to_broadcast([P, 2, B, P]), ALU.mult)
                    last.then_inc(s_gd, 1)
                    dve.wait_ge(s_gp, 1)
                    dve.tensor_copy(f1[:, :], pX[:, :]).then_inc(s_f1c, 1)
                    dve.wait_ge(s_gp, 2)
                    dve.tensor_scalar(gx[:, :], pW[:, :], dtb[:, 0:1], None, ALU.add).then_inc(s_gx, 1)
                    own = 2

                    def step(ins):
                        nonlocal own
                        own += 1
                        ins.then_inc(s_own, 1)
                        dve.wait_ge(s_own, own)

                    dve.wait_ge(s_exp1, 3)
                    dve.tensor_scalar(nega[:, :], nega[:, :], -1.0, None, ALU.mult)
                    step(dve.tensor_scalar(v1[:, :], u[:, :], 2.0, None, ALU.add))
                    step(dve.reciprocal(v1[:, :], v1[:, :]))
                    step(dve.tensor_tensor(u[:, :], u[:, :], v1[:, :], ALU.mult))
                    step(dve.tensor_tensor(v2[:, :], u[:, :], u[:, :], ALU.mult))
                    step(dve.tensor_scalar(v1[:, :], v2[:, :], 1.0 / 15, None, ALU.mult))
                    for k in (13, 11, 9, 7, 5, 3):
                        step(dve.scalar_tensor_tensor(v1[:, :], v1[:, :], 1.0 / k, v2[:, :], ALU.add, ALU.mult))
                    step(dve.scalar_tensor_tensor(v1[:, :], v1[:, :], 1.0, u[:, :], ALU.add, ALU.mult))
                    step(dve.tensor_scalar(v2[:, :], gx[:, :], 0.0, None, ALU.max))
                    dve.scalar_tensor_tensor(v1[:, :], v1[:, :], 2.0, v2[:, :], ALU.mult, ALU.add).then_inc(s_sp, 1)
                    dve.wait_ge(s_exp1, 4)
                    step(dve.tensor_scalar(beta[:, :, :], beta[:, :, :], 1.0, None, ALU.add))
                    dve.reciprocal(beta[:, :, :], beta[:, :, :])
                    step(dve.memset(suf, 1.0))
                    dve.wait_ge(s_a, 1)
                    for lv in range(LEVELS):
                        s = 1 << lv
                        w, p_, f_ = (t.rearrange("p (m u s) -> p m u s", u=2, s=s) for t in (lev[:, lv, :], pre, suf))
                        dve.tensor_copy(w[:, :, 0, :], f_[:, :, 0, :])
                        dve.tensor_copy(w[:, :, 1, :], p_[:, :, 1, :]).then_inc(s_lev, 1)
                        if lv < LEVELS - 1:
                            m = NT // (2 * s)
                            step(dve.tensor_tensor(f_[:, :, 0, :], f_[:, :, 0, :],
                                                   p_[:, :, 1, s - 1:s].to_broadcast([P, m, s]), ALU.mult))
                            step(dve.tensor_tensor(p_[:, :, 1, :], p_[:, :, 1, :],
                                                   p_[:, :, 0, s - 1:s].to_broadcast([P, m, s]), ALU.mult))

                @block.tensor
                def _(pe):
                    pe.wait_ge(s_siluc, 1)
                    for j in range(12):
                        for c in range(DC):
                            last = pe.matmul(pA[:, j * B:(j + 1) * B], wmod[:, c, j * P:(j + 1) * P], siluc[:, c, :],
                                             start=c == 0, stop=c == DC - 1)
                    last.then_inc(s_modps, 1)
                    pe.wait_ge(s_const, 32)
                    turn_in(pe, 0)
                    pe.wait_ge(s_gw, 6 * 16)
                    pe.wait_ge(s_hT, B)
                    for hf in range(2):
                        for c in range(DC):
                            last = pe.matmul(pX[:, hf * HALF:(hf + 1) * HALF], wf1[:, c, :],
                                             hT[:, c, hf * HALF:(hf + 1) * HALF], start=c == 0, stop=c == DC - 1)
                    last.then_inc(s_gp, 1)
                    pe.wait_ge(s_f1c, 1)
                    for hf in range(2):
                        last = pe.matmul(pW[:, hf * HALF:(hf + 1) * HALF], wf2[:, :],
                                         f1[:, hf * HALF:(hf + 1) * HALF], start=True, stop=True)
                    last.then_inc(s_gp, 1)
                    for n in range(NB):
                        for c in range(DC):
                            last = pe.matmul(pA[:, 64 + n * H:64 + (n + 1) * H], hT[:, c, n * P:(n + 1) * P],
                                             wb[:, c, :], start=c == 0, stop=c == DC - 1)
                    last.then_inc(s_gp, 1)
                    pe.wait_ge(s_gd, 1)
                    pe.wait_ge(s_set, 1)
                    pe.wait_ge(s_exp1, 4)
                    for r in range(4):
                        last = pe.matmul(pM[:, r * HALF:(r + 1) * HALF], ones[:, :],
                                         gdiag[:, r, :, :].rearrange("p b n -> p (b n)"), start=True, stop=True)
                    last.then_inc(s_gps, 1)

        PER = {}

        def hsem(name, per):
            s = sem(name)
            PER[id(s)] = per
            return s

        def nth(s, h, k):
            return h * PER[id(s)] + k

        with ExitStack() as heads:
            def hb(name, shape, dt=F32):
                return sb(name, shape, dt, where=heads)

            wh = hb("wh", [P, 4, DC, P])
            cw = hb("cw", [P, 16])
            dec = hb("dec", [P, LEVELS, NT])
            wo, won = hb("wo", [P, D]), hb("won", [P, D])
            K, Q, V = hb("K", [P, NT]), hb("Q", [P, NT]), hb("V", [P, NT])
            SG = hb("SG", [P, NT])
            sqk, sqq = hb("sqk", [P, NT]), hb("sqq", [P, NT])
            Z, sqz = hb("Z", [P, NT]), hb("sqz", [P, NT])
            KQ = hb("KQ", [P, 2, 2, NT])
            A = hb("A", [P, SMALL, NB, 32])
            AqP = hb("AqP", [P, NB, 32])
            AqT = hb("AqT", [P, NB, P])
            A5 = hb("A5", [P, NB, 32])
            A6 = hb("A6", [64, NB, 64])
            A7, Aq7 = hb("A7", [P, B, P]), hb("Aq7", [P, B, P])
            X, XT = hb("X", [P, NB, 32]), hb("XT", [P, NB, 32])
            XC = hb("XC", [P, NB, 64])
            M1 = hb("M1", [P, NB, 32])
            R = hb("R", [P, NB, P])
            dl = hb("dl", [P, NB, P])
            sse = hb("sse", [P, 2 * NB])
            kn, rqs = hb("kn", [P, NB]), hb("rqs", [P, NB])
            bh, cc = hb("bh", [P, NB]), hb("cc", [P, NB])
            t2, ms, rms, fr = hb("t2", [P, NB]), hb("ms", [P, NB]), hb("rms", [P, NB]), hb("fr", [P, NB])

            s_w, s_wo, s_won = hsem("s_w", 32), hsem("s_wo", 16), hsem("s_won", 1)
            s_dec = [hsem(f"s_dec{lv}", 16) for lv in range(LEVELS)]
            s_proj = hsem("s_proj", 4)
            s_ss, s_vt = hsem("s_ss", 2), hsem("s_vt", 1)
            s_A = hsem("s_A", 9)
            s_m1, s_m2 = hsem("s_m1", 6), hsem("s_m2", 5)
            s_app = hsem("s_app", 7)
            s_o, s_ssz, s_ow = hsem("s_o", 1), hsem("s_ssz", 1), hsem("s_ow", 2)
            s_acc = hsem("s_acc", 2)
            s_tap, s_silu, s_sq = hsem("s_tap", 3), hsem("s_silu", 4), hsem("s_sq", 2)
            s_M, s_xc, s_big, s_dl, s_sqz = hsem("s_M", 5), hsem("s_xc", 2), hsem("s_big", 2), hsem("s_dl", 4), hsem("s_sqz", 1)
            s_fir, s_scaled, s_ev = hsem("s_fir", 9), hsem("s_scaled", 8), hsem("s_ev", 7)
            s_sse, s_c, s_R = hsem("s_sse", 1), hsem("s_c", 3), hsem("s_R", 4)
            s_X, s_XT, s_x0 = hsem("s_X", 6), hsem("s_XT", 5), hsem("s_x0", 1)
            s_z, s_ms = hsem("s_z", 1), hsem("s_ms", 5)
            s_root, s_rms, s_aq = hsem("s_root", 2), hsem("s_rms", 1), hsem("s_aq", 1)
            s_zero = sem("s_zero")
            s_passed, s_passed_dve, s_passed_pool, s_passed_sp = (
                sem(n) for n in ("s_passed", "s_passed_dve", "s_passed_pool", "s_passed_sp"))

            def bc(t, rows, n):
                return t.unsqueeze(2).to_broadcast([rows, t.shape[1], n])

            def later(t, s):
                return t.rearrange("p (m u s) -> p m u s", u=2, s=s)[:, :, 1, :]

            def seqs(t, blk, rows=slice(0, P)):
                return t.rearrange("p (b u) n -> p b u n", u=2)[rows, :, blk, :]

            def all_heads(eng, front, body):
                front(0)
                with eng.Fori(0, H - 1) as h:
                    body(h, True)
                body(H - 1, False)

            LO, UP = slice(0, 64), slice(64, P)

            with nc.Block() as block:
                @block.sync
                def _(sp):
                    def weights(h):
                        sp.dma_start(wh[:, :, :, :], d["Wh"][bass.ds(h, 1)].rearrange("a p w c n -> (a p) w c n"))\
                          .then_inc(s_w, 16)

                    def taps(h):
                        sp.dma_start(cw[:, :], d["cw"][bass.ds(h, 1)].rearrange("a p n -> (a p) n")).then_inc(s_w, 16)

                    def decays(h, lv):
                        rows = decay_dram[bass.ds(h * NG, NG), lv, :].unsqueeze(1).to_broadcast([NG, GC, NT])
                        sp.dma_start(dec[:, lv, :], rows).then_inc(s_dec[lv], 16)

                    def out_weights(h):
                        sp.dma_start(wo[:, :], d["Wo"][bass.ds(h, 1)].rearrange("a p n -> (a p) n")).then_inc(s_wo, 16)

                    weights(0)
                    taps(0)
                    for lv in range(LEVELS):
                        decays(0, lv)
                    out_weights(0)
                    with sp.Fori(0, H - 1) as h:
                        sp.wait_ge(s_proj, nth(s_proj, h, 4))
                        weights(h + 1)
                        sp.wait_ge(s_silu, nth(s_silu, h, 4))
                        sp.sem_inc(s_passed_sp, 1)
                        sp.wait_ge(s_fir, nth(s_fir, h, 9))
                        taps(h + 1)
                        for lv in range(LEVELS):
                            sp.wait_ge(s_scaled, nth(s_scaled, h, lv + 1))
                            decays(h + 1, lv)
                        sp.wait_ge(s_won, nth(s_won, h, 1))
                        out_weights(h + 1)
                    for t, n in ((gw[:, :, :], "gate_w"), (fc1[:, :, :], "fc1"), (up[:, :, :], "up"),
                                 (down[:, :, :], "down")):
                        sp.dma_start(t, d[n].rearrange("(c p) n -> p c n", p=P)).then_inc(s_fw, 16)
                    sp.dma_start(gbias[:, :], d["gate_bias"].to_broadcast([P, E])).then_inc(s_fw, 16)
                    sp.dma_start(fc2[:, :], d["fc2"]).then_inc(s_fw, 16)

                @block.gpsimd
                def _(pool):
                    for t in (A, AqP, AqT, XC):
                        last = pool.memset(t, 0.0)
                    last.then_inc(s_zero, 1)
                    pool.wait_ge(s_zero, 1)
                    pool.sem_inc(s_acc, 2)

                    def norms(h):
                        pool.wait_ge(s_sse, nth(s_sse, h, 1))
                        pool.tensor_tensor(kn[:, :], sse[:, 0:NB], halfs[:, 1, :], ALU.pow).then_inc(s_root, 1)
                        pool.tensor_tensor(rqs[:, :], sse[:, NB:2 * NB], halfs[:, 0, :], ALU.pow).then_inc(s_root, 1)

                    def body(h, following):
                        norms(h)
                        pool.wait_ge(s_ev, nth(s_ev, h, 6))
                        pool.sem_inc(s_passed_pool, 1)
                        for q in range(4):
                            r = slice(32 * q, 32 * q + 32)
                            last = pool.tensor_copy(AqT[r, :, r], AqP[r, :, :])
                        last.then_inc(s_aq, 1)
                        pool.wait_ge(s_ms, nth(s_ms, h, 4))
                        pool.tensor_tensor(rms[:, :], ms[:, :], halfs[:, 0, :], ALU.pow).then_inc(s_rms, 1)

                    all_heads(pool, lambda h: None, body)

                @block.scalar
                def _(act):
                    def tap(h, k, acc, ps):
                        if k == 0:
                            act.wait_ge(s_w, nth(s_w, h, 32))
                        act.wait_ge(s_proj, nth(s_proj, h, k + 1))
                        act.mul(acc, ps, cw[:, 4 * k + 3:4 * k + 4]).then_inc(s_tap, 1)

                    def silu(h, k, acc):
                        act.wait_ge(s_fir, nth(s_fir, h, 3 * k + 3))
                        act.activation(acc, acc, ACT.Silu).then_inc(s_silu, 1)

                    def square(h, k, t, to):
                        act.wait_ge(s_silu, nth(s_silu, h, k + 1))
                        act.activation(to, t, ACT.Square).then_inc(s_sq, 1)

                    def gate(h):
                        act.wait_ge(s_proj, nth(s_proj, h, 4))
                        act.activation(SG[:, :], pW[:, :], ACT.Silu, bias=cw[:, 12:13]).then_inc(s_silu, 1)

                    def front(h):
                        tap(h, 0, K[:, :], pX[:, :])
                        tap(h, 1, Q[:, :], pW[:, :])
                        silu(h, 0, K[:, :])
                        tap(h, 2, V[:, :], pX[:, :])
                        silu(h, 1, Q[:, :])
                        square(h, 0, K[:, :], sqk[:, :])
                        square(h, 1, Q[:, :], sqq[:, :])
                        gate(h)
                        silu(h, 2, V[:, :])

                    def rows(h, k):
                        app, blk, r, ps = ((1, 0, LO, pM1), (3, 0, UP, pM3), (5, 1, LO, pM1), (7, 1, UP, pM3))[k]
                        act.wait_ge(s_app, nth(s_app, h, app))
                        act.copy(seqs(dl, blk, r), ps[r, :].rearrange("p (b n) -> p b n", b=B)).then_inc(s_dl, 1)

                    def body(h, following):
                        pm = pM1[:, 0:NB * 32].rearrange("p (n j) -> p n j", n=NB)
                        for lv in range(1, SMALL):
                            act.wait_ge(s_m1, nth(s_m1, h, lv + 1))
                            act.copy(M1[:, :, :], pm).then_inc(s_M, 1)
                        act.wait_ge(s_m1, nth(s_m1, h, 6))
                        for p0 in (32, 96):
                            last = act.copy(M1[p0:p0 + 32, :, :], pm[p0:p0 + 32])
                        last.then_inc(s_M, 1)
                        act.wait_ge(s_XT, nth(s_XT, h, 5))
                        for q in range(4):
                            r = slice(32 * q, 32 * q + 32)
                            c0 = 32 * (q % 2)
                            last = act.copy(XC[r, :, c0:c0 + 32], XT[r, :, :])
                        last.then_inc(s_xc, 1)
                        act.wait_ge(s_A, nth(s_A, h, 8))
                        px64 = pX[0:64, :].rearrange("p (k n i) -> p k n i", k=2, n=NB)
                        act.copy(A6[:, :, :], px64[:, 0, :, :])
                        act.copy(AqT[0:64, :, 64:128], px64[:, 1, :, :]).then_inc(s_big, 1)
                        act.wait_ge(s_m2, nth(s_m2, h, 5))
                        for p0 in (0, 64):
                            r = slice(p0, p0 + 32)
                            last = act.mul(XC[r, :, 32:64], pM3[r, 0:NB * 32].rearrange("p (n j) -> p n j", n=NB), -1.0)
                        last.then_inc(s_xc, 1)
                        act.wait_ge(s_A, nth(s_A, h, 9))
                        px = pW.rearrange("p (k b i) -> p k b i", k=2, b=B)
                        act.copy(A7[:, :, :], px[:, 0, :, :])
                        act.copy(Aq7[:, :, :], px[:, 1, :, :]).then_inc(s_big, 1)
                        rows(h, 0)
                        if following:
                            tap(h + 1, 0, K[:, :], pX[:, :])
                        rows(h, 1)
                        if following:
                            tap(h + 1, 1, Q[:, :], pW[:, :])
                        act.wait_ge(s_wo, nth(s_wo, h, 16))
                        act.mul(won[:, :], wo[:, :], nw[:, 0:1]).then_inc(s_won, 1)
                        rows(h, 2)
                        if following:
                            silu(h + 1, 0, K[:, :])
                        rows(h, 3)
                        if following:
                            tap(h + 1, 2, V[:, :], pX[:, :])
                            square(h + 1, 0, K[:, :], sqk[:, :])
                            silu(h + 1, 1, Q[:, :])
                        act.wait_ge(s_z, nth(s_z, h, 1))
                        act.activation(sqz[:, :], Z[:, :], ACT.Square).then_inc(s_sqz, 1)
                        if following:
                            square(h + 1, 1, Q[:, :], sqq[:, :])
                            gate(h + 1)
                            silu(h + 1, 2, V[:, :])

                    act.wait_ge(s_zero, 1)
                    all_heads(act, front, body)

                @block.vector
                def _(dve):
                    dve.wait_ge(s_zero, 1)
                    mk = [masks[:, lv * 16:(lv + 1) * 16] for lv in range(SMALL)]

                    def fir(h, k, acc, ps, sh):
                        a, p_ = (t.rearrange("p (b t) -> p b t", b=B) for t in (acc, ps))
                        if sh == 1:
                            dve.wait_ge(s_tap, nth(s_tap, h, k + 1))
                        else:
                            dve.wait_ge(s_fir, nth(s_fir, h, 3 * k + sh - 1))
                        w = cw[:, 4 * k + 3 - sh:4 * k + 4 - sh]
                        dve.scalar_tensor_tensor(a[:, :, sh:], p_[:, :, 0:T - sh], w, a[:, :, sh:],
                                                 ALU.mult, ALU.add).then_inc(s_fir, 1)

                    def norms(h):
                        dve.tensor_copy(bh[:, :], beta[:, :, bass.ds(h, 1)].rearrange("p n a -> p (n a)"))\
                           .then_inc(s_c, 1)
                        dve.wait_ge(s_ss, nth(s_ss, h, 2))
                        dve.tensor_scalar(sse[:, :], pM3[:, 0:2 * NB], L2_EPS, None, ALU.add).then_inc(s_sse, 1)
                        dve.wait_ge(s_sse, nth(s_sse, h, 1))
                        dve.reciprocal(cc[:, :], sse[:, 0:NB]).then_inc(s_c, 1)
                        dve.wait_ge(s_c, nth(s_c, h, 2))
                        dve.tensor_tensor(cc[:, :], cc[:, :], bh[:, :], ALU.mult).then_inc(s_c, 1)
                        dve.wait_ge(s_c, nth(s_c, h, 3))
                        dve.tensor_tensor(X[:, :, :], ident32.unsqueeze(1).to_broadcast([P, NB, 32]), bc(cc, P, 32),
                                          ALU.mult).then_inc(s_X, 1)

                    def scale(h, lv):
                        if lv == 0:
                            dve.wait_ge(s_silu, nth(s_silu, h, 2))
                        else:
                            dve.wait_ge(s_A, nth(s_A, h, lv))
                        dve.wait_ge(s_dec[lv], nth(s_dec[lv], h, 16))
                        s = 1 << lv
                        dve.tensor_tensor(KQ[:, lv % 2, 0, :], dec[:, lv, :], K[:, :], ALU.mult)
                        dve.tensor_tensor(later(KQ[:, lv % 2, 1, :], s), later(dec[:, lv, :], s), later(Q[:, :], s),
                                          ALU.mult).then_inc(s_scaled, 1)

                    def own(h):
                        dve.wait_ge(s_A, nth(s_A, h, 1))
                        dve.sem_inc(s_passed_dve, 1)
                        dve.copy_predicated(AqP[:, :, :],
                                            masks[:, SMALL * 16:].unsqueeze(1).to_broadcast([P, NB, 32]),
                                            pA[:, 0:NB * 32].rearrange("p (n i) -> p n i", n=NB)).then_inc(s_ev, 1)

                    def add_head(h, k):
                        dve.wait_ge(s_ow, nth(s_ow, h, k + 1))
                        for m in range(4):
                            n = 4 * k + m
                            ps = (pM[:, 0:NT], pW)[k][:, m * D:(m + 1) * D]
                            last = dve.scalar_tensor_tensor(attn[:, n, :], ps, fr[:, n:n + 1], attn[:, n, :],
                                                            ALU.mult, ALU.add)
                        last.then_inc(s_acc, 1)

                    def pick(h, lv):
                        s = 1 << lv
                        dve.wait_ge(s_A, nth(s_A, h, lv + 2))
                        dve.sem_inc(s_passed_dve, 1)
                        ps = pA[:, 0:NB * 32].rearrange("p (n k m s) -> p n k m s", k=2, m=16 // s, s=s)
                        m = mk[lv].rearrange("p (m s) -> p m s", s=s).unsqueeze(1).to_broadcast([P, NB, 16 // s, s])
                        to = [t.rearrange("p n (m u s) -> p n m u s", u=2, s=s)[:, :, :, 1, :]
                              for t in (A[:, lv, :, :], AqP)]
                        for k in range(2):
                            last = dve.copy_predicated(to[k], m, ps[:, :, k, :, :])
                        last.then_inc(s_ev, 1)

                    def grow(h, lv):
                        if lv == 0:
                            dve.wait_ge(s_m1, nth(s_m1, h, 1))
                            dve.tensor_tensor(M1[:, :, :], pM1[:, 0:NB * 32].rearrange("p (n j) -> p n j", n=NB),
                                              bc(cc, P, 32), ALU.mult).then_inc(s_x0, 1)
                            dve.wait_ge(s_x0, nth(s_x0, h, 1))
                            m2 = M1[:, :, :]
                        else:
                            dve.wait_ge(s_m2, nth(s_m2, h, lv))
                            m2 = pM2[:, 0:NB * 32].rearrange("p (n j) -> p n j", n=NB)
                        dve.tensor_tensor(X[:, :, :], X[:, :, :], m2, ALU.subtract).then_inc(s_X, 1)
                        dve.wait_ge(s_X, nth(s_X, h, lv + 2))
                        dve.transpose(XT.rearrange("p n j -> p (n j)"), X.rearrange("p n j -> p (n j)"))\
                           .then_inc(s_XT, 1)

                    def take(h, k):
                        app, blk, r, ps = ((2, 0, UP, pM2), (4, 1, slice(0, P), pA), (6, 1, UP, pM2))[k]
                        dve.wait_ge(s_app, nth(s_app, h, app))
                        if k == 2:
                            dve.wait_ge(s_R, nth(s_R, h, 3))
                        dve.tensor_tensor(seqs(R, blk, r), seqs(R, blk, r),
                                          ps[r, :].rearrange("p (b n) -> p b n", b=B), ALU.subtract).then_inc(s_R, 1)

                    def front(h):
                        for k, (acc, ps) in enumerate(((K, pX), (Q, pW), (V, pX))):
                            for sh in (1, 2, 3):
                                fir(h, k, acc, ps, sh)
                        norms(h)
                        scale(h, 0)
                        own(h)

                    def body(h, following):
                        scale(h, 1)
                        pick(h, 0)
                        dve.wait_ge(s_vt, nth(s_vt, h, 1))
                        dve.wait_ge(s_root, nth(s_root, h, 2))
                        dve.tensor_tensor(R[:, :, :], pX.rearrange("p (n j) -> p n j", n=NB), bc(kn, P, P),
                                          ALU.mult).then_inc(s_R, 1)
                        scale(h, 2)
                        pick(h, 1)
                        grow(h, 0)
                        scale(h, 3)
                        pick(h, 2)
                        for lv in range(1, 3):
                            scale(h, lv + 3)
                            grow(h, lv)
                            pick(h, lv + 2)
                        scale(h, 6)
                        grow(h, 3)
                        dve.wait_ge(s_A, nth(s_A, h, 7))
                        pa = pA.rearrange("p (n k i) -> p n k i", n=NB, k=2)
                        for p0 in (0, 64):
                            r = slice(p0, p0 + 32)
                            dve.tensor_copy(A5[r, :, :], pa[r, :, 0, :])
                            last = dve.tensor_copy(AqT[r, :, p0 + 32:p0 + 64], pa[r, :, 1, :])
                        last.then_inc(s_ev, 1)
                        scale(h, 7)
                        grow(h, 4)
                        n = h + 1
                        take(h, 0)
                        if following:
                            fir(n, 0, K, pX, 1)
                            fir(n, 0, K, pX, 2)
                        take(h, 1)
                        if following:
                            fir(n, 0, K, pX, 3)
                            fir(n, 1, Q, pW, 1)
                        take(h, 2)
                        dve.tensor_scalar(t2[:, :], rqs[:, :], QSCALE, None, ALU.mult).then_inc(s_ms, 1)
                        if following:
                            fir(n, 1, Q, pW, 2)
                            fir(n, 1, Q, pW, 3)
                        dve.wait_ge(s_o, nth(s_o, h, 1))
                        dve.tensor_tensor(Z[:, :], pM[:, 0:NT], SG[:, :], ALU.mult).then_inc(s_z, 1)
                        dve.wait_ge(s_ms, nth(s_ms, h, 1))
                        dve.tensor_tensor(ms[:, :], t2[:, :], t2[:, :], ALU.mult).then_inc(s_ms, 1)
                        if following:
                            fir(n, 2, V, pX, 1)
                            fir(n, 2, V, pX, 2)
                            fir(n, 2, V, pX, 3)
                        dve.wait_ge(s_ssz, nth(s_ssz, h, 1))
                        dve.wait_ge(s_ms, nth(s_ms, h, 2))
                        dve.tensor_tensor(ms[:, :], pM3[:, 0:NB], ms[:, :], ALU.mult).then_inc(s_ms, 1)
                        dve.wait_ge(s_ms, nth(s_ms, h, 3))
                        dve.tensor_scalar(ms[:, :], ms[:, :], 1.0 / DK, RMS_EPS, ALU.mult, ALU.add).then_inc(s_ms, 1)
                        if following:
                            scale(n, 0)
                        dve.wait_ge(s_rms, nth(s_rms, h, 1))
                        dve.wait_ge(s_acc, nth(s_acc, h, 2))
                        dve.tensor_tensor(fr[:, :], t2[:, :], rms[:, :], ALU.mult).then_inc(s_ms, 1)
                        dve.wait_ge(s_ms, nth(s_ms, h, 5))
                        add_head(h, 0)
                        if following:
                            norms(n)
                            own(n)
                        add_head(h, 1)

                    all_heads(dve, front, body)

                @block.tensor
                def _(pe):
                    def passed():
                        pe.sem_inc(s_passed, 1)

                    def project(h, k, ps, hf):
                        for c in range(DC):
                            last = pe.matmul(ps[:, hf * HALF:(hf + 1) * HALF], wh[:, k, c, :],
                                             hT[:, c, hf * HALF:(hf + 1) * HALF], start=c == 0, stop=c == DC - 1)
                        if hf:
                            last.then_inc(s_proj, 1)

                    def squares(h, k, t):
                        pe.wait_ge(s_sq, nth(s_sq, h, k + 1))
                        for n in range(NB):
                            last = pe.matmul(pM3[:, k * NB + n:k * NB + n + 1], t[:, n * P:(n + 1) * P],
                                             ones[:, 0:1], start=True, stop=True)
                        last.then_inc(s_ss, 1)

                    def own_keys(h):
                        passed()
                        for n in range(NB):
                            for q in range(4):
                                t0 = n * P + 32 * q
                                last = pe.matmul(pA[32 * q:32 * q + 32, n * 32:(n + 1) * 32], K[:, t0:t0 + 32],
                                                 Q[:, t0:t0 + 32], start=True, stop=True)
                        last.then_inc(s_A, 1)

                    def products(h, lv, part):
                        s = 1 << lv
                        if part == 0:
                            if lv < 6:
                                pe.wait_ge(s_ev, nth(s_ev, h, lv + 1))
                            pe.wait_ge(s_scaled, nth(s_scaled, h, lv + 1))
                            passed()
                        blocks, seqs_ = range(4 * part, 4 * part + 4), range(2 * part, 2 * part + 2)
                        kq = KQ[:, lv % 2, :, :]
                        if lv < SMALL:
                            mv_ = kq.rearrange("p k (m u s) -> p k m u s", u=2, s=s)
                            for n in blocks:
                                for q in range(4):
                                    t0 = n * P + 32 * q
                                    m0 = t0 // (2 * s)
                                    last = pe.matmul(pA[32 * q:32 * q + 32, n * 32:(n + 1) * 32], kq[:, 0, t0:t0 + 32],
                                                     mv_[:, :, m0:m0 + 16 // s, 1, :], start=True, stop=True)
                        elif lv == 5:
                            for n in blocks:
                                for p0 in (0, 64):
                                    t0 = n * P + p0
                                    last = pe.matmul(pA[p0:p0 + 32, n * 64:(n + 1) * 64], kq[:, 0, t0:t0 + 32],
                                                     kq[:, :, t0 + 32:t0 + 64], start=True, stop=True)
                        elif lv == 6:
                            px = pX[0:64, :].rearrange("p (k n i) -> p k n i", k=2, n=NB)
                            for n in blocks:
                                for k in range(2):
                                    last = pe.matmul(px[:, k, n, :], kq[:, 0, n * P:n * P + 64],
                                                     kq[:, k, n * P + 64:(n + 1) * P], start=True, stop=True)
                        else:
                            for b in seqs_:
                                for k in range(2):
                                    last = pe.matmul(pW[:, k * HALF + b * P:k * HALF + (b + 1) * P],
                                                     kq[:, 0, b * T:b * T + P], kq[:, k, b * T + P:(b + 1) * T],
                                                     start=True, stop=True)
                        if part:
                            last.then_inc(s_A, 1)

                    def mult_1(h, lv):
                        if lv == 0:
                            pe.wait_ge(s_acc, nth(s_acc, h, 1))
                        pe.wait_ge(s_X, nth(s_X, h, lv + 1))
                        pe.wait_ge(s_ev, nth(s_ev, h, lv + 2))
                        passed()
                        for n in range(NB):
                            if lv < SMALL:
                                for q in range(4):
                                    r = slice(32 * q, 32 * q + 32)
                                    last = pe.matmul(pM1[r, n * 32:(n + 1) * 32], A[r, lv, n, :], X[r, n, :],
                                                     start=True, stop=True)
                            else:
                                for p0 in (0, 64):
                                    last = pe.matmul(pM1[p0 + 32:p0 + 64, n * 32:(n + 1) * 32], A5[p0:p0 + 32, n, :],
                                                     X[p0:p0 + 32, n, :], start=True, stop=True)
                        last.then_inc(s_m1, 1)

                    def mult_2(h, lv):
                        pe.wait_ge(s_M, nth(s_M, h, lv))
                        pe.wait_ge(s_XT, nth(s_XT, h, lv))
                        passed()
                        for n in range(NB):
                            c = slice(n * 32, (n + 1) * 32)
                            if lv < SMALL:
                                for q in range(4):
                                    r = slice(32 * q, 32 * q + 32)
                                    last = pe.matmul(pM2[r, c], XT[r, n, :], M1[r, n, :], start=True, stop=True)
                            else:
                                for p0 in (0, 64):
                                    r = slice(p0 + 32, p0 + 64)
                                    last = pe.matmul(pM3[p0:p0 + 32, c], M1[r, n, :], XT[r, n, :],
                                                     start=True, stop=True)
                        last.then_inc(s_m2, 1)

                    def solve(h, k):
                        blk, r, ps = ((0, LO, pM1), (0, UP, pM3), (1, LO, pM1), (1, UP, pM3))[k]
                        if k:
                            pe.wait_ge(s_R, nth(s_R, h, k + 1))
                        passed()
                        for b in range(B):
                            n = 2 * b + blk
                            last = pe.matmul(ps[r, b * P:(b + 1) * P], XC[r, n, :], R[r, n, :], start=True, stop=True)
                        last.then_inc(s_app, 1)

                    def explain(h, k):
                        pe.wait_ge(s_dl, nth(s_dl, h, k + 1))
                        passed()
                        for b in range(B):
                            if k == 1:
                                last = pe.matmul(pA[:, b * P:(b + 1) * P], A7[:, b, :], dl[:, 2 * b, :],
                                                 start=True, stop=True)
                            else:
                                n = 2 * b + k // 2
                                last = pe.matmul(pM2[UP, b * P:(b + 1) * P], A6[:, n, :], dl[LO, n, :],
                                                 start=True, stop=True)
                        last.then_inc(s_app, 1)

                    def outputs(h, blk):
                        for b in range(B):
                            n = 2 * b + blk
                            o = pM[:, n * P:(n + 1) * P]
                            last = pe.matmul(o, dl[:, n, :], AqT[:, n, :], start=True, stop=blk == 0)
                            if blk:
                                last = pe.matmul(o, dl[:, n - 1, :], Aq7[:, b, :], start=False, stop=True)
                        return last

                    def front(h):
                        pe.wait_ge(s_w, nth(s_w, h, 32))
                        for k, ps in enumerate((pX, pW, pX, pW)):
                            if k >= 2:
                                pe.wait_ge(s_fir, nth(s_fir, h, 3 * (k - 1)))
                            project(h, k, ps, 0)
                            project(h, k, ps, 1)
                        squares(h, 0, sqk)
                        squares(h, 1, sqq)
                        own_keys(h)

                    def out_rows(h, k):
                        for m in range(4):
                            n = 4 * k + m
                            last = pe.matmul((pM[:, 0:NT], pW)[k][:, m * D:(m + 1) * D], Z[:, n * P:(n + 1) * P],
                                             won[:, :], start=True, stop=True)
                        last.then_inc(s_ow, 1)

                    def body(h, following):
                        products(h, 0, 0)
                        products(h, 0, 1)
                        pe.wait_ge(s_silu, nth(s_silu, h, 4))
                        for n in range(NB):
                            last = pe.transpose(pX[:, n * P:(n + 1) * P], V[:, n * P:(n + 1) * P], ident)
                        last.then_inc(s_vt, 1)
                        products(h, 1, 0)
                        products(h, 1, 1)
                        mult_1(h, 0)
                        products(h, 2, 0)
                        products(h, 2, 1)
                        for lv in range(1, SMALL + 1):
                            mult_1(h, lv)
                            if lv == 4:
                                pe.wait_ge(s_R, nth(s_R, h, 1))
                            if lv == 5:
                                pe.wait_ge(s_acc, nth(s_acc, h, 2))
                            products(h, lv + 2, 0)
                            mult_2(h, lv)
                            products(h, lv + 2, 1)
                        pe.wait_ge(s_xc, nth(s_xc, h, 2))
                        n = h + 1
                        solve(h, 0)
                        if following:
                            pe.wait_ge(s_w, nth(s_w, n, 32))
                            pe.wait_ge(s_big, nth(s_big, h, 1))
                            project(n, 0, pX, 0)
                        explain(h, 0)
                        if following:
                            project(n, 0, pX, 1)
                        solve(h, 1)
                        if following:
                            pe.wait_ge(s_big, nth(s_big, h, 2))
                            project(n, 1, pW, 0)
                        explain(h, 1)
                        if following:
                            project(n, 1, pW, 1)
                        solve(h, 2)
                        explain(h, 2)
                        if following:
                            pe.wait_ge(s_fir, nth(s_fir, n, 3))
                            project(n, 2, pX, 0)
                        solve(h, 3)
                        if following:
                            project(n, 2, pX, 1)
                        pe.wait_ge(s_aq, nth(s_aq, h, 1))
                        pe.wait_ge(s_dl, nth(s_dl, h, 4))
                        outputs(h, 0)
                        outputs(h, 1).then_inc(s_o, 1)
                        if following:
                            pe.wait_ge(s_fir, nth(s_fir, n, 6))
                            project(n, 3, pW, 0)
                            project(n, 3, pW, 1)
                        pe.wait_ge(s_sqz, nth(s_sqz, h, 1))
                        for m in range(NB):
                            last = pe.matmul(pM3[:, m:m + 1], sqz[:, m * P:(m + 1) * P], ones[:, 0:1],
                                             start=True, stop=True)
                        last.then_inc(s_ssz, 1)
                        pe.wait_ge(s_z, nth(s_z, h, 1))
                        pe.wait_ge(s_won, nth(s_won, h, 1))
                        out_rows(h, 0)
                        if following:
                            pe.wait_ge(s_ms, nth(s_ms, h, 3))
                            squares(n, 0, sqk)
                            squares(n, 1, sqq)
                            own_keys(n)
                            pe.wait_ge(s_silu, nth(s_silu, n, 3))
                        out_rows(h, 1)

                    all_heads(pe, front, body)

        rt_steps = []

        NS = 4
        AHEAD = 2
        ROUNDS = E // NS
        with ExitStack() as ffn:
            def fb(name, shape, dt=F32):
                return sb(name, shape, dt, where=ffn)

            gated = fb("gated", [P, NB, D])
            sc_, sbs = fb("sc_", [P, NB, E]), fb("sbs", [P, NB, E])
            top2 = fb("top2", [P, NB, G, 8])
            gs = fb("gs", [P, NB, G])
            cmp_, cnt = fb("cmp_", [P, NB, G]), fb("cnt", [P, NB, G])
            keep = fb("keep", [P, NB, G], I32)
            cand = fb("cand", [P, NB, E])
            top8 = fb("top8", [P, NB, 8])
            taken = fb("taken", [P, NB, E])
            wsum, winv = fb("wsum", [P, NB]), fb("winv", [P, NB])
            cwT = fb("cwT", [E, NT])
            xl, yl = fb("xl", [P, NT]), fb("yl", [P, NT])
            rlu = fb("rlu", [P, SHC, NT])
            w1 = [fb(f"w1_{k}", [P, P]) for k in range(NS)]
            w2 = [fb(f"w2_{k}", [P, P]) for k in range(NS)]
            cwb = [fb(f"cwb{k}", [P, NT]) for k in range(NS)]
            rl = [fb(f"rl{k}", [P, NT]) for k in range(NS)]
            hw = [fb(f"hw{k}", [P, NT]) for k in range(NS)]
            zero = fb("zero", [P, P])
            PH = (pX, pW)
            pY = (pM1, pM2)
            PS = (pM[:, 2 * HALF:], pW)
            s_x1, s_ln2, s_lg, s_sig, s_rt, s_cwt, s_cwc, s_cwd, s_xl, s_xlc = (
                sem(n) for n in ("s_x1", "s_ln2", "s_lg", "s_sig", "s_rt", "s_cwt", "s_cwc", "s_cwd", "s_xl", "s_xlc"))
            s_win, s_cin, s_up, s_rl, s_cm, s_hw, s_dn = (
                [sem(f"{n}{k}") for k in range(NS)] for n in ("s_win", "s_cin", "s_up", "s_rl", "s_cm", "s_hw", "s_dn"))
            s_z0, s_yl, s_ylc, s_sh, s_shr, s_shs, s_fo, s_fin, s_out = (
                sem(n) for n in ("s_z0", "s_yl", "s_ylc", "s_sh", "s_shr", "s_shs", "s_fo", "s_fin", "s_out"))
            rt_steps = []

            def add_in(dve, k, branch, blocks, done, at):
                g = gates[:, k, blocks.start // 2:blocks.stop // 2, :].unsqueeze(2)
                nb = (blocks.stop - blocks.start) // 2
                dve.tensor_tensor(gated[:, blocks, :].rearrange("p (b u) f -> p b u f", u=2),
                                  branch.rearrange("p (b u) f -> p b u f", u=2), g.to_broadcast([P, nb, 2, D]),
                                  ALU.mult).then_inc(done, 1)
                dve.wait_ge(done, at)
                dve.tensor_tensor(x[:, blocks, :], x[:, blocks, :], gated[:, blocks, :], ALU.add).then_inc(done, 1)

            with nc.Block() as block:
                @block.sync
                def _(sp):
                    def expert_weights(e, k):
                        for t, n in ((w1[k], "w1"), (w2[k], "w2")):
                            sp.dma_start(t[:, :], d[n][bass.ds(e, 1)].rearrange("a p n -> (a p) n"))\
                              .then_inc(s_win[k], 16)

                    def token_weights(e, k):
                        sp.dma_start(cwb[k][:, :], route_dram[bass.ds(e, 1), :].to_broadcast([P, NT]))\
                          .then_inc(s_cin[k], 16)

                    for k in range(NS):
                        expert_weights(k, k)
                    sp.wait_ge(s_cwc, 1)
                    sp.dma_start(route_dram, cwT[:, :]).then_inc(s_cwd, 16)
                    sp.wait_ge(s_cwd, 16)
                    for k in range(NS):
                        token_weights(k, k)
                    with sp.Fori(0, ROUNDS - 1) as i:
                        for k in range(NS):
                            sp.wait_ge(s_dn[k], i + 1)
                            expert_weights(NS * i + NS + k, k)
                            token_weights(NS * i + NS + k, k)
                    for k in range(2):
                        sp.wait_ge(s_fin, 2 * k + 2)
                        sp.dma_start(out.rearrange("(n p) f -> p n f", p=P)[:, 4 * k:4 * k + 4, :],
                                     x[:, 4 * k:4 * k + 4, :]).then_inc(s_out, 16)
                    sp.wait_ge(s_out, 32)

                @block.gpsimd
                def _(pool):
                    pool.memset(zero[:, :], 0.0).then_inc(s_z0, 1)
                    pool.wait_ge(s_ln2, 3)
                    pool.tensor_tensor(rstd[:, :], veps[:, :], halfs[:, 0, :], ALU.pow).then_inc(s_rstd, 1)

                @block.scalar
                def _(act):
                    modulate(act, 1, 6)
                    act.wait_ge(s_lg, 1)
                    act.activation(sc_[:, :, :], pA[:, 0:NB * E].rearrange("p (n e) -> p n e", n=NB), ACT.Exp,
                                   scale=-1.0).then_inc(s_sig, 1)
                    act.wait_ge(s_xl, 1)
                    act.copy(xl[:, :], pX[:, :]).then_inc(s_xlc, 1)
                    for j in range(SHC):
                        act.wait_ge(s_sh, j + 1)
                        act.activation(rlu[:, j, :], PS[j % 2], ACT.Relu).then_inc(s_shr, 1)
                        act.wait_ge(s_shr, j + 1)
                        act.activation(rlu[:, j, :], rlu[:, j, :], ACT.Square).then_inc(s_shs, 1)

                    def relu(i, k):
                        act.wait_ge(s_up[k], i + 1)
                        act.activation(rl[k][:, :], PH[k % 2][:, :], ACT.Relu).then_inc(s_rl[k], 1)

                    for k in range(NS):
                        relu(0, k)
                    with act.Fori(1, ROUNDS) as i:
                        for k in range(NS):
                            act.wait_ge(s_hw[k], i)
                            relu(i, k)
                    act.wait_ge(s_yl, 1)
                    act.copy(yl[:, 0:HALF], pM1[:, :])
                    act.copy(yl[:, HALF:], pM2[:, :]).then_inc(s_ylc, 1)

                @block.vector
                def _(dve):
                    add_in(dve, 0, attn[:, :, :], slice(0, NB), s_x1, 1)
                    dve.wait_ge(s_x1, 2)
                    for n in range(NB):
                        last = dve.bn_stats(stats[:, n, :], x[:, n, :])
                    last.then_inc(s_ln2, 1)
                    dve.wait_ge(s_ln2, 1)
                    for n in range(NB):
                        last = dve.bn_aggr(mv[:, n, :], stats[:, n, :])
                    last.then_inc(s_ln2, 1)
                    dve.wait_ge(s_ln2, 2)
                    dve.tensor_scalar(veps[:, :], mv[:, :, 1], LN_EPS, None, ALU.add).then_inc(s_ln2, 1)
                    dve.wait_ge(s_rstd, 2)
                    for n in range(NB):
                        dve.tensor_scalar(xn[:, n, :], x[:, n, :], mv[:, n, 0:1], rstd[:, n:n + 1],
                                          ALU.subtract, ALU.mult).then_inc(s_xn, 1)
                    steps = 0

                    def step(ins):
                        nonlocal steps
                        steps += 1
                        ins.then_inc(s_rt, 1)
                        dve.wait_ge(s_rt, steps)

                    dve.wait_ge(s_fw, 6 * 16)
                    dve.wait_ge(s_sig, 1)
                    step(dve.tensor_scalar(sc_[:, :, :], sc_[:, :, :], 1.0, None, ALU.add))
                    step(dve.reciprocal(sc_[:, :, :], sc_[:, :, :]))
                    step(dve.tensor_tensor(sbs[:, :, :], sc_[:, :, :],
                                           gbias.unsqueeze(1).to_broadcast([P, NB, E]), ALU.add))
                    for n in range(NB):
                        for g in range(G):
                            last = dve.max(top2[:, n, g, :], sbs[:, n, g * EG:(g + 1) * EG])
                    step(last)
                    step(dve.tensor_tensor(gs[:, :, :], top2[:, :, :, 0], top2[:, :, :, 1], ALU.add))
                    step(dve.memset(cnt[:, :, :], 0.0))
                    for g in range(G):
                        one = gs[:, :, g:g + 1]
                        if g > 0:
                            dve.tensor_tensor(cmp_[:, :, 0:g], one.to_broadcast([P, NB, g]), gs[:, :, 0:g], ALU.is_gt)
                        if g < G - 1:
                            dve.tensor_tensor(cmp_[:, :, g + 1:], one.to_broadcast([P, NB, G - 1 - g]),
                                              gs[:, :, g + 1:], ALU.is_ge)
                        step(dve.memset(cmp_[:, :, g:g + 1], 0.0))
                        step(dve.tensor_tensor(cnt[:, :, :], cnt[:, :, :], cmp_[:, :, :], ALU.add))
                    dve.memset(cand[:, :, :], FILL)
                    step(dve.tensor_scalar(keep[:, :, :], cnt[:, :, :], float(TOPG), None, ALU.is_lt))
                    step(dve.copy_predicated(cand.rearrange("p n (g e) -> p n g e", g=G),
                                             keep.unsqueeze(3).to_broadcast([P, NB, G, EG]),
                                             sbs.rearrange("p n (g e) -> p n g e", g=G)))
                    for n in range(NB):
                        last = dve.max(top8[:, n, :], cand[:, n, :])
                    step(last)
                    for n in range(NB):
                        last = dve.match_replace(taken[:, n, :], top8[:, n, :], cand[:, n, :], TAKEN)
                    step(last)
                    step(dve.scalar_tensor_tensor(cand[:, :, :], taken[:, :, :], TAKEN, sc_[:, :, :],
                                                  ALU.is_ge, ALU.mult))
                    step(dve.tensor_reduce(wsum[:, :], cand[:, :, :], AX.X, ALU.add))
                    step(dve.reciprocal(winv[:, :], wsum[:, :]))
                    step(dve.tensor_scalar(winv[:, :], winv[:, :], ROUTED_SCALE, None, ALU.mult))
                    dve.tensor_tensor(cand[:, :, :], cand[:, :, :], winv.unsqueeze(2).to_broadcast([P, NB, E]),
                                      ALU.mult).then_inc(s_rt, 1)
                    dve.wait_ge(s_cwt, 1)
                    dve.tensor_copy(cwT[:, :], pX[0:E, :]).then_inc(s_cwc, 1)
                    rt_steps.append(steps + 1)

                    def weigh(i, k):
                        dve.wait_ge(s_cin[k], 16 * i + 16)
                        dve.wait_ge(s_rl[k], i + 1)
                        dve.tensor_tensor(hw[k][:, :], rl[k][:, :], cwb[k][:, :], ALU.mult).then_inc(s_cm[k], 1)
                        dve.wait_ge(s_cm[k], i + 1)
                        dve.tensor_tensor(hw[k][:, :], hw[k][:, :], rl[k][:, :], ALU.mult).then_inc(s_hw[k], 1)

                    for k in range(NS):
                        weigh(0, k)
                    with dve.Fori(1, ROUNDS) as i:
                        for k in range(NS):
                            dve.wait_ge(s_dn[k], i)
                            weigh(i, k)
                    for k, ps in enumerate((pX, pW)):
                        dve.wait_ge(s_fo, k + 1)
                        add_in(dve, 1, ps.rearrange("p (n f) -> p n f", n=4), slice(4 * k, 4 * k + 4), s_fin,
                               2 * k + 1)

                @block.tensor
                def _(pe):
                    pe.wait_ge(s_x1, 2)
                    turn_in(pe, 1)
                    pe.wait_ge(s_fw, 6 * 16)
                    pe.wait_ge(s_hT, 2 * B)
                    for n in range(NB):
                        for c in range(DC):
                            last = pe.matmul(pA[:, n * E:(n + 1) * E], hT[:, c, n * P:(n + 1) * P], gw[:, c, :],
                                             start=c == 0, stop=c == DC - 1)
                    last.then_inc(s_lg, 1)
                    for hf in range(2):
                        for c in range(DC):
                            last = pe.matmul(pX[:, hf * HALF:(hf + 1) * HALF], fc1[:, c, :],
                                             hT[:, c, hf * HALF:(hf + 1) * HALF], start=c == 0, stop=c == DC - 1)
                    last.then_inc(s_xl, 1)
                    pe.wait_ge(s_sig, 1)
                    for j in range(SHC):
                        if j >= 2:
                            pe.wait_ge(s_shr, j - 1)
                        for hf in range(2):
                            for c in range(DC):
                                last = pe.matmul(PS[j % 2][:, hf * HALF:(hf + 1) * HALF], up[:, c, j * P:(j + 1) * P],
                                                 hT[:, c, hf * HALF:(hf + 1) * HALF], start=c == 0, stop=c == DC - 1)
                        last.then_inc(s_sh, 1)
                    pe.wait_ge(s_z0, 1)
                    pe.wait_ge(s_xlc, 1)
                    for hf in range(2):
                        pe.matmul(pY[hf][:, :], zero[:, :], xl[:, hf * HALF:(hf + 1) * HALF], start=True, stop=False,
                                  skip_group_check=True)
                    pe.wait_ge(s_rt, rt_steps[0])
                    for n in range(NB):
                        last = pe.transpose(pX[0:E, n * P:(n + 1) * P], cand[:, n, :], ident)
                    last.then_inc(s_cwt, 1)

                    def ups(i, k):
                        pe.wait_ge(s_win[k], 32 * i + 32)
                        for hf in range(2):
                            last = pe.matmul(PH[k % 2][:, hf * HALF:(hf + 1) * HALF], w1[k][:, :],
                                             xl[:, hf * HALF:(hf + 1) * HALF], start=True, stop=True)
                        last.then_inc(s_up[k], 1)

                    def downs(i, k):
                        pe.wait_ge(s_hw[k], i + 1)
                        for hf in range(2):
                            last = pe.matmul(pY[hf][:, :], w2[k][:, :], hw[k][:, hf * HALF:(hf + 1) * HALF],
                                             start=False, stop=False, skip_group_check=True)
                        last.then_inc(s_dn[k], 1)

                    pe.wait_ge(s_cwc, 1)
                    ups(0, 0)
                    pe.wait_ge(s_shr, SHC)
                    ups(0, 1)
                    with pe.Fori(0, ROUNDS - 1) as i:
                        for k in range(NS):
                            pe.wait_ge(s_rl[k], i + 1)
                            m = (k + AHEAD) % NS
                            ups(i + (k + AHEAD) // NS, m)
                            downs(i, k)
                    for k in range(NS):
                        if k < NS - AHEAD:
                            pe.wait_ge(s_rl[k], ROUNDS)
                            ups(ROUNDS - 1, k + AHEAD)
                        downs(ROUNDS - 1, k)
                    for hf in range(2):
                        last = pe.matmul(pY[hf][:, :], zero[:, :], xl[:, hf * HALF:(hf + 1) * HALF],
                                         start=False, stop=True, skip_group_check=True)
                    last.then_inc(s_yl, 1)
                    pe.wait_ge(s_shs, SHC)
                    pe.wait_ge(s_rl[3], ROUNDS)
                    for k in range(2):
                        for m in range(4):
                            r = slice((4 * k + m) * P, (4 * k + m + 1) * P)
                            for j in range(SHC):
                                pe.matmul(PH[k][:, m * D:(m + 1) * D], rlu[:, j, r], down[:, j, :],
                                          start=j == 0, stop=False)
                            if k == 0 and m == 0:
                                pe.wait_ge(s_ylc, 1)
                            last = pe.matmul(PH[k][:, m * D:(m + 1) * D], yl[:, r], fc2[:, :], start=False, stop=True)
                        last.then_inc(s_fo, 1)


def kernel(**inputs):
    import numpy as _np
    import concourse.bacc as _bacc
    from concourse import mybir as _mybir
    from concourse.bass_utils import run_bass_kernel_spmd as _run

    a = {k: _np.asarray(v) for k, v in inputs.items()}
    at, ff = "L0_attn_", "L0_ffn_"

    def by_head(w):
        return w.reshape(DC, P, H, DK).transpose(2, 1, 0, 3)

    cw = _np.zeros((H, P, 16), _np.float32)
    for k, n in enumerate(("conv_k", "conv_q", "conv_v")):
        cw[:, :, 4 * k:4 * k + 4] = a[at + n].reshape(H, P, KW)
    cw[:, :, 12] = a[at + "bg"].reshape(H, P)
    floats, masks = shape_constants()
    arrays = {
        "x": a[at + "hidden_states"].reshape(NT, D),
        "cT": a["L0_c"].T,
        "wmod": a["L0_wmod"],
        "Wh": _np.stack([by_head(a[at + n]) for n in ("Wk", "Wq", "Wv", "Wg")], axis=2),
        "cw": cw,
        "Wf1": a[at + "Wf1"], "Wf2": a[at + "Wf2"], "Wb": a[at + "Wb"],
        "dt": a[at + "dt_bias"].reshape(P, 1),
        "A_log": _np.repeat(a[at + "A_log"], NG).reshape(P, 1),
        "norm_w": a[at + "norm_w"].reshape(P, 1),
        "Wo": a[at + "Wo"].reshape(H, DK, D),
        "gate_w": a[ff + "gate_w"].T, "gate_bias": a[ff + "gate_bias"].reshape(1, E),
        "fc1": a[ff + "fc1_w"].T, "fc2": a[ff + "fc2_w"].T,
        "w1": a[ff + "w1"].transpose(0, 2, 1), "w2": a[ff + "w2"].transpose(0, 2, 1),
        "up": a[ff + "shared_up_w"].T, "down": a[ff + "shared_down_w"].T,
        "floats": floats, "masks": masks,
    }
    arrays = {k: _np.ascontiguousarray(v) for k, v in arrays.items()}
    nc = _bacc.Bacc("TRN2", target_bir_lowering=False, num_devices=1)
    args = {k: nc.dram_tensor(k + "_dram", v.shape, _mybir.dt.from_np(v.dtype), kind="ExternalInput").ap()
            for k, v in arrays.items()}
    out = nc.dram_tensor("out_dram", (NT, D), F32, kind="ExternalOutput").ap()
    build(nc, args, out)
    r = _run(nc, [{k + "_dram": v for k, v in arrays.items()}], core_ids=[0])
    return r.results[0]["out_dram"].reshape(B, T, D)
```

```python
from contextlib import ExitStack

import numpy as np
import concourse.bass as bass
from concourse import mybir

ALU = mybir.AluOpType
ACT = mybir.ActivationFunctionType
F32 = mybir.dt.float32
I32 = mybir.dt.int32
AX = mybir.AxisListType

P = 128
B, T, D = 4, 256, 256
NT = B * T
NB = NT // P
DC = D // P
HALF = 512
H, DK = 16, 128
NG = 8
GC = DK // NG
LEVELS = 8
SMALL = 5
KW = 4
E, G, EG, TOPG, TOPK = 32, 4, 8, 2, 8
SHC = 4
ROUTED_SCALE = 2.5
QSCALE = DK ** -0.5
LN_EPS, L2_EPS, RMS_EPS = 1e-5, 1e-6, 1e-5
FILL = -3.0e38
TAKEN = 3.0e38


def shape_constants():
    ident = np.eye(P, dtype=np.float32)
    ident32 = np.tile(np.eye(32, dtype=np.float32), (4, 1))
    floats = np.concatenate([ident, ident32], axis=1)
    masks = np.zeros((P, SMALL * 64 + 32), np.int32)
    for lv in range(SMALL):
        s = 1 << lv
        for c in range(64):
            i = (c // s) * 2 * s + s + c % s
            for j in range(P):
                masks[j, lv * 64 + c] = int(j // (2 * s) == i // (2 * s) and j % (2 * s) < s)
    masks[:, SMALL * 64:] = ident32.astype(np.int32)
    return floats, masks


def build(nc, d, out):
    ctx = ExitStack()
    with ctx:
        def sb(name, shape, dt=F32, where=ctx):
            return where.enter_context(nc.sbuf_tensor(name, shape, dt))[(slice(None),) * len(shape)]

        def pb(name, cols):
            return ctx.enter_context(nc.psum_tensor(name, [P, cols], F32))[:, :]

        def sem(name):
            return ctx.enter_context(nc.semaphore(name))

        pX, pW = pb("pX", 2 * HALF), pb("pW", 2 * HALF)
        pM = pb("pM", 4 * HALF)
        pM1, pM2, pM3, pA = (pM[:, k * HALF:(k + 1) * HALF] for k in range(4))
        pV = pM[:, 2 * HALF:]

        decay_dram = nc.dram_tensor("decay_dram", [P, LEVELS, NT], F32, kind="Internal").ap()
        route_dram = nc.dram_tensor("route_dram", [E, NT], F32, kind="Internal").ap()

        x = sb("x", [P, NB, D])
        hT = sb("hT", [P, DC, NT])
        modT = sb("modT", [P, 12, B])
        consts = sb("consts", [P, P + 32])
        masks = sb("masks", [P, SMALL * 64 + 32], I32)
        ident, ident32 = consts[:, 0:P], consts[:, P:P + 32]
        ones = sb("ones", [P, P])
        beta = sb("beta", [P, NB, H])
        attn = sb("attn", [P, NB, D])
        gates = sb("gates", [P, 2, B, D])
        nw = sb("nw", [P, 1])
        stats = sb("stats", [P, NB, 6])
        mv = sb("mv", [P, NB, 2])
        veps = sb("veps", [P, NB])
        rstd = sb("rstd", [P, NB])
        halfs = sb("halfs", [P, 2, NB])
        xn = sb("xn", [P, NB, D])
        gw = sb("gw", [P, DC, E])
        gbias = sb("gbias", [P, E])
        fc1 = sb("fc1", [P, DC, P])
        fc2 = sb("fc2", [P, D])
        up = sb("up", [P, DC, SHC * P])
        down = sb("down", [P, SHC, D])
        s_ffn_in = sem("s_ffn_in")

        s_x, s_mod_in, s_const, s_small_in = (sem(n) for n in ("s_x", "s_mod_in", "s_const", "s_small_in"))
        s_set, s_siluc, s_modps, s_mod = (sem(n) for n in ("s_set", "s_siluc", "s_modps", "s_mod"))
        s_ln, s_rstd, s_xn, s_xT, s_hT0, s_hT1 = (sem(n) for n in ("s_ln", "s_rstd", "s_xn", "s_xT", "s_hT0", "s_hT1"))
        s_logits, s_f1c, s_exp1, s_sp, s_a = (sem(n) for n in ("s_logits", "s_f1c", "s_exp1", "s_sp", "s_a"))
        s_lev, s_gd, s_gps, s_gates = (sem(n) for n in ("s_lev", "s_gd", "s_gps", "s_gates"))
        s_stored = [sem(f"s_stored{lv}") for lv in range(LEVELS)]

        def layer_norm(dve, done, base):
            for n in range(NB):
                last = dve.bn_stats(stats[:, n, :], x[:, n, :])
            last.then_inc(done, 1)
            dve.wait_ge(done, base + 1)
            for n in range(NB):
                last = dve.bn_aggr(mv[:, n, :], stats[:, n, :])
            last.then_inc(done, 1)
            dve.wait_ge(done, base + 2)
            dve.tensor_scalar(veps[:, :], mv[:, :, 1], LN_EPS, None, ALU.add).then_inc(done, 1)
            dve.wait_ge(s_rstd, (base // 3) + 1)
            for n in range(NB):
                dve.tensor_scalar(xn[:, n, :], x[:, n, :], mv[:, n, 0:1], rstd[:, n:n + 1],
                                  ALU.subtract, ALU.mult).then_inc(s_xn, 1)

        def turn_in(pe, base):
            for n in range(NB):
                pe.wait_ge(s_xn, base * NB + n + 1)
                for c, ps in enumerate((pX, pW)):
                    last = pe.transpose(ps[:, n * P:(n + 1) * P], xn[:, n, c * P:(c + 1) * P], ident)
                last.then_inc(s_xT, 1)

        def modulate_0(act, base, row):
            for b in range(B):
                act.wait_ge(s_xT, base * NB + 4 * (b // 2) + 4)
                act.activation(hT[:, 0, b * T:(b + 1) * T], pX[:, b * T:(b + 1) * T], ACT.Identity,
                               bias=modT[:, row, b:b + 1], scale=modT[:, row + 2, b:b + 1]).then_inc(s_hT0, 1)

        def modulate_1(dve, base, row):
            for b in range(B):
                dve.wait_ge(s_xT, base * NB + 4 * (b // 2) + 4)
                dve.tensor_scalar(hT[:, 1, b * T:(b + 1) * T], pW[:, b * T:(b + 1) * T], modT[:, row + 3, b:b + 1],
                                  modT[:, row + 1, b:b + 1], ALU.mult, ALU.add).then_inc(s_hT1, 1)

        def modulated(pe, base, batches):
            pe.wait_ge(s_hT0, base * B + batches)
            pe.wait_ge(s_hT1, base * B + batches)

        PER = {}

        def hsem(name, per):
            s = sem(name)
            PER[id(s)] = per
            return s

        def nth(s, h, k):
            return h * PER[id(s)] + k

        with ExitStack() as heads:
            def hb(name, shape, dt=F32):
                return sb(name, shape, dt, where=heads)

            wh = hb("wh", [P, 4, DC, P])
            cw = hb("cw", [P, 16])
            dec = hb("dec", [P, LEVELS, NT])
            wo, won = hb("wo", [P, D]), hb("won", [P, D])
            K, Q, V = hb("K", [P, NT]), hb("Q", [P, NT]), hb("V", [P, NT])
            SG = hb("SG", [P, NT])
            sqk, sqq = hb("sqk", [P, NT]), hb("sqq", [P, NT])
            Z, sqz = hb("Z", [P, NT]), hb("sqz", [P, NT])
            KQ = hb("KQ", [P, 2, 2, NT])
            A = hb("A", [P, SMALL, NB, P])
            AqT = hb("AqT", [P, NB, P])
            A5 = hb("A5", [P, NB, 32])
            A6 = hb("A6", [64, NB, 64])
            A7, Aq7 = hb("A7", [P, B, P]), hb("Aq7", [P, B, P])
            X, XT = hb("X", [P, NB, 32]), hb("XT", [P, NB, 32])
            XC = hb("XC", [P, NB, 64])
            M1 = hb("M1", [P, NB, 32])
            R = hb("R", [P, NB, P])
            dl = hb("dl", [P, NB, P])
            sse = hb("sse", [P, 2 * NB])
            kn, rqs = hb("kn", [P, NB]), hb("rqs", [P, NB])
            bh, cc = hb("bh", [P, NB]), hb("cc", [P, NB])
            t2, ms, rms, fr = hb("t2", [P, NB]), hb("ms", [P, NB]), hb("rms", [P, NB]), hb("fr", [P, NB])

            s_weights_in, s_wo_in, s_won = hsem("s_weights_in", 32), hsem("s_wo_in", 16), hsem("s_won", 1)
            s_decays_in = [hsem(f"s_decays_in{lv}", 16) for lv in range(LEVELS)]
            s_projected = hsem("s_projected", 4)
            s_summed, s_v_turned = hsem("s_summed", 2), hsem("s_v_turned", 1)
            s_pairs = hsem("s_pairs", 9)
            s_AX, s_XAX = hsem("s_AX", 6), hsem("s_XAX", 5)
            s_chain = hsem("s_chain", 7)
            s_outputs, s_z_summed, s_out_rows = hsem("s_outputs", 1), hsem("s_z_summed", 1), hsem("s_out_rows", 2)
            s_added = hsem("s_added", 2)
            s_tapped, s_silu, s_squared = hsem("s_tapped", 3), hsem("s_silu", 4), hsem("s_squared", 2)
            s_AX_kept, s_XC_part, s_wide, s_rows, s_z_squared = hsem("s_AX_kept", 5), hsem("s_XC_part", 2), hsem("s_wide", 3), hsem("s_rows", 4), hsem("s_z_squared", 1)
            s_fir, s_scaled, s_picked = hsem("s_fir", 9), hsem("s_scaled", 8), hsem("s_picked", 6)
            s_sse, s_c, s_R = hsem("s_sse", 1), hsem("s_c", 3), hsem("s_R", 4)
            s_X_grown, s_XT_turned, s_x0 = hsem("s_X_grown", 6), hsem("s_XT_turned", 5), hsem("s_x0", 1)
            s_gated, s_ms = hsem("s_gated", 1), hsem("s_ms", 5)
            s_root, s_rms, s_qscaled = hsem("s_root", 2), hsem("s_rms", 1), hsem("s_qscaled", 8)
            s_zero = sem("s_zero")
            s_passed, s_passed_dve, s_passed_pool, s_passed_sp = (
                sem(n) for n in ("s_passed", "s_passed_dve", "s_passed_pool", "s_passed_sp"))

            def bc(t, rows, n):
                return t.unsqueeze(2).to_broadcast([rows, t.shape[1], n])

            def later(t, s):
                return t.rearrange("p (m u s) -> p m u s", u=2, s=s)[:, :, 1, :]

            def seqs(t, blk, rows=slice(0, P)):
                return t.rearrange("p (b u) n -> p b u n", u=2)[rows, :, blk, :]

            def all_heads(eng, front, body):
                front(0)
                with eng.Fori(0, H - 1) as h:
                    body(h, True)
                body(H - 1, False)

            LO, UP = slice(0, 64), slice(64, P)

            cT = sb("cT", [P, DC, B], where=heads)
            siluc = sb("siluc", [P, DC, B], where=heads)
            wmod = dec.rearrange("p l t -> p (l t)")[:, 0:DC * 12 * P].rearrange("p (c n) -> p c n", c=DC)
            gsign = sb("gsign", [P, 4, B], where=heads)
            gmag = sb("gmag", [P, 4, B], where=heads)
            wf1 = sb("wf1", [P, DC, P], where=heads)
            wf2 = sb("wf2", [P, P], where=heads)
            wb = sb("wb", [P, DC, H], where=heads)
            dtb = sb("dtb", [P, 1], where=heads)
            alog = sb("alog", [P, 1], where=heads)
            nega = sb("nega", [P, 1], where=heads)
            f1, gx = Z, sqz
            u, v1, v2 = KQ[:, 0, 0, :], KQ[:, 0, 1, :], KQ[:, 1, 0, :]
            lev = dec
            pre, suf = (t.rearrange("p n j -> p (n j)") for t in (R, dl))
            gdiag = [t.rearrange("p (c b n) -> p c b n", c=DC, b=B) for t in (sqk, sqq)]
            s_modc, s_gx, s_own = sem("s_modc"), sem("s_gx"), sem("s_own")

            with nc.Block() as block:
                @block.sync
                def _(sp):
                    sp.dma_start(cT[:, :, :], d["cT"].rearrange("(c p) b -> p c b", p=P)).then_inc(s_mod_in, 16)
                    sp.dma_start(wmod[:, :, :], d["wmod"].rearrange("(c p) n -> p c n", p=P)).then_inc(s_mod_in, 16)
                    sp.dma_start(x[:, :, :], d["x"].rearrange("(n p) f -> p n f", p=P)).then_inc(s_x, 16)
                    sp.dma_start(consts[:, :], d["floats"]).then_inc(s_const, 16)
                    sp.dma_start(masks[:, :], d["masks"]).then_inc(s_const, 16)
                    for t, n in ((wf1[:, :, :], "Wf1"), (wb[:, :, :], "Wb")):
                        sp.dma_start(t, d[n].rearrange("(c p) n -> p c n", p=P)).then_inc(s_small_in, 16)
                    sp.dma_start(wf2[:, :], d["Wf2"]).then_inc(s_small_in, 16)
                    sp.dma_start(dtb[:, :], d["dt"]).then_inc(s_small_in, 16)
                    sp.dma_start(alog[:, :], d["A_log"]).then_inc(s_small_in, 16)
                    sp.dma_start(nw[:, :], d["norm_w"]).then_inc(s_small_in, 16)
                    def weights(h):
                        sp.dma_start(wh[:, :, :, :], d["Wh"][bass.ds(h, 1)].rearrange("a p w c n -> (a p) w c n"))\
                          .then_inc(s_weights_in, 16)

                    def taps(h):
                        sp.dma_start(cw[:, :], d["cw"][bass.ds(h, 1)].rearrange("a p n -> (a p) n")).then_inc(s_weights_in, 16)

                    def decays(h, lv):
                        rows = decay_dram[bass.ds(h * NG, NG), lv, :].unsqueeze(1).to_broadcast([NG, GC, NT])
                        sp.dma_start(dec[:, lv, :], rows).then_inc(s_decays_in[lv], 16)

                    def out_weights(h):
                        sp.dma_start(wo[:, :], d["Wo"][bass.ds(h, 1)].rearrange("a p n -> (a p) n")).then_inc(s_wo_in, 16)

                    weights(0)
                    taps(0)
                    out_weights(0)
                    for lv in range(LEVELS + 1):
                        if lv < LEVELS:
                            sp.wait_ge(s_lev, lv + 1)
                            sp.dma_start(decay_dram[:, lv, :], lev[:, lv, :]).then_inc(s_stored[lv], 16)
                        if lv:
                            sp.wait_ge(s_stored[lv - 1], 16)
                            decays(0, lv - 1)
                    with sp.Fori(0, H - 1) as h:
                        sp.wait_ge(s_projected, nth(s_projected, h, 4))
                        weights(h + 1)
                        sp.wait_ge(s_silu, nth(s_silu, h, 4))
                        sp.sem_inc(s_passed_sp, 1)
                        sp.wait_ge(s_fir, nth(s_fir, h, 9))
                        taps(h + 1)
                        for lv in range(LEVELS):
                            sp.wait_ge(s_scaled, nth(s_scaled, h, lv + 1))
                            sp.wait_ge(s_qscaled, nth(s_qscaled, h, lv + 1))
                            decays(h + 1, lv)
                        sp.wait_ge(s_won, nth(s_won, h, 1))
                        out_weights(h + 1)
                    for t, n in ((gw[:, :, :], "gate_w"), (fc1[:, :, :], "fc1"), (up[:, :, :], "up"),
                                 (down[:, :, :], "down")):
                        sp.dma_start(t, d[n].rearrange("(c p) n -> p c n", p=P)).then_inc(s_ffn_in, 16)
                    sp.dma_start(gbias[:, :], d["gate_bias"].to_broadcast([P, E])).then_inc(s_ffn_in, 16)
                    sp.dma_start(fc2[:, :], d["fc2"]).then_inc(s_ffn_in, 16)

                @block.gpsimd
                def _(pool):
                    pool.memset(halfs[:, 0, :], -0.5)
                    pool.memset(halfs[:, 1, :], 0.5)
                    pool.memset(attn[:, :, :], 0.0)
                    pool.memset(ones[:, :], 1.0).then_inc(s_set, 1)
                    pool.wait_ge(s_set, 1)
                    pool.wait_ge(s_ln, 3)
                    pool.tensor_tensor(rstd[:, :], veps[:, :], halfs[:, 0, :], ALU.pow).then_inc(s_rstd, 1)
                    for t in (A, AqT, XC):
                        last = pool.memset(t, 0.0)
                    last.then_inc(s_zero, 1)
                    pool.wait_ge(s_zero, 1)
                    pool.sem_inc(s_added, 2)

                    def norms(h):
                        pool.wait_ge(s_sse, nth(s_sse, h, 1))
                        pool.tensor_tensor(kn[:, :], sse[:, 0:NB], halfs[:, 1, :], ALU.pow).then_inc(s_root, 1)
                        pool.tensor_tensor(rqs[:, :], sse[:, NB:2 * NB], halfs[:, 0, :], ALU.pow).then_inc(s_root, 1)

                    def scale(h, lv):
                        if lv < 2:
                            pool.wait_ge(s_silu, nth(s_silu, h, 2))
                        else:
                            pool.wait_ge(s_pairs, nth(s_pairs, h, lv))
                        pool.wait_ge(s_decays_in[lv], nth(s_decays_in[lv], h, 16))
                        s = 1 << lv
                        pool.tensor_tensor(later(KQ[:, lv % 2, 1, :], s), later(dec[:, lv, :], s), later(Q[:, :], s),
                                           ALU.mult).then_inc(s_qscaled, 1)

                    def front(h):
                        scale(h, 0)
                        scale(h, 1)

                    def body(h, following):
                        norms(h)
                        for lv in range(2, LEVELS):
                            scale(h, lv)
                        if following:
                            scale(h + 1, 0)
                        pool.wait_ge(s_ms, nth(s_ms, h, 4))
                        pool.tensor_tensor(rms[:, :], ms[:, :], halfs[:, 0, :], ALU.pow).then_inc(s_rms, 1)
                        if following:
                            scale(h + 1, 1)

                    all_heads(pool, front, body)

                @block.scalar
                def _(act):
                    act.wait_ge(s_mod_in, 32)
                    act.activation(siluc[:, :, :], cT[:, :, :], ACT.Silu).then_inc(s_siluc, 1)
                    act.wait_ge(s_mod, 1)
                    modulate_0(act, 0, 0)
                    act.wait_ge(s_small_in, 6 * 16)
                    act.activation(nega[:, :], alog[:, :], ACT.Exp).then_inc(s_exp1, 1)
                    act.wait_ge(s_gx, 1)
                    act.activation(u[:, :], gx[:, :], ACT.Abs).then_inc(s_exp1, 1)
                    act.wait_ge(s_exp1, 2)
                    act.activation(u[:, :], u[:, :], ACT.Exp, scale=-1.0).then_inc(s_exp1, 1)
                    act.wait_ge(s_logits, 3)
                    act.activation(beta[:, :, :], pA[:, 64:64 + NB * H].rearrange("p (n h) -> p n h", n=NB),
                                   ACT.Exp, scale=-1.0).then_inc(s_exp1, 1)
                    act.wait_ge(s_gps, 1)
                    for k in range(2):
                        for c in range(DC):
                            r = 2 * k + c
                            last = act.copy(gates[:, k, :, c * P:(c + 1) * P],
                                            pM[:, r * HALF:(r + 1) * HALF].rearrange("p (b n) -> p b n", b=B))
                    last.then_inc(s_gates, 1)
                    act.wait_ge(s_sp, 1)
                    act.activation(pre, v1[:, :], ACT.Exp, scale=nega[:, 0:1]).then_inc(s_a, 1)
                    def tap(h, k, acc, ps):
                        if k == 0:
                            act.wait_ge(s_weights_in, nth(s_weights_in, h, 32))
                        act.wait_ge(s_projected, nth(s_projected, h, k + 1))
                        act.mul(acc, ps, cw[:, 4 * k + 3:4 * k + 4]).then_inc(s_tapped, 1)

                    def silu(h, k, acc):
                        act.wait_ge(s_fir, nth(s_fir, h, 3 * k + 3))
                        act.activation(acc, acc, ACT.Silu).then_inc(s_silu, 1)

                    def square(h, k, t, to):
                        act.wait_ge(s_silu, nth(s_silu, h, k + 1))
                        act.activation(to, t, ACT.Square).then_inc(s_squared, 1)

                    def gate(h):
                        act.wait_ge(s_projected, nth(s_projected, h, 4))
                        act.activation(SG[:, :], pV, ACT.Silu, bias=cw[:, 12:13]).then_inc(s_silu, 1)

                    def front(h):
                        tap(h, 0, K[:, :], pX[:, :])
                        tap(h, 1, Q[:, :], pW[:, :])
                        silu(h, 0, K[:, :])
                        tap(h, 2, V[:, :], pX[:, :])
                        silu(h, 1, Q[:, :])
                        square(h, 0, K[:, :], sqk[:, :])
                        square(h, 1, Q[:, :], sqq[:, :])
                        gate(h)
                        silu(h, 2, V[:, :])

                    def rows(h, k):
                        app, blk, r, ps = ((1, 0, LO, pM1), (3, 0, UP, pM3), (5, 1, LO, pM1), (7, 1, UP, pM3))[k]
                        act.wait_ge(s_chain, nth(s_chain, h, app))
                        act.copy(seqs(dl, blk, r), ps[r, :].rearrange("p (b n) -> p b n", b=B)).then_inc(s_rows, 1)

                    def body(h, following):
                        act.wait_ge(s_v_turned, nth(s_v_turned, h, 1))
                        act.wait_ge(s_root, nth(s_root, h, 2))
                        for n in range(NB):
                            last = act.mul(R[:, n, :], pV[:, n * P:(n + 1) * P], kn[:, n:n + 1])
                        last.then_inc(s_R, 1)
                        pm = pM1[:, 0:NB * 32].rearrange("p (n j) -> p n j", n=NB)
                        for lv in range(1, SMALL):
                            act.wait_ge(s_AX, nth(s_AX, h, lv + 1))
                            act.copy(M1[:, :, :], pm).then_inc(s_AX_kept, 1)
                        act.wait_ge(s_pairs, nth(s_pairs, h, 7))
                        pa = pW.rearrange("p (n k q i) -> p n k q i", n=NB, k=2, q=2)
                        for q in range(2):
                            r = slice(64 * q, 64 * q + 32)
                            act.copy(A5[r, :, :], pa[r, :, 0, q, :])
                            last = act.copy(AqT[r, :, 64 * q + 32:64 * q + 64], pa[r, :, 1, q, :])
                        last.then_inc(s_wide, 1)
                        act.wait_ge(s_AX, nth(s_AX, h, 6))
                        for p0 in (32, 96):
                            last = act.copy(M1[p0:p0 + 32, :, :], pm[p0:p0 + 32])
                        last.then_inc(s_AX_kept, 1)
                        act.wait_ge(s_XT_turned, nth(s_XT_turned, h, 5))
                        for q in range(4):
                            r = slice(32 * q, 32 * q + 32)
                            c0 = 32 * (q % 2)
                            last = act.copy(XC[r, :, c0:c0 + 32], XT[r, :, :])
                        last.then_inc(s_XC_part, 1)
                        act.wait_ge(s_XAX, nth(s_XAX, h, 5))
                        for p0 in (0, 64):
                            r = slice(p0, p0 + 32)
                            last = act.mul(XC[r, :, 32:64], pM3[r, 0:NB * 32].rearrange("p (n j) -> p n j", n=NB), -1.0)
                        last.then_inc(s_XC_part, 1)
                        act.wait_ge(s_pairs, nth(s_pairs, h, 8))
                        px64 = pX[0:64, :].rearrange("p (n k i) -> p n k i", n=NB, k=2)
                        act.copy(A6[:, :, :], px64[:, :, 0, :])
                        act.copy(AqT[0:64, :, 64:128], px64[:, :, 1, :]).then_inc(s_wide, 1)
                        act.wait_ge(s_pairs, nth(s_pairs, h, 9))
                        px = pW.rearrange("p (k b i) -> p k b i", k=2, b=B)
                        act.copy(A7[:, :, :], px[:, 0, :, :])
                        act.copy(Aq7[:, :, :], px[:, 1, :, :]).then_inc(s_wide, 1)
                        rows(h, 0)
                        if following:
                            tap(h + 1, 0, K[:, :], pX[:, :])
                        rows(h, 1)
                        act.wait_ge(s_wo_in, nth(s_wo_in, h, 16))
                        act.mul(won[:, :], wo[:, :], nw[:, 0:1]).then_inc(s_won, 1)
                        rows(h, 2)
                        if following:
                            tap(h + 1, 1, Q[:, :], pW[:, :])
                            silu(h + 1, 0, K[:, :])
                        rows(h, 3)
                        if following:
                            tap(h + 1, 2, V[:, :], pX[:, :])
                            square(h + 1, 0, K[:, :], sqk[:, :])
                            silu(h + 1, 1, Q[:, :])
                        act.wait_ge(s_gated, nth(s_gated, h, 1))
                        act.activation(sqz[:, :], Z[:, :], ACT.Square).then_inc(s_z_squared, 1)
                        if following:
                            square(h + 1, 1, Q[:, :], sqq[:, :])
                            gate(h + 1)
                            silu(h + 1, 2, V[:, :])

                    act.wait_ge(s_zero, 1)
                    all_heads(act, front, body)

                @block.vector
                def _(dve):
                    dve.wait_ge(s_x, 16)
                    layer_norm(dve, s_ln, 0)
                    dve.wait_ge(s_modps, 1)
                    dve.tensor_copy(modT[:, :, :], pA[:, 0:48].rearrange("p (j b) -> p j b", b=B)).then_inc(s_modc, 1)
                    dve.wait_ge(s_modc, 1)
                    for r in (2, 8):
                        dve.tensor_scalar(modT[:, r:r + 2, :], modT[:, r:r + 2, :], 1.0, None, ALU.add)
                    for k, r in enumerate((4, 10)):
                        gate = modT[:, r:r + 2, :]
                        dve.tensor_scalar(gsign[:, 2 * k:2 * k + 2, :], gate, 0.0, 2.0, ALU.is_ge, ALU.mult)
                        last = dve.scalar_tensor_tensor(gmag[:, 2 * k:2 * k + 2, :], gate, -1.0, gate, ALU.mult, ALU.max)
                    last.then_inc(s_own, 1)
                    dve.wait_ge(s_own, 1)
                    dve.tensor_scalar(gsign[:, :, :], gsign[:, :, :], -1.0, None, ALU.add).then_inc(s_own, 1)
                    dve.wait_ge(s_own, 2)
                    for k, r in enumerate((4, 10)):
                        last = dve.scalar_tensor_tensor(modT[:, r:r + 2, :], gmag[:, 2 * k:2 * k + 2, :], 0.25,
                                                        gsign[:, 2 * k:2 * k + 2, :], ALU.max, ALU.mult)
                    last.then_inc(s_mod, 1)
                    dve.wait_ge(s_mod, 1)
                    modulate_1(dve, 0, 0)
                    dve.wait_ge(s_const, 32)
                    for k, r in enumerate((4, 10)):
                        last = dve.tensor_tensor(gdiag[k],
                                                 modT[:, r:r + 2, :].unsqueeze(3).to_broadcast([P, 2, B, P]),
                                                 ident.unsqueeze(1).unsqueeze(1).to_broadcast([P, 2, B, P]), ALU.mult)
                    last.then_inc(s_gd, 1)
                    dve.wait_ge(s_logits, 1)
                    dve.tensor_copy(f1[:, :], pX[:, :]).then_inc(s_f1c, 1)
                    dve.wait_ge(s_logits, 2)
                    dve.tensor_scalar(gx[:, :], pW[:, :], dtb[:, 0:1], None, ALU.add).then_inc(s_gx, 1)
                    own = 2

                    def step(ins):
                        nonlocal own
                        own += 1
                        ins.then_inc(s_own, 1)
                        dve.wait_ge(s_own, own)

                    dve.wait_ge(s_exp1, 3)
                    dve.tensor_scalar(nega[:, :], nega[:, :], -1.0, None, ALU.mult)
                    step(dve.tensor_scalar(v1[:, :], u[:, :], 2.0, None, ALU.add))
                    step(dve.reciprocal(v1[:, :], v1[:, :]))
                    step(dve.tensor_tensor(u[:, :], u[:, :], v1[:, :], ALU.mult))
                    step(dve.tensor_tensor(v2[:, :], u[:, :], u[:, :], ALU.mult))
                    step(dve.tensor_scalar(v1[:, :], v2[:, :], 1.0 / 15, None, ALU.mult))
                    for k in (13, 11, 9, 7, 5, 3):
                        step(dve.scalar_tensor_tensor(v1[:, :], v1[:, :], 1.0 / k, v2[:, :], ALU.add, ALU.mult))
                    step(dve.scalar_tensor_tensor(v1[:, :], v1[:, :], 1.0, u[:, :], ALU.add, ALU.mult))
                    step(dve.tensor_scalar(v2[:, :], gx[:, :], 0.0, None, ALU.max))
                    dve.scalar_tensor_tensor(v1[:, :], v1[:, :], 2.0, v2[:, :], ALU.mult, ALU.add).then_inc(s_sp, 1)
                    dve.wait_ge(s_exp1, 4)
                    step(dve.tensor_scalar(beta[:, :, :], beta[:, :, :], 1.0, None, ALU.add))
                    dve.reciprocal(beta[:, :, :], beta[:, :, :])
                    dve.wait_ge(s_zero, 1)
                    mk = [masks[:, lv * 64:(lv + 1) * 64] for lv in range(SMALL)]

                    def fir(h, k, acc, ps, sh):
                        a, p_ = (t.rearrange("p (b t) -> p b t", b=B) for t in (acc, ps))
                        if sh == 1:
                            dve.wait_ge(s_tapped, nth(s_tapped, h, k + 1))
                        else:
                            dve.wait_ge(s_fir, nth(s_fir, h, 3 * k + sh - 1))
                        w = cw[:, 4 * k + 3 - sh:4 * k + 4 - sh]
                        dve.scalar_tensor_tensor(a[:, :, sh:], p_[:, :, 0:T - sh], w, a[:, :, sh:],
                                                 ALU.mult, ALU.add).then_inc(s_fir, 1)

                    def norms(h):
                        dve.tensor_copy(bh[:, :], beta[:, :, bass.ds(h, 1)].rearrange("p n a -> p (n a)"))\
                           .then_inc(s_c, 1)
                        dve.wait_ge(s_summed, nth(s_summed, h, 2))
                        dve.tensor_scalar(sse[:, :], pW[:, 0:2 * NB], L2_EPS, None, ALU.add).then_inc(s_sse, 1)
                        dve.wait_ge(s_sse, nth(s_sse, h, 1))
                        dve.reciprocal(cc[:, :], sse[:, 0:NB]).then_inc(s_c, 1)
                        dve.wait_ge(s_c, nth(s_c, h, 2))
                        dve.tensor_tensor(cc[:, :], cc[:, :], bh[:, :], ALU.mult).then_inc(s_c, 1)
                        dve.wait_ge(s_c, nth(s_c, h, 3))
                        dve.tensor_tensor(X[:, :, :], ident32.unsqueeze(1).to_broadcast([P, NB, 32]), bc(cc, P, 32),
                                          ALU.mult).then_inc(s_X_grown, 1)

                    def scale(h, lv):
                        if lv < 2:
                            dve.wait_ge(s_silu, nth(s_silu, h, 2))
                        else:
                            dve.wait_ge(s_pairs, nth(s_pairs, h, lv))
                        dve.wait_ge(s_decays_in[lv], nth(s_decays_in[lv], h, 16))
                        dve.tensor_tensor(KQ[:, lv % 2, 0, :], dec[:, lv, :], K[:, :], ALU.mult).then_inc(s_scaled, 1)

                    def own_key(h):
                        dve.wait_ge(s_pairs, nth(s_pairs, h, 1))
                        dve.sem_inc(s_passed_dve, 1)
                        for q in range(4):
                            r = slice(32 * q, 32 * q + 32)
                            last = dve.copy_predicated(AqT[r, :, r],
                                                       masks[r, SMALL * 64:].unsqueeze(1).to_broadcast([32, NB, 32]),
                                                       pW[r, HALF:HALF + NB * 32].rearrange("p (n i) -> p n i", n=NB))
                        last.then_inc(s_picked, 1)

                    def add_head(h, k):
                        dve.wait_ge(s_out_rows, nth(s_out_rows, h, k + 1))
                        for m in range(4):
                            n = 4 * k + m
                            ps = pM[:, n * D:(n + 1) * D]
                            last = dve.scalar_tensor_tensor(attn[:, n, :], ps, fr[:, n:n + 1], attn[:, n, :],
                                                            ALU.mult, ALU.add)
                        last.then_inc(s_added, 1)

                    def pick(h, lv):
                        s = 1 << lv
                        dve.wait_ge(s_pairs, nth(s_pairs, h, lv + 2))
                        dve.wait_ge(s_picked, nth(s_picked, h, lv + 1))
                        dve.sem_inc(s_passed_dve, 1)
                        ps = (pX, pW)[lv % 2].rearrange("p (n k m s) -> p n k m s", k=2, m=64 // s, s=s)
                        m = mk[lv].rearrange("p (m s) -> p m s", s=s).unsqueeze(1).to_broadcast([P, NB, 64 // s, s])
                        to = [t.rearrange("p n (m u s) -> p n m u s", u=2, s=s)[:, :, :, 1, :]
                              for t in (A[:, lv, :, :], AqT)]
                        for k in range(2):
                            last = dve.copy_predicated(to[k], m, ps[:, :, k, :, :])
                        last.then_inc(s_picked, 1)

                    def grow(h, lv):
                        if lv == 0:
                            dve.wait_ge(s_AX, nth(s_AX, h, 1))
                            dve.tensor_tensor(M1[:, :, :], pM1[:, 0:NB * 32].rearrange("p (n j) -> p n j", n=NB),
                                              bc(cc, P, 32), ALU.mult).then_inc(s_x0, 1)
                            dve.wait_ge(s_x0, nth(s_x0, h, 1))
                            m2 = M1[:, :, :]
                        else:
                            dve.wait_ge(s_XAX, nth(s_XAX, h, lv))
                            m2 = pM2[:, 0:NB * 32].rearrange("p (n j) -> p n j", n=NB)
                        dve.tensor_tensor(X[:, :, :], X[:, :, :], m2, ALU.subtract).then_inc(s_X_grown, 1)
                        dve.wait_ge(s_X_grown, nth(s_X_grown, h, lv + 2))
                        dve.transpose(XT.rearrange("p n j -> p (n j)"), X.rearrange("p n j -> p (n j)"))\
                           .then_inc(s_XT_turned, 1)

                    def take(h, k):
                        app, blk, r, ps = ((2, 0, UP, pM2), (4, 1, slice(0, P), pA), (6, 1, UP, pM2))[k]
                        dve.wait_ge(s_chain, nth(s_chain, h, app))
                        if k == 2:
                            dve.wait_ge(s_R, nth(s_R, h, 3))
                        dve.tensor_tensor(seqs(R, blk, r), seqs(R, blk, r),
                                          ps[r, :].rearrange("p (b n) -> p b n", b=B), ALU.subtract).then_inc(s_R, 1)

                    def level_tables():
                        step(dve.memset(suf, 1.0))
                        dve.wait_ge(s_a, 1)
                        for lv in range(LEVELS):
                            s = 1 << lv
                            w, p_, f_ = (t.rearrange("p (m u s) -> p m u s", u=2, s=s) for t in (lev[:, lv, :], pre, suf))
                            dve.tensor_copy(w[:, :, 0, :], f_[:, :, 0, :])
                            dve.tensor_copy(w[:, :, 1, :], p_[:, :, 1, :]).then_inc(s_lev, 1)
                            if lv < LEVELS - 1:
                                m = NT // (2 * s)
                                step(dve.tensor_tensor(f_[:, :, 0, :], f_[:, :, 0, :],
                                                       p_[:, :, 1, s - 1:s].to_broadcast([P, m, s]), ALU.mult))
                                step(dve.tensor_tensor(p_[:, :, 1, :], p_[:, :, 1, :],
                                                       p_[:, :, 0, s - 1:s].to_broadcast([P, m, s]), ALU.mult))

                    def front(h):
                        for k, (acc, ps) in enumerate(((K, pX), (Q, pW), (V, pX))):
                            for sh in (1, 2, 3):
                                fir(h, k, acc, ps, sh)
                            if k == 0:
                                level_tables()
                        scale(h, 0)
                        scale(h, 1)
                        own_key(h)
                        norms(h)

                    def body(h, following):
                        pick(h, 0)
                        scale(h, 2)
                        pick(h, 1)
                        grow(h, 0)
                        scale(h, 3)
                        pick(h, 2)
                        for lv in range(1, 3):
                            scale(h, lv + 3)
                            grow(h, lv)
                            pick(h, lv + 2)
                        scale(h, 6)
                        grow(h, 3)
                        scale(h, 7)
                        grow(h, 4)
                        n = h + 1
                        take(h, 0)
                        if following:
                            fir(n, 0, K, pX, 1)
                            fir(n, 0, K, pX, 2)
                        take(h, 1)
                        if following:
                            fir(n, 0, K, pX, 3)
                        take(h, 2)
                        dve.tensor_scalar(t2[:, :], rqs[:, :], QSCALE, None, ALU.mult).then_inc(s_ms, 1)
                        if following:
                            fir(n, 1, Q, pW, 1)
                            fir(n, 1, Q, pW, 2)
                            fir(n, 1, Q, pW, 3)
                        dve.wait_ge(s_outputs, nth(s_outputs, h, 1))
                        dve.tensor_tensor(Z[:, :], pM[:, 0:NT], SG[:, :], ALU.mult).then_inc(s_gated, 1)
                        dve.wait_ge(s_ms, nth(s_ms, h, 1))
                        dve.tensor_tensor(ms[:, :], t2[:, :], t2[:, :], ALU.mult).then_inc(s_ms, 1)
                        if following:
                            fir(n, 2, V, pX, 1)
                            fir(n, 2, V, pX, 2)
                            fir(n, 2, V, pX, 3)
                        dve.wait_ge(s_z_summed, nth(s_z_summed, h, 1))
                        dve.wait_ge(s_ms, nth(s_ms, h, 2))
                        dve.tensor_tensor(ms[:, :], pW[:, 0:NB], ms[:, :], ALU.mult).then_inc(s_ms, 1)
                        dve.wait_ge(s_ms, nth(s_ms, h, 3))
                        dve.tensor_scalar(ms[:, :], ms[:, :], 1.0 / DK, RMS_EPS, ALU.mult, ALU.add).then_inc(s_ms, 1)
                        if following:
                            scale(n, 0)
                        dve.wait_ge(s_rms, nth(s_rms, h, 1))
                        dve.wait_ge(s_added, nth(s_added, h, 2))
                        dve.tensor_tensor(fr[:, :], t2[:, :], rms[:, :], ALU.mult).then_inc(s_ms, 1)
                        dve.wait_ge(s_ms, nth(s_ms, h, 5))
                        add_head(h, 0)
                        if following:
                            scale(n, 1)
                        add_head(h, 1)
                        if following:
                            own_key(n)
                            norms(n)

                    all_heads(dve, front, body)

                @block.tensor
                def _(pe):
                    pe.wait_ge(s_siluc, 1)
                    for j in range(12):
                        for c in range(DC):
                            last = pe.matmul(pA[:, j * B:(j + 1) * B], wmod[:, c, j * P:(j + 1) * P], siluc[:, c, :],
                                             start=c == 0, stop=c == DC - 1)
                    last.then_inc(s_modps, 1)
                    pe.wait_ge(s_const, 32)
                    turn_in(pe, 0)
                    pe.wait_ge(s_small_in, 6 * 16)
                    for hf in range(2):
                        modulated(pe, 0, 2 * hf + 2)
                        for c in range(DC):
                            last = pe.matmul(pX[:, hf * HALF:(hf + 1) * HALF], wf1[:, c, :],
                                             hT[:, c, hf * HALF:(hf + 1) * HALF], start=c == 0, stop=c == DC - 1)
                    last.then_inc(s_logits, 1)
                    pe.wait_ge(s_f1c, 1)
                    for hf in range(2):
                        last = pe.matmul(pW[:, hf * HALF:(hf + 1) * HALF], wf2[:, :],
                                         f1[:, hf * HALF:(hf + 1) * HALF], start=True, stop=True)
                    last.then_inc(s_logits, 1)
                    for n in range(NB):
                        for c in range(DC):
                            last = pe.matmul(pA[:, 64 + n * H:64 + (n + 1) * H], hT[:, c, n * P:(n + 1) * P],
                                             wb[:, c, :], start=c == 0, stop=c == DC - 1)
                    last.then_inc(s_logits, 1)
                    pe.wait_ge(s_gd, 1)
                    pe.wait_ge(s_set, 1)
                    pe.wait_ge(s_exp1, 4)
                    for r in range(4):
                        last = pe.matmul(pM[:, r * HALF:(r + 1) * HALF], ones[:, :],
                                         gdiag[r // 2][:, r % 2, :, :].rearrange("p b n -> p (b n)"),
                                         start=True, stop=True)
                    last.then_inc(s_gps, 1)
                    def passed():
                        pe.sem_inc(s_passed, 1)

                    def project(h, k, ps, t0, t1):
                        for c in range(DC):
                            last = pe.matmul(ps[:, t0:t1], wh[:, k, c, :], hT[:, c, t0:t1],
                                             start=c == 0, stop=c == DC - 1)
                        if t1 == NT:
                            last.then_inc(s_projected, 1)

                    def squares(h, k, t):
                        pe.wait_ge(s_squared, nth(s_squared, h, k + 1))
                        for n in range(NB):
                            last = pe.matmul(pW[:, k * NB + n:k * NB + n + 1], t[:, n * P:(n + 1) * P],
                                             ones[:, 0:1], start=True, stop=True)
                        last.then_inc(s_summed, 1)

                    def own_keys(h):
                        passed()
                        for n in range(NB):
                            for q in range(4):
                                t0 = n * P + 32 * q
                                last = pe.matmul(pW[32 * q:32 * q + 32, HALF + n * 32:HALF + (n + 1) * 32], K[:, t0:t0 + 32],
                                                 Q[:, t0:t0 + 32], start=True, stop=True)
                        last.then_inc(s_pairs, 1)

                    def products(h, lv, part):
                        s = 1 << lv
                        ps = (pX, pW)[lv % 2]
                        if part == 0:
                            if lv == 0:
                                pe.wait_ge(s_fir, nth(s_fir, h, 9))
                            elif lv == 1:
                                pe.wait_ge(s_picked, nth(s_picked, h, 1))
                                pe.wait_ge(s_sse, nth(s_sse, h, 1))
                            elif lv < 7:
                                pe.wait_ge(s_picked, nth(s_picked, h, lv))
                            else:
                                pe.wait_ge(s_wide, nth(s_wide, h, 1))
                            pe.wait_ge(s_scaled, nth(s_scaled, h, lv + 1))
                            pe.wait_ge(s_qscaled, nth(s_qscaled, h, lv + 1))
                            passed()
                        kq = KQ[:, lv % 2, :, :]
                        if lv < 7:
                            rows = P if lv < 6 else 64
                            mv_ = kq.rearrange("p k (m u s) -> p k m u s", u=2, s=s)
                            for n in range(4 * part, 4 * part + 4):
                                m0 = n * P // (2 * s)
                                last = pe.matmul(ps[0:rows, n * P:(n + 1) * P], kq[:, 0, n * P:n * P + rows],
                                                 mv_[:, :, m0:m0 + 64 // s, 1, :], start=True, stop=True)
                        else:
                            for b in range(2 * part, 2 * part + 2):
                                for k in range(2):
                                    last = pe.matmul(ps[:, k * HALF + b * P:k * HALF + (b + 1) * P],
                                                     kq[:, 0, b * T:b * T + P], kq[:, k, b * T + P:(b + 1) * T],
                                                     start=True, stop=True)
                        if part:
                            last.then_inc(s_pairs, 1)

                    def mult_1(h, lv):
                        if lv == 0:
                            pe.wait_ge(s_added, nth(s_added, h, 1))
                        pe.wait_ge(s_X_grown, nth(s_X_grown, h, lv + 1))
                        if lv < SMALL:
                            pe.wait_ge(s_picked, nth(s_picked, h, lv + 2))
                        else:
                            pe.wait_ge(s_wide, nth(s_wide, h, 1))
                        passed()
                        for n in range(NB):
                            if lv < SMALL:
                                last = pe.matmul(pM1[:, n * 32:(n + 1) * 32], A[:, lv, n, :], X[:, n, :],
                                                 start=True, stop=True)
                            else:
                                for p0 in (0, 64):
                                    last = pe.matmul(pM1[p0 + 32:p0 + 64, n * 32:(n + 1) * 32], A5[p0:p0 + 32, n, :],
                                                     X[p0:p0 + 32, n, :], start=True, stop=True)
                        last.then_inc(s_AX, 1)

                    def mult_2(h, lv):
                        pe.wait_ge(s_AX_kept, nth(s_AX_kept, h, lv))
                        pe.wait_ge(s_XT_turned, nth(s_XT_turned, h, lv))
                        passed()
                        for n in range(NB):
                            c = slice(n * 32, (n + 1) * 32)
                            if lv < SMALL:
                                for q in range(4):
                                    r = slice(32 * q, 32 * q + 32)
                                    last = pe.matmul(pM2[r, c], XT[r, n, :], M1[r, n, :], start=True, stop=True)
                            else:
                                for p0 in (0, 64):
                                    r = slice(p0 + 32, p0 + 64)
                                    last = pe.matmul(pM3[p0:p0 + 32, c], M1[r, n, :], XT[r, n, :],
                                                     start=True, stop=True)
                        last.then_inc(s_XAX, 1)

                    def solve(h, k):
                        blk, r, ps = ((0, LO, pM1), (0, UP, pM3), (1, LO, pM1), (1, UP, pM3))[k]
                        if k:
                            pe.wait_ge(s_R, nth(s_R, h, k + 1))
                        passed()
                        for b in range(B):
                            n = 2 * b + blk
                            last = pe.matmul(ps[r, b * P:(b + 1) * P], XC[r, n, :], R[r, n, :], start=True, stop=True)
                        last.then_inc(s_chain, 1)

                    def explain(h, k):
                        pe.wait_ge(s_rows, nth(s_rows, h, k + 1))
                        passed()
                        for b in range(B):
                            if k == 1:
                                last = pe.matmul(pA[:, b * P:(b + 1) * P], A7[:, b, :], dl[:, 2 * b, :],
                                                 start=True, stop=True)
                            else:
                                n = 2 * b + k // 2
                                last = pe.matmul(pM2[UP, b * P:(b + 1) * P], A6[:, n, :], dl[LO, n, :],
                                                 start=True, stop=True)
                        last.then_inc(s_chain, 1)

                    def outputs(h, blk):
                        for b in range(B):
                            n = 2 * b + blk
                            o = pM[:, n * P:(n + 1) * P]
                            last = pe.matmul(o, dl[:, n, :], AqT[:, n, :], start=True, stop=blk == 0)
                            if blk:
                                last = pe.matmul(o, dl[:, n - 1, :], Aq7[:, b, :], start=False, stop=True)
                        return last

                    def front(h):
                        pe.wait_ge(s_weights_in, nth(s_weights_in, h, 32))
                        pe.wait_ge(s_gx, 1)
                        pe.wait_ge(s_gates, 1)
                        for k, ps in enumerate((pX, pW, pX, pV)):
                            if k == 2:
                                pe.wait_ge(s_fir, nth(s_fir, h, 3))
                            project(h, k, ps, 0, HALF)
                            project(h, k, ps, HALF, NT)
                        pe.wait_ge(s_fir, nth(s_fir, h, 6))
                        squares(h, 0, sqk)
                        own_keys(h)
                        products(h, 0, 0)
                        squares(h, 1, sqq)
                        products(h, 0, 1)

                    def out_rows(h, k):
                        for m in range(4):
                            n = 4 * k + m
                            last = pe.matmul(pM[:, n * D:(n + 1) * D], Z[:, n * P:(n + 1) * P],
                                             won[:, :], start=True, stop=True)
                        last.then_inc(s_out_rows, 1)

                    def body(h, following):
                        products(h, 1, 0)
                        products(h, 1, 1)
                        pe.wait_ge(s_silu, nth(s_silu, h, 4))
                        pe.wait_ge(s_added, nth(s_added, h, 2))
                        for n in range(NB):
                            last = pe.transpose(pV[:, n * P:(n + 1) * P], V[:, n * P:(n + 1) * P], ident)
                        last.then_inc(s_v_turned, 1)
                        mult_1(h, 0)
                        products(h, 2, 0)
                        products(h, 2, 1)
                        for lv in range(1, SMALL + 1):
                            mult_1(h, lv)
                            products(h, lv + 2, 0)
                            mult_2(h, lv)
                            products(h, lv + 2, 1)
                        pe.wait_ge(s_XC_part, nth(s_XC_part, h, 2))
                        n = h + 1
                        solve(h, 0)
                        if following:
                            pe.wait_ge(s_weights_in, nth(s_weights_in, n, 32))
                            pe.wait_ge(s_wide, nth(s_wide, h, 2))
                            project(n, 0, pX, 0, HALF)
                        explain(h, 0)
                        if following:
                            project(n, 0, pX, HALF, NT)
                        solve(h, 1)
                        if following:
                            pe.wait_ge(s_wide, nth(s_wide, h, 3))
                            project(n, 1, pW, 0, HALF)
                        explain(h, 1)
                        if following:
                            project(n, 1, pW, HALF, HALF + T)
                        solve(h, 2)
                        if following:
                            project(n, 1, pW, HALF + T, NT)
                        explain(h, 2)
                        if following:
                            pe.wait_ge(s_fir, nth(s_fir, n, 3))
                            project(n, 2, pX, 0, HALF)
                        solve(h, 3)
                        if following:
                            project(n, 2, pX, HALF, NT)
                        pe.wait_ge(s_picked, nth(s_picked, h, 6))
                        pe.wait_ge(s_rows, nth(s_rows, h, 4))
                        outputs(h, 0)
                        outputs(h, 1).then_inc(s_outputs, 1)
                        if following:
                            project(n, 3, pV, 0, HALF)
                            project(n, 3, pV, HALF, NT)
                            pe.wait_ge(s_fir, nth(s_fir, n, 6))
                        pe.wait_ge(s_z_squared, nth(s_z_squared, h, 1))
                        for m in range(NB):
                            last = pe.matmul(pW[:, m:m + 1], sqz[:, m * P:(m + 1) * P], ones[:, 0:1],
                                             start=True, stop=True)
                        last.then_inc(s_z_summed, 1)
                        pe.wait_ge(s_gated, nth(s_gated, h, 1))
                        pe.wait_ge(s_won, nth(s_won, h, 1))
                        out_rows(h, 0)
                        if following:
                            pe.wait_ge(s_ms, nth(s_ms, h, 3))
                            squares(n, 0, sqk)
                            pe.wait_ge(s_silu, nth(s_silu, n, 3))
                        out_rows(h, 1)
                        if following:
                            own_keys(n)
                            products(n, 0, 0)
                            squares(n, 1, sqq)
                            products(n, 0, 1)

                    all_heads(pe, front, body)

        rt_steps = []

        NS = 4
        AHEAD = 2
        ROUNDS = E // NS
        with ExitStack() as ffn:
            def fb(name, shape, dt=F32):
                return sb(name, shape, dt, where=ffn)

            gated = fb("gated", [P, NB, D])
            sc_, sbs = fb("sc_", [P, NB, E]), fb("sbs", [P, NB, E])
            top2 = fb("top2", [P, NB, G, 8])
            gs = fb("gs", [P, NB, G])
            cmp_, cnt = fb("cmp_", [P, NB, G]), fb("cnt", [P, NB, G])
            keep = fb("keep", [P, NB, G], I32)
            cand = fb("cand", [P, NB, E])
            top8 = fb("top8", [P, NB, 8])
            taken = fb("taken", [P, NB, E])
            wsum, winv = fb("wsum", [P, NB]), fb("winv", [P, NB])
            cwT = fb("cwT", [E, NT])
            xl, yl = fb("xl", [P, NT]), fb("yl", [P, NT])
            rlu = fb("rlu", [P, SHC, NT])
            w1 = [fb(f"w1_{k}", [P, P]) for k in range(NS)]
            w2 = [fb(f"w2_{k}", [P, P]) for k in range(NS)]
            cwb = [fb(f"cwb{k}", [P, NT]) for k in range(NS)]
            rl = [fb(f"rl{k}", [P, NT]) for k in range(NS)]
            hw = [fb(f"hw{k}", [P, NT]) for k in range(NS)]
            zero = fb("zero", [P, P])
            PH = (pX, pW)
            pY = (pM1, pM2)
            PS = (pM[:, 2 * HALF:], pW)
            s_x1, s_ln2, s_gate_logits, s_gate_exp, s_routing, s_routes_turned, s_routes_kept, s_routes_stored, s_latent, s_latent_in = (
                sem(n) for n in ("s_x1", "s_ln2", "s_gate_logits", "s_gate_exp", "s_routing", "s_routes_turned", "s_routes_kept", "s_routes_stored", "s_latent", "s_latent_in"))
            s_expert_in, s_routes_in, s_up, s_rl, s_half_weighed, s_weighed, s_down = (
                [sem(f"{n}{k}") for k in range(NS)] for n in ("s_expert_in", "s_routes_in", "s_up", "s_rl", "s_half_weighed", "s_weighed", "s_down"))
            s_z0, s_latent_kept, s_shared_up, s_shared_relu, s_shared_squared, s_ffn_out, s_fin, s_out = (
                sem(n) for n in ("s_z0", "s_latent_kept", "s_shared_up", "s_shared_relu", "s_shared_squared", "s_ffn_out", "s_fin", "s_out"))
            rt_steps = []

            def add_in(dve, k, branch, blocks, done, at):
                g = gates[:, k, blocks.start // 2:blocks.stop // 2, :].unsqueeze(2)
                nb = (blocks.stop - blocks.start) // 2
                dve.tensor_tensor(gated[:, blocks, :].rearrange("p (b u) f -> p b u f", u=2),
                                  branch.rearrange("p (b u) f -> p b u f", u=2), g.to_broadcast([P, nb, 2, D]),
                                  ALU.mult).then_inc(done, 1)
                dve.wait_ge(done, at)
                dve.tensor_tensor(x[:, blocks, :], x[:, blocks, :], gated[:, blocks, :], ALU.add).then_inc(done, 1)

            with nc.Block() as block:
                @block.sync
                def _(sp):
                    def expert_weights(e, k):
                        for t, n in ((w1[k], "w1"), (w2[k], "w2")):
                            sp.dma_start(t[:, :], d[n][bass.ds(e, 1)].rearrange("a p n -> (a p) n"))\
                              .then_inc(s_expert_in[k], 16)

                    def token_weights(e, k):
                        sp.dma_start(cwb[k][:, :], route_dram[bass.ds(e, 1), :].to_broadcast([P, NT]))\
                          .then_inc(s_routes_in[k], 16)

                    for k in range(NS):
                        expert_weights(k, k)
                    sp.wait_ge(s_routes_kept, 1)
                    sp.dma_start(route_dram, cwT[:, :]).then_inc(s_routes_stored, 16)
                    sp.wait_ge(s_routes_stored, 16)
                    for k in range(NS):
                        token_weights(k, k)
                    with sp.Fori(0, ROUNDS - 1) as i:
                        for k in range(NS):
                            sp.wait_ge(s_down[k], i + 1)
                            expert_weights(NS * i + NS + k, k)
                            token_weights(NS * i + NS + k, k)
                    for k in range(2):
                        sp.wait_ge(s_fin, 2 * k + 2)
                        sp.dma_start(out.rearrange("(n p) f -> p n f", p=P)[:, 4 * k:4 * k + 4, :],
                                     x[:, 4 * k:4 * k + 4, :]).then_inc(s_out, 16)
                    sp.wait_ge(s_out, 32)

                @block.gpsimd
                def _(pool):
                    pool.memset(zero[:, :], 0.0).then_inc(s_z0, 1)
                    pool.wait_ge(s_ln2, 3)
                    pool.tensor_tensor(rstd[:, :], veps[:, :], halfs[:, 0, :], ALU.pow).then_inc(s_rstd, 1)

                @block.scalar
                def _(act):
                    modulate_0(act, 1, 6)
                    act.wait_ge(s_gate_logits, 1)
                    act.activation(sc_[:, :, :], pA[:, 0:NB * E].rearrange("p (n e) -> p n e", n=NB), ACT.Exp,
                                   scale=-1.0).then_inc(s_gate_exp, 1)
                    act.wait_ge(s_latent, 1)
                    act.copy(xl[:, :], pX[:, :]).then_inc(s_latent_in, 1)
                    for j in range(SHC):
                        act.wait_ge(s_shared_up, j + 1)
                        act.activation(rlu[:, j, :], PS[j % 2], ACT.Relu).then_inc(s_shared_relu, 1)
                        act.wait_ge(s_shared_relu, j + 1)
                        act.activation(rlu[:, j, :], rlu[:, j, :], ACT.Square).then_inc(s_shared_squared, 1)

                    def relu(i, k):
                        act.wait_ge(s_up[k], i + 1)
                        act.activation(rl[k][:, :], PH[k % 2][:, :], ACT.Relu).then_inc(s_rl[k], 1)

                    for k in range(NS):
                        relu(0, k)
                    with act.Fori(1, ROUNDS) as i:
                        for k in range(NS):
                            act.wait_ge(s_weighed[k], i)
                            relu(i, k)
                    act.wait_ge(s_down[NS - 1], ROUNDS)
                    act.copy(yl[:, 0:HALF], pM1[:, :])
                    act.copy(yl[:, HALF:], pM2[:, :]).then_inc(s_latent_kept, 1)

                @block.vector
                def _(dve):
                    add_in(dve, 0, attn[:, :, :], slice(0, NB), s_x1, 1)
                    dve.wait_ge(s_x1, 2)
                    for n in range(NB):
                        last = dve.bn_stats(stats[:, n, :], x[:, n, :])
                    last.then_inc(s_ln2, 1)
                    dve.wait_ge(s_ln2, 1)
                    for n in range(NB):
                        last = dve.bn_aggr(mv[:, n, :], stats[:, n, :])
                    last.then_inc(s_ln2, 1)
                    dve.wait_ge(s_ln2, 2)
                    dve.tensor_scalar(veps[:, :], mv[:, :, 1], LN_EPS, None, ALU.add).then_inc(s_ln2, 1)
                    dve.wait_ge(s_rstd, 2)
                    for n in range(NB):
                        dve.tensor_scalar(xn[:, n, :], x[:, n, :], mv[:, n, 0:1], rstd[:, n:n + 1],
                                          ALU.subtract, ALU.mult).then_inc(s_xn, 1)
                    modulate_1(dve, 1, 6)
                    steps = 0

                    def step(ins):
                        nonlocal steps
                        steps += 1
                        ins.then_inc(s_routing, 1)
                        dve.wait_ge(s_routing, steps)

                    dve.wait_ge(s_ffn_in, 6 * 16)
                    dve.wait_ge(s_gate_exp, 1)
                    step(dve.tensor_scalar(sc_[:, :, :], sc_[:, :, :], 1.0, None, ALU.add))
                    step(dve.reciprocal(sc_[:, :, :], sc_[:, :, :]))
                    step(dve.tensor_tensor(sbs[:, :, :], sc_[:, :, :],
                                           gbias.unsqueeze(1).to_broadcast([P, NB, E]), ALU.add))
                    for n in range(NB):
                        for g in range(G):
                            last = dve.max(top2[:, n, g, :], sbs[:, n, g * EG:(g + 1) * EG])
                    step(last)
                    step(dve.tensor_tensor(gs[:, :, :], top2[:, :, :, 0], top2[:, :, :, 1], ALU.add))
                    step(dve.memset(cnt[:, :, :], 0.0))
                    for g in range(G):
                        one = gs[:, :, g:g + 1]
                        if g > 0:
                            dve.tensor_tensor(cmp_[:, :, 0:g], one.to_broadcast([P, NB, g]), gs[:, :, 0:g], ALU.is_gt)
                        if g < G - 1:
                            dve.tensor_tensor(cmp_[:, :, g + 1:], one.to_broadcast([P, NB, G - 1 - g]),
                                              gs[:, :, g + 1:], ALU.is_ge)
                        step(dve.memset(cmp_[:, :, g:g + 1], 0.0))
                        step(dve.tensor_tensor(cnt[:, :, :], cnt[:, :, :], cmp_[:, :, :], ALU.add))
                    dve.memset(cand[:, :, :], FILL)
                    step(dve.tensor_scalar(keep[:, :, :], cnt[:, :, :], float(TOPG), None, ALU.is_lt))
                    step(dve.copy_predicated(cand.rearrange("p n (g e) -> p n g e", g=G),
                                             keep.unsqueeze(3).to_broadcast([P, NB, G, EG]),
                                             sbs.rearrange("p n (g e) -> p n g e", g=G)))
                    for n in range(NB):
                        last = dve.max(top8[:, n, :], cand[:, n, :])
                    step(last)
                    for n in range(NB):
                        last = dve.match_replace(taken[:, n, :], top8[:, n, :], cand[:, n, :], TAKEN)
                    step(last)
                    step(dve.scalar_tensor_tensor(cand[:, :, :], taken[:, :, :], TAKEN, sc_[:, :, :],
                                                  ALU.is_ge, ALU.mult))
                    step(dve.tensor_reduce(wsum[:, :], cand[:, :, :], AX.X, ALU.add))
                    step(dve.reciprocal(winv[:, :], wsum[:, :]))
                    step(dve.tensor_scalar(winv[:, :], winv[:, :], ROUTED_SCALE, None, ALU.mult))
                    dve.tensor_tensor(cand[:, :, :], cand[:, :, :], winv.unsqueeze(2).to_broadcast([P, NB, E]),
                                      ALU.mult).then_inc(s_routing, 1)
                    dve.wait_ge(s_routes_turned, 1)
                    dve.tensor_copy(cwT[:, :], pX[0:E, :]).then_inc(s_routes_kept, 1)
                    rt_steps.append(steps + 1)

                    def weigh(i, k):
                        dve.wait_ge(s_routes_in[k], 16 * i + 16)
                        dve.wait_ge(s_rl[k], i + 1)
                        dve.tensor_tensor(hw[k][:, :], rl[k][:, :], cwb[k][:, :], ALU.mult).then_inc(s_half_weighed[k], 1)
                        dve.wait_ge(s_half_weighed[k], i + 1)
                        dve.tensor_tensor(hw[k][:, :], hw[k][:, :], rl[k][:, :], ALU.mult).then_inc(s_weighed[k], 1)

                    for k in range(NS):
                        weigh(0, k)
                    with dve.Fori(1, ROUNDS) as i:
                        for k in range(NS):
                            dve.wait_ge(s_down[k], i)
                            weigh(i, k)
                    for k, ps in enumerate((pX, pW)):
                        dve.wait_ge(s_ffn_out, k + 1)
                        add_in(dve, 1, ps.rearrange("p (n f) -> p n f", n=4), slice(4 * k, 4 * k + 4), s_fin,
                               2 * k + 1)

                @block.tensor
                def _(pe):
                    pe.wait_ge(s_x1, 2)
                    turn_in(pe, 1)
                    pe.wait_ge(s_ffn_in, 6 * 16)
                    for n in range(NB):
                        modulated(pe, 1, n // 2 + 1)
                        for c in range(DC):
                            last = pe.matmul(pA[:, n * E:(n + 1) * E], hT[:, c, n * P:(n + 1) * P], gw[:, c, :],
                                             start=c == 0, stop=c == DC - 1)
                    last.then_inc(s_gate_logits, 1)
                    for hf in range(2):
                        for c in range(DC):
                            last = pe.matmul(pX[:, hf * HALF:(hf + 1) * HALF], fc1[:, c, :],
                                             hT[:, c, hf * HALF:(hf + 1) * HALF], start=c == 0, stop=c == DC - 1)
                    last.then_inc(s_latent, 1)
                    pe.wait_ge(s_gate_exp, 1)
                    for j in range(SHC):
                        if j >= 2:
                            pe.wait_ge(s_shared_relu, j - 1)
                        for hf in range(2):
                            for c in range(DC):
                                last = pe.matmul(PS[j % 2][:, hf * HALF:(hf + 1) * HALF], up[:, c, j * P:(j + 1) * P],
                                                 hT[:, c, hf * HALF:(hf + 1) * HALF], start=c == 0, stop=c == DC - 1)
                        last.then_inc(s_shared_up, 1)
                        if j == SHC - 2:
                            pe.wait_ge(s_latent_in, 1)
                            pe.wait_ge(s_routing, rt_steps[0])
                            for n in range(NB):
                                last = pe.transpose(pX[0:E, n * P:(n + 1) * P], cand[:, n, :], ident)
                            last.then_inc(s_routes_turned, 1)
                    pe.wait_ge(s_z0, 1)
                    pe.wait_ge(s_latent_in, 1)
                    for hf in range(2):
                        pe.matmul(pY[hf][:, :], zero[:, :], xl[:, hf * HALF:(hf + 1) * HALF], start=True, stop=False,
                                  skip_group_check=True)

                    def ups(i, k):
                        pe.wait_ge(s_expert_in[k], 32 * i + 32)
                        for hf in range(2):
                            last = pe.matmul(PH[k % 2][:, hf * HALF:(hf + 1) * HALF], w1[k][:, :],
                                             xl[:, hf * HALF:(hf + 1) * HALF], start=True, stop=True)
                        last.then_inc(s_up[k], 1)

                    def downs(i, k, stop=False):
                        pe.wait_ge(s_weighed[k], i + 1)
                        for hf in range(2):
                            last = pe.matmul(pY[hf][:, :], w2[k][:, :], hw[k][:, hf * HALF:(hf + 1) * HALF],
                                             start=False, stop=stop, skip_group_check=True)
                        last.then_inc(s_down[k], 1)

                    pe.wait_ge(s_routes_kept, 1)
                    ups(0, 0)
                    pe.wait_ge(s_shared_relu, SHC)
                    ups(0, 1)
                    with pe.Fori(0, ROUNDS - 1) as i:
                        for k in range(NS):
                            pe.wait_ge(s_rl[k], i + 1)
                            m = (k + AHEAD) % NS
                            ups(i + (k + AHEAD) // NS, m)
                            downs(i, k)
                    for k in range(NS):
                        if k < NS - AHEAD:
                            pe.wait_ge(s_rl[k], ROUNDS)
                            ups(ROUNDS - 1, k + AHEAD)
                        downs(ROUNDS - 1, k, stop=k == NS - 1)
                    pe.wait_ge(s_shared_squared, SHC)
                    pe.wait_ge(s_rl[3], ROUNDS)
                    for k in range(2):
                        for m in range(4):
                            r = slice((4 * k + m) * P, (4 * k + m + 1) * P)
                            for j in range(SHC):
                                pe.matmul(PH[k][:, m * D:(m + 1) * D], rlu[:, j, r], down[:, j, :],
                                          start=j == 0, stop=False)
                            if k == 0 and m == 0:
                                pe.wait_ge(s_latent_kept, 1)
                            last = pe.matmul(PH[k][:, m * D:(m + 1) * D], yl[:, r], fc2[:, :], start=False, stop=True)
                        last.then_inc(s_ffn_out, 1)


def kernel(**inputs):
    import numpy as _np
    import concourse.bacc as _bacc
    from concourse import mybir as _mybir
    from concourse.bass_utils import run_bass_kernel_spmd as _run

    a = {k: _np.asarray(v) for k, v in inputs.items()}
    at, ff = "L0_attn_", "L0_ffn_"

    def by_head(w):
        return w.reshape(DC, P, H, DK).transpose(2, 1, 0, 3)

    cw = _np.zeros((H, P, 16), _np.float32)
    for k, n in enumerate(("conv_k", "conv_q", "conv_v")):
        cw[:, :, 4 * k:4 * k + 4] = a[at + n].reshape(H, P, KW)
    cw[:, :, 12] = a[at + "bg"].reshape(H, P)
    floats, masks = shape_constants()
    arrays = {
        "x": a[at + "hidden_states"].reshape(NT, D),
        "cT": a["L0_c"].T,
        "wmod": a["L0_wmod"],
        "Wh": _np.stack([by_head(a[at + n]) for n in ("Wk", "Wq", "Wv", "Wg")], axis=2),
        "cw": cw,
        "Wf1": a[at + "Wf1"], "Wf2": a[at + "Wf2"], "Wb": a[at + "Wb"],
        "dt": a[at + "dt_bias"].reshape(P, 1),
        "A_log": _np.repeat(a[at + "A_log"], NG).reshape(P, 1),
        "norm_w": a[at + "norm_w"].reshape(P, 1),
        "Wo": a[at + "Wo"].reshape(H, DK, D),
        "gate_w": a[ff + "gate_w"].T, "gate_bias": a[ff + "gate_bias"].reshape(1, E),
        "fc1": a[ff + "fc1_w"].T, "fc2": a[ff + "fc2_w"].T,
        "w1": a[ff + "w1"].transpose(0, 2, 1), "w2": a[ff + "w2"].transpose(0, 2, 1),
        "up": a[ff + "shared_up_w"].T, "down": a[ff + "shared_down_w"].T,
        "floats": floats, "masks": masks,
    }
    arrays = {k: _np.ascontiguousarray(v) for k, v in arrays.items()}
    nc = _bacc.Bacc("TRN2", target_bir_lowering=False, num_devices=1)
    args = {k: nc.dram_tensor(k + "_dram", v.shape, _mybir.dt.from_np(v.dtype), kind="ExternalInput").ap()
            for k, v in arrays.items()}
    out = nc.dram_tensor("out_dram", (NT, D), F32, kind="ExternalOutput").ap()
    build(nc, args, out)
    r = _run(nc, [{k + "_dram": v for k, v in arrays.items()}], core_ids=[0])
    return r.results[0]["out_dram"].reshape(B, T, D)
```
